# Optimizing a Trainium2 kernel written in Bass

```python
import numpy as np
import jax
import jax.numpy as jnp

def _softmax(x, axis=-1):
    return jax.nn.softmax(x, axis=axis)

def _gelu(x):
    return jax.nn.gelu(x, approximate=True)

def _silu(x):
    return jax.nn.silu(x)

def _sigmoid(x):
    return jax.nn.sigmoid(x)

def _layernorm(x, axis=-1, eps=1e-05):
    m = jnp.mean(x, axis=axis, keepdims=True)
    v = jnp.var(x, axis=axis, keepdims=True)
    return (x - m) / jnp.sqrt(v + eps)

def _scatter_add(tgt, idx, src, axis=0):
    return tgt.at[idx].add(src)

def _segment_sum(src, seg, n):
    return jax.ops.segment_sum(src, seg, n)
kernel_name = 'mk_sandwich_d2_jaxref_r8_458bab'

def setup_inputs(seed: int=0):
    np.random.seed(seed)
    _w = jnp.asarray

    def _L0_attn_setup():
        import jax, jax.numpy as jnp
        import numpy as np
        HEADS = 32
        key = jax.random.key(seed)
        ks = jax.random.split(key, 5)
        H = 512
        B, S = (2, 256)
        w_scale = 1.0 / np.sqrt(H)
        return {'x': jax.random.normal(ks[0], (B, S, H), dtype=jnp.float32), 'attn_qkvw': jax.random.normal(ks[1], (H, 3 * H), dtype=jnp.float32) * w_scale, 'attn_qkvb': jax.random.normal(ks[2], (3 * H,), dtype=jnp.float32) * 0.02, 'attn_ow': jax.random.normal(ks[3], (H, H), dtype=jnp.float32) * w_scale, 'attn_ob': jax.random.normal(ks[4], (H,), dtype=jnp.float32) * 0.02}
    _L0_attn_in = _L0_attn_setup()

    def _L0_ffn_setup():
        import jax, jax.numpy as jnp
        import numpy as np
        _TRIPLES = [(1, 2, 3), (1, 4, 5), (1, 7, 6), (2, 4, 6), (2, 5, 7), (3, 4, 7), (3, 6, 5)]

        def _oct_struct():
            S = np.zeros((8, 8, 8), np.float32)
            S[0, 0, 0] = 1.0
            for i in range(1, 8):
                S[0, i, i] = 1.0
                S[i, 0, i] = 1.0
                S[i, i, 0] = -1.0
            for a, b, c in _TRIPLES:
                for x, y, z in ((a, b, c), (b, c, a), (c, a, b)):
                    S[x, y, z] = 1.0
                    S[y, x, z] = -1.0
            return jnp.asarray(S)
        S_OCT = _oct_struct()
        N_EMBD = 512
        HIDDEN = 1366

        def ternary_dequant(W):
            scale = jnp.mean(jnp.abs(W))
            Wq = scale * jnp.clip(jnp.round(W / scale), -1.0, 1.0)
            return W + jax.lax.stop_gradient(Wq - W)

        def oct_ternary_linear(xp, W):
            Wq = ternary_dequant(W)
            M = jnp.einsum('jik,jod->koid', S_OCT, Wq)
            return jnp.einsum('...id,koid->...ko', xp, M)
        key = jax.random.key(seed)
        k1, k2, k3, k4 = jax.random.split(key, 4)
        B, T = (2, 256)
        d8, h8 = (N_EMBD // 8, HIDDEN // 8)
        std_in = 1.0 / np.sqrt(N_EMBD)
        std_h = 1.0 / np.sqrt(HIDDEN)
        return {'x': jax.random.normal(k1, (B, T, N_EMBD), jnp.float32), 'w_gate': jax.random.normal(k2, (8, h8, d8), jnp.float32) * std_in, 'w_up': jax.random.normal(k3, (8, h8, d8), jnp.float32) * std_in, 'w_down': jax.random.normal(k4, (8, d8, h8), jnp.float32) * std_h}
    _L0_ffn_in = _L0_ffn_setup()

    def _L1_attn_setup():
        import jax, jax.numpy as jnp
        import numpy as np
        B, S, HID = (1, 256, 512)
        H, HK, D = (32, 8, 128)
        L = D // 4
        key = jax.random.key(seed)
        ks = jax.random.split(key, 7)
        s = 0.02
        return {'hidden_states': jax.random.normal(ks[0], (B, S, HID), jnp.float32), 'Wq': jax.random.normal(ks[1], (H * D, HID), jnp.float32) * s, 'Wk_down': jax.random.normal(ks[2], (HK * L, HID), jnp.float32) * s, 'Wv_down': jax.random.normal(ks[3], (HK * L, HID), jnp.float32) * s, 'Wk_up': jax.random.normal(ks[4], (HK * D, HK * L), jnp.float32) * s, 'Wv_up': jax.random.normal(ks[5], (HK * D, HK * L), jnp.float32) * s, 'Wo': jax.random.normal(ks[6], (HID, H * D), jnp.float32) * s}
    _L1_attn_in = _L1_attn_setup()

    def _L1_ffn_setup():
        import jax, jax.numpy as jnp
        import numpy as np
        B, S, D, O, R, E = (4, 256, 512, 512, 16, 8)
        SCALING = 32.0 / 16.0
        key = jax.random.key(seed)
        ks = jax.random.split(key, 7)
        x = jax.random.normal(ks[0], (B, S, D), dtype=jnp.float32)
        W_base = jax.random.normal(ks[1], (O, D), dtype=jnp.float32) * 0.02
        b_base = jnp.zeros((O,), dtype=jnp.float32)
        A_w = jax.random.normal(ks[2], (R, D), dtype=jnp.float32) * 0.02
        B_w = jax.random.normal(ks[3], (O, R), dtype=jnp.float32) * 0.02
        router_w = jax.random.normal(ks[4], (E, D), dtype=jnp.float32) * 0.02
        cores = jax.random.normal(ks[5], (E, R, R), dtype=jnp.float32)
        return {'x': x, 'W_base': W_base, 'b_base': b_base, 'A_w': A_w, 'B_w': B_w, 'router_w': router_w, 'cores': cores}
    _L1_ffn_in = _L1_ffn_setup()
    _d = {'L0_attn_x': _L0_attn_in['x'], 'L0_attn_attn_qkvw': _L0_attn_in['attn_qkvw'], 'L0_attn_attn_qkvb': _L0_attn_in['attn_qkvb'], 'L0_attn_attn_ow': _L0_attn_in['attn_ow'], 'L0_attn_attn_ob': _L0_attn_in['attn_ob'], 'L0_ffn_w_gate': _L0_ffn_in['w_gate'], 'L0_ffn_w_up': _L0_ffn_in['w_up'], 'L0_ffn_w_down': _L0_ffn_in['w_down'], 'L1_attn_Wq': _L1_attn_in['Wq'], 'L1_attn_Wk_down': _L1_attn_in['Wk_down'], 'L1_attn_Wv_down': _L1_attn_in['Wv_down'], 'L1_attn_Wk_up': _L1_attn_in['Wk_up'], 'L1_attn_Wv_up': _L1_attn_in['Wv_up'], 'L1_attn_Wo': _L1_attn_in['Wo'], 'L1_ffn_W_base': _L1_ffn_in['W_base'], 'L1_ffn_b_base': _L1_ffn_in['b_base'], 'L1_ffn_A_w': _L1_ffn_in['A_w'], 'L1_ffn_B_w': _L1_ffn_in['B_w'], 'L1_ffn_router_w': _L1_ffn_in['router_w'], 'L1_ffn_cores': _L1_ffn_in['cores']}
    _x0 = _d['L0_attn_x']
    _d['L0_attn_x'] = jax.random.normal(jax.random.fold_in(jax.random.key(seed), 1), (2, 512, 512), dtype=_x0.dtype)
    del _x0
    return _d

def reference(L0_attn_x, L0_attn_attn_qkvw, L0_attn_attn_qkvb, L0_attn_attn_ow, L0_attn_attn_ob, L0_ffn_w_gate, L0_ffn_w_up, L0_ffn_w_down, L1_attn_Wq, L1_attn_Wk_down, L1_attn_Wv_down, L1_attn_Wk_up, L1_attn_Wv_up, L1_attn_Wo, L1_ffn_W_base, L1_ffn_b_base, L1_ffn_A_w, L1_ffn_B_w, L1_ffn_router_w, L1_ffn_cores):

    def _L0_attn_ref(x, attn_qkvw, attn_qkvb, attn_ow, attn_ob):
        import jax, jax.numpy as jnp
        import numpy as np
        HEADS = 32
        B, S, H = x.shape
        hd = H // HEADS
        scale = 1.0 / np.sqrt(hd)
        qkv = x @ attn_qkvw + attn_qkvb
        qkv = qkv.reshape(B, S, 3, HEADS, hd)
        q = jnp.transpose(qkv[:, :, 0], (0, 2, 1, 3))
        k = jnp.transpose(qkv[:, :, 1], (0, 2, 1, 3))
        v = jnp.transpose(qkv[:, :, 2], (0, 2, 1, 3))
        scores = jnp.einsum('bhqd,bhkd->bhqk', q, k) * scale
        probs = jax.nn.softmax(scores, axis=-1)
        ctx = jnp.einsum('bhqk,bhkd->bhqd', probs, v)
        ctx = jnp.transpose(ctx, (0, 2, 1, 3)).reshape(B, S, H)
        return ctx @ attn_ow + attn_ob

    def _L0_ffn_ref(x, w_gate, w_up, w_down):
        import jax, jax.numpy as jnp
        import numpy as np
        _TRIPLES = [(1, 2, 3), (1, 4, 5), (1, 7, 6), (2, 4, 6), (2, 5, 7), (3, 4, 7), (3, 6, 5)]

        def _oct_struct():
            S = np.zeros((8, 8, 8), np.float32)
            S[0, 0, 0] = 1.0
            for i in range(1, 8):
                S[0, i, i] = 1.0
                S[i, 0, i] = 1.0
                S[i, i, 0] = -1.0
            for a, b, c in _TRIPLES:
                for x, y, z in ((a, b, c), (b, c, a), (c, a, b)):
                    S[x, y, z] = 1.0
                    S[y, x, z] = -1.0
            return jnp.asarray(S)
        S_OCT = _oct_struct()
        N_EMBD = 512
        HIDDEN = 1366

        def ternary_dequant(W):
            scale = jnp.mean(jnp.abs(W))
            Wq = scale * jnp.clip(jnp.round(W / scale), -1.0, 1.0)
            return W + jax.lax.stop_gradient(Wq - W)

        def oct_ternary_linear(xp, W):
            Wq = ternary_dequant(W)
            M = jnp.einsum('jik,jod->koid', S_OCT, Wq)
            return jnp.einsum('...id,koid->...ko', xp, M)
        B, T, D = x.shape
        xp = x.reshape(B, T, 8, D // 8)
        gate = oct_ternary_linear(xp, w_gate).reshape(B, T, -1)
        up = oct_ternary_linear(xp, w_up).reshape(B, T, -1)
        h = jax.nn.silu(gate) * up
        hp = h.reshape(B, T, 8, h.shape[-1] // 8)
        out = oct_ternary_linear(hp, w_down).reshape(B, T, D)
        return out

    def _L1_attn_ref(hidden_states, Wq, Wk_down, Wv_down, Wk_up, Wv_up, Wo):
        import jax, jax.numpy as jnp
        import numpy as np
        B, S, HID = (1, 256, 512)
        H, HK, D = (32, 8, 128)
        L = D // 4
        b, s, _ = hidden_states.shape
        q = (hidden_states @ Wq.T).reshape(b, s, H, D).transpose(0, 2, 1, 3)
        kc = (hidden_states @ Wk_down.T).reshape(b, s, HK, L).transpose(0, 2, 1, 3)
        vc = (hidden_states @ Wv_down.T).reshape(b, s, HK, L).transpose(0, 2, 1, 3)
        lat = jnp.concatenate([kc, vc], axis=-1).reshape(b, s, HK * 2 * L)
        k_cmp, v_cmp = jnp.split(lat, 2, axis=-1)
        k = (k_cmp @ Wk_up.T).reshape(b, s, HK, D).transpose(0, 2, 1, 3)
        v = (v_cmp @ Wv_up.T).reshape(b, s, HK, D).transpose(0, 2, 1, 3)
        n_rep = H // HK
        k = jnp.repeat(k, n_rep, axis=1)
        v = jnp.repeat(v, n_rep, axis=1)
        scale = 1.0 / jnp.sqrt(jnp.asarray(D, hidden_states.dtype))
        scores = jnp.einsum('bhqd,bhkd->bhqk', q, k) * scale
        causal = jnp.tril(jnp.ones((s, s), dtype=bool))
        scores = jnp.where(causal, scores, jnp.asarray(-1000000000.0, scores.dtype))
        attn = jax.nn.softmax(scores, axis=-1)
        out = jnp.einsum('bhqk,bhkd->bhqd', attn, v)
        out = out.transpose(0, 2, 1, 3).reshape(b, s, H * D)
        return out @ Wo.T

    def _L1_ffn_ref(x, W_base, b_base, A_w, B_w, router_w, cores):
        import jax, jax.numpy as jnp
        import numpy as np
        B, S, D, O, R, E = (4, 256, 512, 512, 16, 8)
        SCALING = 32.0 / 16.0
        result = jnp.einsum('bsd,od->bso', x, W_base) + b_base
        ax = jnp.einsum('bsd,rd->bsr', x, A_w)
        probs = jax.nn.softmax(jnp.einsum('bsd,ed->bse', x, router_w), axis=-1)
        per_expert = jnp.einsum('bsr,erq->bseq', ax, cores)
        mixed = jnp.einsum('bseq,bse->bsq', per_expert, probs)
        result = result + jnp.einsum('bsr,or->bso', mixed, B_w) * SCALING
        return result
    x = L0_attn_x
    x = x + _layernorm(_L0_attn_ref(_layernorm(x, axis=-1), L0_attn_attn_qkvw, L0_attn_attn_qkvb, L0_attn_attn_ow, L0_attn_attn_ob), axis=-1)
    x = x + _layernorm(_L0_ffn_ref(_layernorm(x, axis=-1), L0_ffn_w_gate, L0_ffn_w_up, L0_ffn_w_down), axis=-1)
    x = x + _layernorm(_L1_attn_ref(_layernorm(x, axis=-1), L1_attn_Wq, L1_attn_Wk_down, L1_attn_Wv_down, L1_attn_Wk_up, L1_attn_Wv_up, L1_attn_Wo), axis=-1)
    x = x + _layernorm(_L1_ffn_ref(_layernorm(x, axis=-1), L1_ffn_W_base, L1_ffn_b_base, L1_ffn_A_w, L1_ffn_B_w, L1_ffn_router_w, L1_ffn_cores), axis=-1)
    return x

_drawn_inputs = setup_inputs


def setup_inputs(seed=0):
    import zlib

    import numpy as np

    out = dict(_drawn_inputs(seed))
    spreads = {'L1_ffn_b_base': (0.0, 0.1)}
    factors = {'L1_attn_Wq': 3.485, 'L1_attn_Wk_up': 3.429}
    for name, (base, spread) in spreads.items():
        noise = np.random.default_rng([zlib.crc32(name.encode()), seed]).standard_normal(out[name].shape)
        drawn = base * np.exp(spread * noise) if base else spread * noise
        out[name] = jnp.asarray(drawn.astype(out[name].dtype))
    for name, factor in factors.items():
        out[name] = (out[name] * factor).astype(out[name].dtype)
    return out
```

```python
from contextlib import ExitStack

import concourse.bass as bass
from concourse import mybir

F32 = mybir.dt.float32
F32R = mybir.dt.float32r
ACT = mybir.ActivationFunctionType
ALU = mybir.AluOpType
AX_X = mybir.AxisListType.X

P = 128
B, S, D = 2, 512, 512
TOK = B * S
NT = TOK // P
QT = S // P
KC = D // P
EPS = 1e-5

H0, HD0 = 32, 16
HPC = P // HD0

O8 = 8
DI = D // O8
DH = 1366 // O8
MAIN = P
REM = DH - MAIN
NHC = O8 + O8 // 2

H1, HK, D1 = 32, 8, 128
LAT = D1 // 4
REP = H1 // HK
NLAT = HK * LAT
LC = NLAT // P

R, E = 16, 8
LORA_SCALE = 32.0 / 16.0

TRIPLES = [(1, 2, 3), (1, 4, 5), (1, 7, 6), (2, 4, 6), (2, 5, 7), (3, 4, 7), (3, 6, 5)]
MASKED = -1.0e30


def octonion_table():
    s = {(0, 0, 0): 1}
    for i in range(1, 8):
        s[0, i, i] = 1
        s[i, 0, i] = 1
        s[i, i, 0] = -1
    for a, b, c in TRIPLES:
        for x, y, z in ((a, b, c), (b, c, a), (c, a, b)):
            s[x, y, z] = 1
            s[y, x, z] = -1
    return {(i, k): (j, v) for (j, i, k), v in s.items()}


OCT = octonion_table()


def settle(eng):
    eng.nop(nofuse=True)


def program(nc, a, out, stop="all"):
    with ExitStack() as whole:
        bank = [whole.enter_context(nc.psum_tensor(f"bank{i}", [P, 512], F32)) for i in range(8)]

        def sems(stack, names):
            got = [nc.alloc_semaphore(n) for n in names.split()]

            def clear():
                nc.clear_and_free_semaphores(got)
                nc.all_engine_barrier()
            stack.callback(clear)
            return got

        def sb(stack, name, shape, dt=F32):
            return stack.enter_context(nc.sbuf_tensor(name, shape, dt))

        ident = sb(whole, "ident", [P, P])
        neghalf = sb(whole, "neghalf", [P, 1])
        xT_hi = sb(whole, "xT_hi", [P, KC, TOK], F32R)
        xT_lo = sb(whole, "xT_lo", [P, KC, TOK], F32R)
        x_mid = nc.dram_tensor("x_mid", (TOK, D), F32, kind="Internal").ap()

        with ExitStack() as first:
            x_res = sb(first, "x_res", [P, NT, D])
            ctx0 = sb(first, "ctx0", [P, NT, D])
            with ExitStack() as st:
                qk = sb(st, "qk", [P, 4, KC, TOK], F32R)
                v0 = sb(st, "v0", [P, NT, D])
                with ExitStack() as tmp:
                    project_qkv(nc, tmp, sb, sems, bank, a, ident, neghalf, x_res, ctx0, xT_hi, xT_lo, qk, v0)
                if stop == "A":
                    dump(nc, whole, sems, out, qk[:, 0:2, :, :].bitcast(F32).rearrange("p a b c -> p (a b c)")[:, 0:4096])
                    return
                with ExitStack() as tmp:
                    attention0(nc, tmp, sb, sems, bank, ident, qk, v0, ctx0)
            if stop == "B":
                dump(nc, whole, sems, out, ctx0[:, :, :])
                return
            with ExitStack() as tmp:
                middle(nc, tmp, sb, sems, bank, a, ident, neghalf, x_res, ctx0, xT_hi, xT_lo, x_mid)
            if stop == "C":
                dump(nc, whole, sems, out, x_res[:, :, :])
                return
        y1 = sb(whole, "y1", [P, NT, D])
        with ExitStack() as tmp:
            attention1(nc, tmp, sb, sems, bank, a, ident, xT_hi, xT_lo, y1)
        if stop == "D":
            dump(nc, whole, sems, out, y1[:, :, :])
            return
        with ExitStack() as tmp:
            cores_ffn(nc, tmp, sb, sems, bank, a, ident, neghalf, y1, x_mid, out)


def dump(nc, st, sems, out, what):
    (s,) = sems(st, "dumped")
    with nc.Block() as block:
        @block.sync
        def _(sp):
            dst = out.rearrange("(t p) h -> p t h", p=P)
            src = what if len(what.shape) == 3 else what.rearrange("p (t h) -> p t h", t=NT)
            sp.dma_start(dst, src).then_inc(s, 16)
            sp.wait_ge(s, 16)


def project_qkv(nc, st, sb, sems, bank, a, ident, neghalf, x_res, ctx0, xT_hi, xT_lo, qk, v0):
    scale = HD0 ** -0.5
    w_hi = sb(st, "wqkv_hi", [P, KC, 3 * D], F32R)
    w_lo = sb(st, "wqkv_lo", [P, KC, 3 * D], F32R)
    raw = [ctx0[:, 0:KC, :], ctx0[:, KC:2 * KC, :], sb(st, "raw_v", [P, KC, D])[:, :, :]]
    bias = sb(st, "qkv_bias", [P, 3 * KC])
    bias_q = sb(st, "q_bias_scaled", [P, KC])
    v_bias = sb(st, "v_bias", [P, D])
    stats = sb(st, "statsA", [P, 6])
    mv = sb(st, "mvA", [P, 2])
    veps = sb(st, "vepsA", [P, 1])
    rstd = sb(st, "rstdA", [P, 1])
    xn = sb(st, "xnA", [P, 2, D])
    (x_in, w_in, small_in, ident_ok, zeroed, stat, aggr, eps_added, rstd_ok, normed, turned, xT_hi_ok, xT_lo_ok,
     w_hi_ok, w_lo_ok, qbias_ok, proj, out_hi, out_lo, v_out) = sems(
        st, "A_x_in A_w_in A_small_in A_ident A_zeroed A_stat A_aggr A_eps A_rstd A_normed A_turned A_xT_hi A_xT_lo "
            "A_w_hi A_w_lo A_qbias A_proj A_out_hi A_out_lo A_v_out")
    x_v = a["x"].rearrange("(t p) h -> p t h", p=P)
    w_v = a["qkvw"].rearrange("(c p) n -> p c n", p=P)
    w_sems = [w_in] + sems(st, "A_wk_in A_wv_in")
    NM = 2 * KC

    with nc.Block() as block:
        @block.sync
        def _(sp):
            sp.dma_start(x_res[:, :, :], x_v).then_inc(x_in, 16)
            for n in range(3):
                sp.dma_start(raw[n], w_v[:, :, n * D:(n + 1) * D]).then_inc(w_sems[n], 16)
            sp.dma_start(bias[:, :], a["qkvb_cols"]).then_inc(small_in, 16)
            sp.dma_start(v_bias[:, :], a["qkvb"][2 * D:3 * D].rearrange("(a n) -> a n", a=1).to_broadcast([P, D])
                         ).then_inc(small_in, 16)

        @block.gpsimd
        def _(pool):
            pool.memset(neghalf[:, :], -0.5).then_inc(zeroed, 1)
            pool.memset(ident[:, :], 0.0).then_inc(zeroed, 1)
            pool.wait_ge(zeroed, 2)
            pool.affine_select(out=ident[:, :], in_=ident[:, :], compare_op=ALU.not_equal, fill=1.0, base=0,
                               pattern=[[-1, P]], channel_multiplier=1).then_inc(ident_ok, 1)
            with pool.Fori(0, NT) as t:
                pool.wait_ge(aggr, t + 1)
                settle(pool)
                pool.tensor_scalar(veps[:, :], mv[:, 1:2], EPS, None, ALU.add).then_inc(eps_added, 1)
                pool.wait_ge(eps_added, t + 1)
                settle(pool)
                pool.tensor_tensor(rstd[:, :], veps[:, :], neghalf[:, :], ALU.pow).then_inc(rstd_ok, 1)

        @block.scalar
        def _(act):
            nc.scalar.preload_act_table(ACT.Exp)
            act.wait_ge(small_in, 32)
            act.activation(bias_q[:, :], bias[:, 0:KC], ACT.Copy, scale=scale).then_inc(qbias_ok, 1)
            for n in range(3):
                act.wait_ge(w_sems[n], 16)
                act.activation(w_hi[:, :, n * D:(n + 1) * D], raw[n], ACT.Copy,
                               scale=scale if n == 0 else 1.0).then_inc(w_hi_ok, 1)
            for t in range(NT):
                act.wait_ge(turned, t + 1)
                act.activation(xT_hi[:, :, t * P:(t + 1) * P], bank[t % 2][:, :].rearrange("p (c q) -> p c q", c=KC),
                               ACT.Copy).then_inc(xT_hi_ok, 1)
            act.wait_ge(qbias_ok, 1)
            for b in range(B):
                for m in range(NM):
                    j = b * NM + m
                    act.wait_ge(proj, j + 1)
                    dst = qk[:, 0 if m < KC else 2, m % KC, b * S:(b + 1) * S]
                    act.activation(dst, bank[2 + j % 4][:, :], ACT.Identity,
                                   bias=bias_q[:, m:m + 1] if m < KC else bias[:, m:m + 1]).then_inc(out_hi, 1)

        @block.vector
        def _(dve):
            dve.wait_ge(x_in, 16)
            for t in range(NT):
                if t:
                    dve.wait_ge(aggr, t)
                dve.bn_stats(stats[:, :], x_res[:, t, :]).then_inc(stat, 1)
                dve.wait_ge(stat, t + 1)
                if t:
                    dve.wait_ge(normed, t)
                dve.bn_aggr(mv[:, :], stats[:, :]).then_inc(aggr, 1)
                dve.wait_ge(rstd_ok, t + 1)
                if t >= 2:
                    dve.wait_ge(turned, t - 1)
                dve.tensor_scalar(xn[:, t % 2, :], x_res[:, t, :], mv[:, 0:1], rstd[:, :], ALU.subtract,
                                  ALU.mult).then_inc(normed, 1)
                if t < 3:
                    dve.wait_ge(w_hi_ok, t + 1)
                    dve.scalar_tensor_tensor(out=w_lo[:, :, t * D:(t + 1) * D], in0=raw[t],
                                             scalar=scale if t == 0 else 1.0,
                                             in1=w_hi[:, :, t * D:(t + 1) * D].bitcast(F32), op0=ALU.mult,
                                             op1=ALU.subtract).then_inc(w_lo_ok, 1)
                dve.wait_ge(xT_hi_ok, t + 1)
                dve.tensor_tensor(xT_lo[:, :, t * P:(t + 1) * P], bank[t % 2][:, :].rearrange("p (c q) -> p c q", c=KC),
                                  xT_hi[:, :, t * P:(t + 1) * P].bitcast(F32), ALU.subtract).then_inc(xT_lo_ok, 1)
            dve.wait_ge(qbias_ok, 1)
            for b in range(B):
                for m in range(NM):
                    j = b * NM + m
                    dve.wait_ge(out_hi, j + 1)
                    piece = 0 if m < KC else 2
                    cols = slice(b * S, (b + 1) * S)
                    dve.scalar_tensor_tensor(out=qk[:, piece + 1, m % KC, cols], in0=bank[2 + j % 4][:, :],
                                             scalar=bias_q[:, m:m + 1] if m < KC else bias[:, m:m + 1],
                                             in1=qk[:, piece, m % KC, cols].bitcast(F32), op0=ALU.add,
                                             op1=ALU.subtract).then_inc(out_lo, 1)
            for t in range(NT):
                dve.wait_ge(proj, B * NM + t + 1)
                dve.tensor_tensor(v0[:, t, :], bank[6 + t % 2][:, :], v_bias[:, :], ALU.add).then_inc(v_out, 1)

        @block.tensor
        def _(pe):
            pe.wait_ge(ident_ok, 1)
            for t in range(NT):
                pe.wait_ge(normed, t + 1)
                if t >= 2:
                    pe.wait_ge(xT_lo_ok, t - 1)
                for c in range(KC):
                    mm = pe.transpose(bank[t % 2][:, c * P:(c + 1) * P], xn[:, t % 2, c * P:(c + 1) * P], ident[:, :])
                mm.then_inc(turned, 1)
            pe.wait_ge(w_lo_ok, 3)
            for b in range(B):
                pe.wait_ge(xT_lo_ok, (b + 1) * QT)
                for m in range(NM):
                    j = b * NM + m
                    if j >= 4:
                        pe.wait_ge(out_lo, j - 3)
                    three(pe, bank[2 + j % 4][:, :], [
                        (w_hi[:, c, m * P:(m + 1) * P], w_lo[:, c, m * P:(m + 1) * P],
                         xT_hi[:, c, b * S:(b + 1) * S], xT_lo[:, c, b * S:(b + 1) * S]) for c in range(KC)]
                    ).then_inc(proj, 1)
            for t in range(NT):
                if t >= 2:
                    pe.wait_ge(v_out, t - 1)
                three(pe, bank[6 + t % 2][:, :], [
                    (xT_hi[:, c, t * P:(t + 1) * P], xT_lo[:, c, t * P:(t + 1) * P],
                     w_hi[:, c, 2 * D:3 * D], w_lo[:, c, 2 * D:3 * D]) for c in range(KC)]).then_inc(proj, 1)


def three(pe, dst, chunks, stop=True):
    steps = [p for s_hi, s_lo, m_hi, m_lo in chunks for p in ((s_hi, m_hi), (s_hi, m_lo), (s_lo, m_hi))]
    for n, (s, m) in enumerate(steps):
        mm = pe.matmul(dst, s, m, start=(n == 0), stop=(stop and n == len(steps) - 1))
    return mm


def attention0(nc, st, sb, sems, bank, ident, qk, v0, ctx0):
    G = 2 * B * QT
    SLOTS = 3 * HD0
    qks = [sb(st, f"qk_stack{i}", [SLOTS, 2, TOK], F32R) for i in range(2)]
    probs = [sb(st, f"probs{i}", [P, S]) for i in range(4)]
    probsT = [sb(st, f"probsT{i}", [P, QT, P]) for i in range(4)]
    negmax = sb(st, "negmax0", [P, 4])
    den = sb(st, "den0", [P, 2, QT])
    rden = sb(st, "rden0", [P, 2, QT])
    stk0, stk1, scored, maxed, exped, turned, copied, weighted, inverted, normed = sems(
        st, "B_stack0 B_stack1 B_scored B_maxed B_exped B_turned B_copied B_weighted B_inverted B_normed")
    stk = [stk0, stk1]
    DVE_COPIES = [k % 16 in (1, 3, 5, 8, 10, 12, 14) for k in range(G)]
    n_act = G - sum(DVE_COPIES)
    (copied_act,) = sems(st, "B_copied_act")
    by_dve = [sum(DVE_COPIES[:k]) for k in range(G + 1)]
    by_act = [k - by_dve[k] for k in range(G + 1)]
    LOOPS = H0 // 2
    UNITS_PER_HEAD = B * QT

    def wait_copied(eng, i, k):
        if k < 0:
            i, k = i - 1, k + G
        if DVE_COPIES[k]:
            eng.wait_ge(copied, i * by_dve[G] + by_dve[k + 1])
        else:
            eng.wait_ge(copied_act, i * by_act[G] + by_act[k + 1])

    with nc.Block() as block:
        @block.sync
        def _(sp):
            def stacks(c, first):
                for h8 in range(HPC):
                    rows = slice(h8 * HD0, (h8 + 1) * HD0)
                    if not (first and h8 < 2):
                        sp.wait_ge(scored, (c * HPC + h8 - 1) * UNITS_PER_HEAD)
                        settle(sp)
                    for slot, (pq, pk) in enumerate(((0, 2), (0, 3), (1, 2))):
                        for n, piece in enumerate((pq, pk)):
                            src = qk[rows, piece, c, :] if first else qk[rows, piece, bass.ds(c, 1), :]
                            dst = qks[h8 % 2][slot * HD0:(slot + 1) * HD0, n, :]
                            sp.dma_start(dst.bitcast(F32), src.bitcast(F32)).then_inc(stk[h8 % 2], 16)

            stacks(0, True)
            with sp.Fori(1, KC) as c:
                stacks(c, False)

        @block.tensor
        def _(pe):
            def scores(i, k):
                if k >= G:
                    i, k = i + 1, k - G
                head, b, q = k // UNITS_PER_HEAD, k // QT % B, k % QT
                if k % UNITS_PER_HEAD == 0:
                    pe.wait_ge(stk[head], (i + 1) * 96)
                yield_wait_exped(i, k)
                pe.matmul(bank[k % 4][:, :], qks[head][:, 0, b * S + q * P:b * S + (q + 1) * P],
                          qks[head][:, 1, b * S:(b + 1) * S], start=True, stop=True).then_inc(scored, 1)

            def yield_wait_exped(i, k):
                if not (isinstance(i, int) and i == 0 and k < 4):
                    pe.wait_ge(exped, i * G + k - 3)

            def unit(i, k, first, last):
                if not (last and k + 3 >= G):
                    scores(i, k + 3)
                pe.wait_ge(exped, i * G + k + 1)
                if not (first and k < 2):
                    wait_copied(pe, i, k - 2)
                for j in range(QT):
                    mm = pe.transpose(bank[4 + k % 2][:, j * P:(j + 1) * P], probs[k % 4][:, j * P:(j + 1) * P],
                                      ident[:, :])
                mm.then_inc(turned, 1)
                if not (first and k < 2):
                    context(i, k - 2)

            def context(i, k):
                if k < 0:
                    i, k = i - 1, k + G
                head, b, q = k // UNITS_PER_HEAD, k // QT % B, k % QT
                wait_copied(pe, i, k)
                m = k // QT
                if q == 0 and not (isinstance(i, int) and i == 0 and m < 2):
                    pe.wait_ge(normed, i * (G // QT) + m - 1)
                for j in range(QT):
                    mm = pe.matmul(bank[6 + m % 2][:, q * HD0:(q + 1) * HD0], probsT[k % 4][:, j, :],
                                   v0[:, b * QT + j, bass.ds(i * 2 * HD0 + head * HD0, HD0)],
                                   start=(j == 0), stop=(j == QT - 1))
                mm.then_inc(weighted, 1)

            for k in range(3):
                scores(0, k)
            for k in range(G):
                unit(0, k, True, False)
            with pe.Fori(1, LOOPS - 1) as i:
                for k in range(G):
                    unit(i, k, False, False)
            for k in range(G):
                unit(LOOPS - 1, k, False, True)
            context(LOOPS - 1, G - 2)
            context(LOOPS - 1, G - 1)

        @block.vector
        def _(dve):
            def head_max(i, k):
                if k >= G:
                    i, k = i + 1, k - G
                dve.wait_ge(scored, i * G + k + 1)
                if not (isinstance(i, int) and i == 0 and k < 4):
                    dve.wait_ge(exped, i * G + k - 3)
                dve.tensor_reduce(negmax[:, k % 4:k % 4 + 1], bank[k % 4][:, :], AX_X, ALU.max,
                                  negate=True).then_inc(maxed, 1)

            def normalise(i, m):
                if m < 0:
                    i, m = i - 1, m + G // QT
                g = i * (G // QT) + m
                head, b = m // B, m % B
                dve.wait_ge(exped, i * G + (m + 1) * QT)
                if not (isinstance(i, int) and i == 0 and m < 2):
                    dve.wait_ge(normed, g - 1)
                dve.reciprocal(rden[:, m % 2, :], den[:, m % 2, :]).then_inc(inverted, 1)
                dve.wait_ge(weighted, i * G + (m + 1) * QT)
                dve.wait_ge(inverted, g + 1)
                dve.tensor_tensor(ctx0[:, b * QT:(b + 1) * QT, bass.ds(i * 2 * HD0 + head * HD0, HD0)],
                                  bank[6 + m % 2][:, 0:QT * HD0].rearrange("p (q d) -> p q d", q=QT),
                                  rden[:, m % 2, :, None].to_broadcast([P, QT, HD0]), ALU.mult).then_inc(normed, 1)

            def unit(i, k, first, last):
                if not (last and k + 2 >= G):
                    head_max(i, k + 2)
                if not (first and k == 0):
                    copy(i, k - 1)
                if k % QT == 2 and not (first and k == 2):
                    normalise(i, k // QT - 1)

            def copy(i, k):
                if k < 0:
                    i, k = i - 1, k + G
                if DVE_COPIES[k]:
                    dve.wait_ge(turned, i * G + k + 1)
                    if not (isinstance(i, int) and i == 0 and k < 4):
                        dve.wait_ge(weighted, i * G + k - 3)
                    dve.tensor_copy(probsT[k % 4][:, :, :], bank[4 + k % 2][:, :].rearrange("p (j q) -> p j q", j=QT)
                                    ).then_inc(copied, 1)

            for k in range(2):
                head_max(0, k)
            for k in range(G):
                unit(0, k, True, False)
            with dve.Fori(1, LOOPS - 1) as i:
                for k in range(G):
                    unit(i, k, False, False)
            for k in range(G):
                unit(LOOPS - 1, k, False, True)
            copy(LOOPS - 1, G - 1)
            normalise(LOOPS - 1, G // QT - 1)

        @block.scalar
        def _(act):
            nc.scalar.preload_act_table(ACT.Exp)

            def exponent(i, k):
                if k >= G:
                    i, k = i + 1, k - G
                act.wait_ge(maxed, i * G + k + 1)
                if not (isinstance(i, int) and i == 0 and k < 4):
                    act.wait_ge(turned, i * G + k - 3)
                m = k // QT
                if k % QT == 0 and not (isinstance(i, int) and i == 0 and m < 2):
                    act.wait_ge(inverted, i * (G // QT) + m - 1)
                act.activation(probs[k % 4][:, :], bank[k % 4][:, :], ACT.Exp, bias=negmax[:, k % 4:k % 4 + 1],
                               accum_out=den[:, m % 2, k % QT:k % QT + 1]).then_inc(exped, 1)

            def unit(i, k, first, last):
                if not (last and k + 1 >= G):
                    exponent(i, k + 1)
                if not (first and k == 0):
                    copy(i, k - 1)

            def copy(i, k):
                if k < 0:
                    i, k = i - 1, k + G
                if not DVE_COPIES[k]:
                    act.wait_ge(turned, i * G + k + 1)
                    if not (isinstance(i, int) and i == 0 and k < 4):
                        act.wait_ge(weighted, i * G + k - 3)
                    act.activation(probsT[k % 4][:, :, :], bank[4 + k % 2][:, :].rearrange("p (j q) -> p j q", j=QT),
                                   ACT.Copy).then_inc(copied_act, 1)

            exponent(0, 0)
            for k in range(G):
                unit(0, k, True, False)
            with act.Fori(1, LOOPS - 1) as i:
                for k in range(G):
                    unit(i, k, False, False)
            for k in range(G):
                unit(LOOPS - 1, k, False, True)
            copy(LOOPS - 1, G - 1)


def middle(nc, st, sb, sems, bank, a, ident, neghalf, x_res, ctx0, xT_hi, xT_lo, x_mid):
    ow_hi = sb(st, "ow_hi", [P, KC, D], F32R)
    ow_lo = sb(st, "ow_lo", [P, KC, D], F32R)
    m_gate = sb(st, "m_gate", [P, KC, O8, DH], F32R)
    m_up = sb(st, "m_up", [P, KC, O8, DH], F32R)
    m_down = sb(st, "m_down", [P, NHC, D], F32R)
    ob = sb(st, "ob", [P, D])
    scales = sb(st, "tern_scales", [P, 3])
    with ExitStack() as tmp:
        build_ternary(nc, tmp, sb, sems, bank, a, ow_hi, ow_lo, m_gate, m_up, m_down, ob, scales)

    cs = sb(st, "ctx_tile", [P, D])
    cT_hi = sb(st, "cT_hi", [P, KC, P], F32R)
    cT_lo = sb(st, "cT_lo", [P, KC, P], F32R)
    tT_hi = sb(st, "tT_hi", [P, KC, P], F32R)
    tT_lo = sb(st, "tT_lo", [P, KC, P], F32R)
    gact = sb(st, "gact", [P, 3, D])
    h = sb(st, "hidden", [P, NHC * P])
    hT_hi = sb(st, "hT_hi", [P, NHC, P], F32R)
    hT_lo = sb(st, "hT_lo", [P, NHC, P], F32R)
    y = sb(st, "y_attn", [P, D])
    y2 = sb(st, "y_ffn", [P, D])
    xn1 = sb(st, "xn1", [P, D])
    xn2 = sb(st, "xn2", [P, D])
    stats = sb(st, "statsC", [P, 4, 6])
    mv = sb(st, "mvC", [P, 4, 2])
    veps = sb(st, "vepsC", [P, 4, 1])
    rstd = sb(st, "rstdC", [P, 4, 1])
    (zeroed, cs_ok, c_turned, cT_hi_ok, cT_lo_ok, o_done, y_ok, x_turned, tT_hi_ok, tT_lo_ok, gu_done, act_ok, h_ok,
     h_turned, hT_hi_ok, hT_lo_ok, d_done, y2_ok, x2_turned, xT_hi_ok, xT_lo_ok, x1_ok, x2_ok,
     stored) = sems(
        st, "C_zeroed C_cs C_c_turned C_cT_hi C_cT_lo C_o_done C_y C_x_turned C_tT_hi C_tT_lo C_gu_done C_act C_h "
            "C_h_turned C_hT_hi C_hT_lo C_d_done C_y2 C_x2_turned C_xT_hi C_xT_lo C_x1 C_x2 C_stored")
    stat, aggr, eps_ok, rstd_ok, applied = (sems(st, " ".join(f"C_{n}{k}" for k in range(4)))
                                            for n in ("stat", "aggr", "eps", "rstd", "applied"))
    h_main = h[:, 0:O8 * P].rearrange("p (i d) -> p i d", i=O8)
    h_rem = h[:, O8 * P:].rearrange("p (i d) -> p i d", i=O8)
    mid_v = x_mid.rearrange("(t p) h -> p t h", p=P)
    HI = O8 // 2

    def tile_of(buf, t):
        return buf[:, t, :] if isinstance(t, int) else buf[:, bass.ds(t, 1), :]

    def columns_of(buf, t):
        return buf[:, :, t * P:(t + 1) * P] if isinstance(t, int) else buf[:, :, bass.ds(t * P, P)]

    def steps(eng, before, step):
        before()
        step(0, True, False)
        with eng.Fori(1, NT - 1) as t:
            step(t, False, False)
        step(NT - 1, False, True)

    def quads(b):
        return b[:, :].rearrange("p (c q) -> p c q", c=KC)

    with nc.Block() as block:
        @block.sync
        def _(sp):
            def store(t, first, last):
                sp.wait_ge(x2_ok, t + 1)
                sp.dma_start(tile_of(mid_v, t), tile_of(x_res, t)).then_inc(stored, 16)
            steps(sp, lambda: None, store)
            sp.wait_ge(stored, 16 * NT)

        @block.gpsimd
        def _(pool):
            def power(n, t):
                pool.wait_ge(eps_ok[n], t + 1)
                settle(pool)
                pool.tensor_tensor(rstd[:, n, :], veps[:, n, :], neghalf[:, :], ALU.pow).then_inc(rstd_ok[n], 1)

            def stage(t):
                if not (isinstance(t, int) and t == 0):
                    pool.wait_ge(c_turned, t)
                    settle(pool)
                pool.tensor_copy(cs[:, :], tile_of(ctx0, t)).then_inc(cs_ok, 1)

            def before():
                pool.memset(h[:, O8 * P:], 0.0).then_inc(zeroed, 1)
                stage(0)
                power(0, 0)
                stage(1)
                power(1, 0)

            def step(t, first, last):
                if not first:
                    power(2, t - 1)
                    power(3, t - 1)
                if not last:
                    power(0, t + 1)
                    power(1, t + 1)

            before()
            step(0, True, False)
            with pool.Fori(1, NT - 1) as t:
                stage(t + 1)
                step(t, False, False)
            step(NT - 1, False, True)
            power(2, NT - 1)
            power(3, NT - 1)

        @block.tensor
        def _(pe):
            def turn(src, dst, sem):
                for c in range(KC):
                    mm = pe.transpose(dst[:, c * P:(c + 1) * P], src[:, c * P:(c + 1) * P], ident[:, :])
                mm.then_inc(sem, 1)

            def turn_ctx(t, first):
                pe.wait_ge(cs_ok, t + 1)
                if not first:
                    pe.wait_ge(xT_lo_ok, t - 1)
                turn(cs, bank[0], c_turned)

            def project(t, first):
                pe.wait_ge(cT_lo_ok, t + 1)
                if not first:
                    pe.wait_ge(y2_ok, t - 1)
                three(pe, bank[1][:, :], [(cT_hi[:, c, :], cT_lo[:, c, :], ow_hi[:, c, :], ow_lo[:, c, :])
                                          for c in range(KC)]).then_inc(o_done, 1)

            def turn_x1(t):
                pe.wait_ge(applied[1], t + 1)
                turn(xn1, bank[0], x_turned)

            def turn_x2(t):
                pe.wait_ge(applied[3], t + 1)
                turn(xn2, bank[0], x2_turned)

            def before():
                turn_ctx(0, True)
                project(0, True)
                turn_x1(0)

            def step(t, first, last):
                pe.wait_ge(tT_lo_ok, t + 1)
                for g in range(3):
                    if not first:
                        pe.wait_ge(hT_lo_ok, 3 * t - 2 + g)
                        pe.wait_ge(h_ok, 3 * t - 2 + g)
                    for m, b in ((m_gate, bank[2 + g]), (m_up, bank[5 + g])):
                        dst = b[:, :] if g < 2 else b[:, 0:O8 * REM]
                        mats = [m[:, c, g * HI:(g + 1) * HI, 0:MAIN] if g < 2 else m[:, c, :, MAIN:DH]
                                for c in range(KC)]
                        for n, (s, c) in enumerate((s, c) for c in range(KC) for s in (tT_hi, tT_lo)):
                            mm = pe.matmul(dst, s[:, c, :], mats[c], start=(n == 0), stop=(n == 2 * KC - 1))
                    mm.then_inc(gu_done, 1)
                if not first:
                    turn_x2(t - 1)
                if not last:
                    turn_ctx(t + 1, first)
                    project(t + 1, first)
                for g in range(3):
                    pe.wait_ge(h_ok, 3 * t + g + 1)
                    for c in range(KC):
                        n = g * KC + c
                        mm = pe.transpose(bank[2 + g][:, c * P:(c + 1) * P], h[:, n * P:(n + 1) * P], ident[:, :])
                    mm.then_inc(h_turned, 1)
                if not last:
                    pe.wait_ge(y_ok, t + 2)
                else:
                    pe.wait_ge(y2_ok, t)
                for n in range(NHC):
                    if n % KC == 0:
                        pe.wait_ge(hT_lo_ok, 3 * t + n // KC + 1)
                    for s in (hT_hi, hT_lo):
                        mm = pe.matmul(bank[1][:, :], s[:, n, :], m_down[:, n, :], start=(n == 0 and s is hT_hi),
                                       stop=(n == NHC - 1 and s is hT_lo))
                mm.then_inc(d_done, 1)
                if not last:
                    turn_x1(t + 1)

            steps(pe, before, step)
            turn_x2(NT - 1)

        @block.scalar
        def _(act):
            nc.scalar.preload_act_table(ACT.Silu)

            def split_ctx(t, first):
                act.wait_ge(c_turned, t + 1)
                if not first:
                    act.wait_ge(o_done, t)
                act.activation(cT_hi[:, :, :], quads(bank[0]), ACT.Copy).then_inc(cT_hi_ok, 1)

            def split_x1(t, first):
                act.wait_ge(x_turned, t + 1)
                if not first:
                    act.wait_ge(gu_done, 3 * t)
                act.activation(tT_hi[:, :, :], quads(bank[0]), ACT.Copy).then_inc(tT_hi_ok, 1)

            def split_x2(t):
                act.wait_ge(x2_turned, t + 1)
                settle(act)
                act.activation(columns_of(xT_hi, t), quads(bank[0]), ACT.Copy).then_inc(xT_hi_ok, 1)

            def before():
                split_ctx(0, True)
                split_x1(0, True)

            def step(t, first, last):
                for g in range(3):
                    n = D if g < 2 else O8 * REM
                    act.wait_ge(gu_done, 3 * t + g + 1)
                    if not first:
                        act.wait_ge(h_ok, 3 * t - 2 + g)
                    act.activation(gact[:, g, 0:n], bank[2 + g][:, 0:n], ACT.Silu, scale=scales[:, 0:1]
                                   ).then_inc(act_ok, 1)
                if not first:
                    split_x2(t - 1)
                if not last:
                    split_ctx(t + 1, False)
                for g in range(3):
                    act.wait_ge(h_turned, 3 * t + g + 1)
                    if not first:
                        act.wait_ge(d_done, t)
                    act.activation(hT_hi[:, g * KC:(g + 1) * KC, :], quads(bank[2 + g]), ACT.Copy
                                   ).then_inc(hT_hi_ok, 1)
                if not last:
                    split_x1(t + 1, False)
                act.wait_ge(d_done, t + 1)
                if not first:
                    act.wait_ge(applied[2], t)
                act.activation(y2[:, :], bank[1][:, :], ACT.Copy, scale=scales[:, 2:3]).then_inc(y2_ok, 1)

            steps(act, before, step)
            split_x2(NT - 1)

        @block.vector
        def _(dve):
            def statistics(n, t, src, ready, first):
                dve.wait_ge(ready, t + 1)
                if not first:
                    dve.wait_ge(aggr[n], t)
                    settle(dve)
                dve.bn_stats(stats[:, n, :], src).then_inc(stat[n], 1)
                dve.wait_ge(stat[n], t + 1)
                if not first:
                    dve.wait_ge(applied[n], t)
                settle(dve)
                dve.bn_aggr(mv[:, n, :], stats[:, n, :]).then_inc(aggr[n], 1)
                dve.wait_ge(aggr[n], t + 1)
                if not first:
                    dve.wait_ge(rstd_ok[n], t)
                dve.tensor_scalar(veps[:, n, :], mv[:, n, 1:2], EPS, None, ALU.add).then_inc(eps_ok[n], 1)

            def apply(n, t, dst, src):
                dve.wait_ge(rstd_ok[n], t + 1)
                dve.tensor_scalar(dst, src, mv[:, n, 0:1], rstd[:, n, :], ALU.subtract, ALU.mult
                                  ).then_inc(applied[n], 1)

            def attention_out(t, first):
                dve.wait_ge(o_done, t + 1)
                if not first:
                    dve.wait_ge(x1_ok, t)
                dve.tensor_tensor(y[:, :], bank[1][:, :], ob[:, :], ALU.add).then_inc(y_ok, 1)
                statistics(0, t, y[:, :], y_ok, first)

            def first_residual(t, first):
                apply(0, t, y[:, :], y[:, :])
                dve.wait_ge(applied[0], t + 1)
                dve.tensor_tensor(tile_of(x_res, t), tile_of(x_res, t), y[:, :], ALU.add).then_inc(x1_ok, 1)
                statistics(1, t, tile_of(x_res, t), x1_ok, first)
                if not first:
                    dve.wait_ge(x_turned, t)
                apply(1, t, xn1[:, :], tile_of(x_res, t))

            def low(sem_hi, t, dst, hi, src, sem):
                dve.wait_ge(sem_hi, t + 1)
                dve.tensor_tensor(dst, src, hi.bitcast(F32), ALU.subtract).then_inc(sem, 1)

            def second_residual(t, first):
                statistics(2, t, y2[:, :], y2_ok, first)
                apply(2, t, y2[:, :], y2[:, :])

            def second_norm(t, first):
                dve.wait_ge(applied[2], t + 1)
                dve.tensor_tensor(tile_of(x_res, t), tile_of(x_res, t), y2[:, :], ALU.add).then_inc(x2_ok, 1)
                statistics(3, t, tile_of(x_res, t), x2_ok, first)
                if not first:
                    dve.wait_ge(x2_turned, t)
                apply(3, t, xn2[:, :], tile_of(x_res, t))

            def before():
                low(cT_hi_ok, 0, cT_lo[:, :, :], cT_hi[:, :, :], quads(bank[0]), cT_lo_ok)
                attention_out(0, True)
                first_residual(0, True)
                low(tT_hi_ok, 0, tT_lo[:, :, :], tT_hi[:, :, :], quads(bank[0]), tT_lo_ok)
                dve.wait_ge(zeroed, 1)

            def step(t, first, last):
                if not first:
                    second_residual(t - 1, isinstance(t, int) and t == 1)
                    second_norm(t - 1, isinstance(t, int) and t == 1)
                for g in range(3):
                    dve.wait_ge(act_ok, 3 * t + g + 1)
                    if not first:
                        dve.wait_ge(h_turned, 3 * t - 2 + g)
                    if g < 2:
                        dve.tensor_tensor(h_main[:, g * HI:(g + 1) * HI, :],
                                          gact[:, g, :].rearrange("p (i d) -> p i d", i=HI),
                                          bank[5 + g][:, :].rearrange("p (i d) -> p i d", i=HI), ALU.mult
                                          ).then_inc(h_ok, 1)
                    else:
                        dve.tensor_tensor(h_rem[:, :, 0:REM],
                                          gact[:, g, 0:O8 * REM].rearrange("p (i d) -> p i d", i=O8),
                                          bank[5 + g][:, 0:O8 * REM].rearrange("p (i d) -> p i d", i=O8), ALU.mult
                                          ).then_inc(h_ok, 1)
                if not first:
                    low(xT_hi_ok, t - 1, columns_of(xT_lo, t - 1), columns_of(xT_hi, t - 1), quads(bank[0]), xT_lo_ok)
                if not last:
                    low(cT_hi_ok, t + 1, cT_lo[:, :, :], cT_hi[:, :, :], quads(bank[0]), cT_lo_ok)
                    attention_out(t + 1, False)
                for g in range(3):
                    low(hT_hi_ok, 3 * t + g, hT_lo[:, g * KC:(g + 1) * KC, :], hT_hi[:, g * KC:(g + 1) * KC, :],
                        quads(bank[2 + g]), hT_lo_ok)
                if not last:
                    first_residual(t + 1, False)
                    low(tT_hi_ok, t + 1, tT_lo[:, :, :], tT_hi[:, :, :], quads(bank[0]), tT_lo_ok)

            before()
            step(0, True, False)
            step(1, False, False)
            with dve.Fori(2, NT - 1) as t:
                step(t, False, False)
            step(NT - 1, False, True)
            second_residual(NT - 1, False)
            second_norm(NT - 1, False)
            low(xT_hi_ok, NT - 1, columns_of(xT_lo, NT - 1), columns_of(xT_hi, NT - 1), quads(bank[0]), xT_lo_ok)


def build_ternary(nc, st, sb, sems, bank, a, ow_hi, ow_lo, m_gate, m_up, m_down, ob, scales):
    N_W = O8 * DH * DI
    ow_raw = sb(st, "ow_raw", [P, KC, D])
    raw = [sb(st, n, s) for n, s in (("gate_raw", [P, O8, DH]), ("up_raw", [P, O8, DH]),
                                     ("down_raw", [P, O8, DI]), ("down_rem_raw", [P, O8, DI]))]
    above = [sb(st, f"above{i}", list(r.shape)) for i, r in enumerate(raw)]
    ones = sb(st, "ones_sq", [P, P])
    sums = sb(st, "sums", [P, 4])
    means = sb(st, "means", [P, 4])
    half = sb(st, "half", [P, 2, 3])
    (w_in, ow_in, cleared, summed, totalled, means_ok, down_ok, half_ok, scales_ok, above_ok, minus_ok, ow_hi_ok,
     ow_lo_ok) = sems(st, "T_w_in T_ow_in T_cleared T_summed T_totalled T_means T_down_mean T_half T_scales "
                          "T_above T_minus T_ow_hi T_ow_lo")
    HALVES = (slice(0, DI), slice(DI, P))
    REMS = (slice(0, REM), slice(DI, DI + REM))
    SCALE_OF = (0, 1, 2, 2)

    with nc.Block() as block:
        @block.sync
        def _(sp):
            sp.wait_ge(cleared, 3)
            for rows in HALVES:
                sp.dma_start(raw[0][rows, :, :], a["gateT"]).then_inc(w_in, 16)
                sp.dma_start(raw[1][rows, :, :], a["upT"]).then_inc(w_in, 16)
            sp.dma_start(raw[2][:, :, :], a["downT"][0:MAIN]).then_inc(w_in, 16)
            for rows in REMS:
                sp.dma_start(raw[3][rows, :, :], a["downT"][MAIN:DH]).then_inc(w_in, 16)
            sp.dma_start(ow_raw[:, :, :], a["ow"].rearrange("(c p) n -> p c n", p=P)).then_inc(ow_in, 16)
            sp.dma_start(ob[:, :], a["ob"].rearrange("(a n) -> a n", a=1).to_broadcast([P, D])).then_inc(ow_in, 16)
            sp.wait_ge(ow_in, 32)

        @block.gpsimd
        def _(pool):
            pool.memset(raw[3][:, :, :], 0.0).then_inc(cleared, 1)
            pool.memset(sums[:, :], 0.0).then_inc(cleared, 1)
            pool.memset(ones[:, :], 1.0).then_inc(cleared, 1)
            pool.wait_ge(ow_hi_ok, 1)
            pool.tensor_tensor(ow_lo[:, :, :], ow_raw[:, :, :], ow_hi[:, :, :].bitcast(F32), ALU.subtract
                               ).then_inc(ow_lo_ok, 1)

        @block.tensor
        def _(pe):
            pe.wait_ge(summed, 4)
            pe.matmul(bank[0][:, 0:4], ones[:, :], sums[:, :], start=True, stop=True).then_inc(totalled, 1)

        def signed_copy(engine, dst, src, sign):
            if engine == "act":
                return nc.scalar.activation(dst, src, ACT.Copy, scale=-float(sign))
            return nc.vector.tensor_scalar(dst, src, -float(sign), None, ALU.mult)

        def octonion_in(eng, name, m, minus):
            for c in range(KC):
                for n, rows in enumerate(HALVES):
                    for k in range(O8):
                        j, sign = OCT[2 * c + n, k]
                        signed_copy(name, m[rows, c, k, :], minus[rows, j, :], sign)

        @block.scalar
        def _(act):
            act.wait_ge(ow_in, 32)
            act.activation(ow_hi[:, :, :], ow_raw[:, :, :], ACT.Copy).then_inc(ow_hi_ok, 1)
            act.wait_ge(minus_ok, 1)
            octonion_in(act, "act", m_up, above[1])

        @block.vector
        def _(dve):
            dve.wait_ge(cleared, 3)
            dve.wait_ge(w_in, 7 * 16)
            for n, rows in enumerate((P, P, P, DI)):
                dve.tensor_reduce(sums[0:rows, n:n + 1], raw[n][0:rows, :, :], mybir.AxisListType.XY, ALU.add,
                                  apply_absolute_value=True).then_inc(summed, 1)
            dve.wait_ge(totalled, 1)
            dve.tensor_scalar(means[:, 0:2], bank[0][:, 0:2], 0.5 / N_W, None, ALU.mult).then_inc(means_ok, 1)
            dve.tensor_scalar(means[:, 2:4], bank[0][:, 2:4], 1.0 / N_W, None, ALU.mult).then_inc(means_ok, 1)
            dve.wait_ge(means_ok, 2)
            dve.tensor_tensor(means[:, 2:3], means[:, 2:3], means[:, 3:4], ALU.add).then_inc(down_ok, 1)
            dve.wait_ge(down_ok, 1)
            dve.tensor_scalar(half[:, 0, :], means[:, 0:3], 0.5, None, ALU.mult).then_inc(half_ok, 1)
            dve.tensor_scalar(half[:, 1, :], means[:, 0:3], -0.5, None, ALU.mult).then_inc(half_ok, 1)
            dve.tensor_copy(scales[:, 0:2], means[:, 0:2]).then_inc(scales_ok, 1)
            dve.tensor_tensor(scales[:, 2:3], means[:, 1:2], means[:, 2:3], ALU.mult).then_inc(scales_ok, 1)
            dve.wait_ge(half_ok, 2)
            for n in (1, 0, 2, 3):
                s = SCALE_OF[n]
                dve.tensor_scalar(above[n][:, :, :], raw[n][:, :, :], half[:, 0, s:s + 1], None, ALU.is_gt
                                  ).then_inc(above_ok, 1)
            for n in (1, 0, 2, 3):
                s = SCALE_OF[n]
                dve.wait_ge(above_ok, 4)
                dve.scalar_tensor_tensor(out=above[n][:, :, :], in0=raw[n][:, :, :], scalar=half[:, 1, s:s + 1],
                                         in1=above[n][:, :, :], op0=ALU.is_lt, op1=ALU.subtract
                                         ).then_inc(minus_ok, 1)
            dve.wait_ge(minus_ok, 4)
            octonion_in(dve, "dve", m_gate, above[0])
            for i in range(O8):
                for k in range(O8):
                    j, sign = OCT[i, k]
                    signed_copy("dve", m_down[:, i, k * DI:(k + 1) * DI], above[2][:, j, :], sign)
                    rows = HALVES[i % 2]
                    signed_copy("dve", m_down[rows, O8 + i // 2, k * DI:(k + 1) * DI], above[3][rows, j, :], sign)


def attention1(nc, st, sb, sems, bank, a, ident, xT_hi, xT_lo, y1):
    SUB = NLAT // (2 * LAT)
    lat_hi = sb(st, "lat_hi", [P, B, 2 * LC, S], F32R)
    lat_lo = sb(st, "lat_lo", [P, B, 2 * LC, S], F32R)
    identr = sb(st, "identr", [P, P], F32R)
    mask = sb(st, "mask", [P, P], F32R)
    with ExitStack() as tmp:
        compress(nc, tmp, sb, sems, bank, a, ident, identr, mask, xT_hi, xT_lo, y1, lat_hi, lat_lo, SUB)

    HQ = REP
    W = HQ * D1
    STEPS = B * HQ
    wq_raw = sb(st, "wq_raw", [P, KC, W])
    wq_hi = sb(st, "wq_hi", [P, KC, W], F32R)
    wq_lo = sb(st, "wq_lo", [P, KC, W], F32R)
    wo_raw = sb(st, "wo_raw", [P, HQ, D])
    wo_hi = sb(st, "wo_hi", [P, HQ, D], F32R)
    wo_lo = sb(st, "wo_lo", [P, HQ, D], F32R)
    wu_raw = sb(st, "wu_raw", [P, 2, LC, D1])
    wu_hi = sb(st, "wu_hi", [P, 2, LC, D1], F32R)
    wu_lo = sb(st, "wu_lo", [P, 2, LC, D1], F32R)
    kT_hi = sb(st, "kT_hi", [P, B, S], F32R)
    kT_lo = sb(st, "kT_lo", [P, B, S], F32R)
    v_hi = sb(st, "v_hi", [P, B, S], F32R)
    v_lo = sb(st, "v_lo", [P, B, S], F32R)
    qT_hi = sb(st, "qT_hi", [P, S], F32R)
    qT_lo = sb(st, "qT_lo", [P, S], F32R)
    probs = sb(st, "probs_b", [P, 10 * P])
    pT_hi = sb(st, "pT_hi", [P, 10 * P], F32R)
    pT_lo = sb(st, "pT_lo", [P, 10 * P], F32R)
    cT_hi = sb(st, "c1T_hi", [P, B, HQ, S], F32R)
    cT_lo = sb(st, "c1T_lo", [P, B, HQ, S], F32R)
    negmax = sb(st, "negmax_b", [P, QT])
    den = sb(st, "den_b", [P, QT])
    rden = sb(st, "rden_b", [P, QT])
    (wq_in, wo_in, wu_in, wq_hi_ok, wq_lo_ok, wo_hi_ok, wo_lo_ok, wu_hi_ok, wu_lo_ok, kv_done, kv_hi_ok, kv_lo_ok,
     projected, q_hi_ok, q_lo_ok, scored, maxed, exped, inverted, normed, turned, pT_hi_ok, pT_lo_ok, weighted,
     c_hi_ok, c_lo_ok, o_done, o_added) = sems(
        st, "D_wq_in D_wo_in D_wu_in D_wq_hi D_wq_lo D_wo_hi D_wo_lo D_wu_hi D_wu_lo D_kv_done D_kv_hi D_kv_lo "
            "D_projected D_q_hi D_q_lo D_scored D_maxed D_exped D_inverted D_normed D_turned D_pT_hi D_pT_lo "
            "D_weighted D_c_hi D_c_lo D_o_done D_o_added")
    SCALE = D1 ** -0.5
    SCORES = ((0, ((3, 0),)), (1, ((2, 0), (0, 3 * P))), (2, ((1, 0),)))
    ORDER = [(b, q, at) for b, tiles in SCORES for q, at in tiles]
    BANK_MAXED = {3: 1, 2: 3, 0: 3, 1: 4}
    PROB_AT = [0, P, 3 * P, 6 * P]
    TURNS = ((3, ((0, 0),)), (4, ((1, 0), (3, 3 * P))), (5, ((2, 0),)))
    T_AT = {0: 0, 1: 4 * P, 3: 7 * P, 2: 8 * P}
    T_BANK = ((3, 0, 4 * P), (4, 4 * P, 4 * P), (5, 8 * P, 2 * P))
    PIECES = 3

    def kv_piece(s):
        if 1 <= s <= 3:
            return 1, False, s - 1
        if 5 <= s <= 7:
            return 0, True, s - 5
        return None

    def steps(eng, step):
        for s in range(STEPS):
            step(0, s, True, False)
        with eng.Fori(1, HK - 1) as g:
            for s in range(STEPS):
                step(g, s, False, False)
        for s in range(STEPS):
            step(HK - 1, s, False, True)

    def pieces_before(g, s, last):
        return 2 * PIECES * g + PIECES + max(0, min(s, 4) - 1) + (0 if last else max(0, s - 5))

    with nc.Block() as block:
        @block.sync
        def _(sp):
            wq_v = a["WqT"].rearrange("(c p) n -> p c n", p=P)
            wo_v = a["WoT"].rearrange("(h d) n -> d h n", d=D1)
            wk_v = a["WkupT"].rearrange("(c p) n -> p c n", p=P)
            wv_v = a["WvupT"].rearrange("(c p) n -> p c n", p=P)

            def part(v, axis, g, n):
                at = slice(g * n, (g + 1) * n) if isinstance(g, int) else bass.ds(g * n, n)
                return v[:, :, at] if axis == 2 else v[:, at, :]

            def load(g):
                if not (isinstance(g, int) and g == 0):
                    sp.wait_ge(wu_lo_ok, g)
                    settle(sp)
                sp.dma_start(wu_raw[:, 0, :, :], part(wk_v, 2, g, D1)).then_inc(wu_in, 16)
                sp.dma_start(wu_raw[:, 1, :, :], part(wv_v, 2, g, D1)).then_inc(wu_in, 16)
                if not (isinstance(g, int) and g == 0):
                    sp.wait_ge(wq_lo_ok, g * HQ)
                    settle(sp)
                sp.dma_start(wq_raw[:, :, :], part(wq_v, 2, g, W)).then_inc(wq_in, 16)
                if not (isinstance(g, int) and g == 0):
                    sp.wait_ge(wo_lo_ok, g)
                    settle(sp)
                sp.dma_start(wo_raw[:, :, :], part(wo_v, 1, g, HQ)).then_inc(wo_in, 16)

            load(0)
            with sp.Fori(1, HK) as g:
                load(g)
            sp.wait_ge(wo_in, 16 * HK)

        def split_points(g, s, last):
            out = []
            if s == 4 and not last:
                out.append(("wu", g + 1, 0))
            if s >= 4 and not last:
                out.append(("wq", g + 1, s - 4))
            if s == 4:
                out.append(("wo", g, 0))
            return out

        def views(kind, h):
            if kind == "wu":
                return wu_raw[:, :, :, :], wu_hi[:, :, :, :], wu_lo[:, :, :, :]
            if kind == "wo":
                return wo_raw[:, :, :], wo_hi[:, :, :], wo_lo[:, :, :]
            c = slice(h * D1, (h + 1) * D1)
            return wq_raw[:, :, c], wq_hi[:, :, c], wq_lo[:, :, c]

        @block.gpsimd
        def _(pool):
            def low(kind, g, h):
                raw, hi, lo = views(kind, h)
                done, sem = {"wu": (wu_hi_ok, wu_lo_ok), "wq": (wq_hi_ok, wq_lo_ok), "wo": (wo_hi_ok, wo_lo_ok)}[kind]
                pool.wait_ge(done, (g * HQ + h if kind == "wq" else g) + 1)
                pool.tensor_tensor(lo, raw, hi.bitcast(F32), ALU.subtract).then_inc(sem, 1)

            low("wu", 0, 0)
            for h in range(HQ):
                low("wq", 0, h)
            steps(pool, lambda g, s, first, last: [low(*x) for x in split_points(g, s, last)])

        @block.tensor
        def _(pe):
            def scores(g, s, first):
                b = s // HQ
                n = g * STEPS + s
                pe.wait_ge(q_lo_ok, n + 1)
                pe.wait_ge(kv_lo_ok, 2 * PIECES * g + (PIECES if b == 0 else 2 * PIECES))
                for bk, tiles in SCORES:
                    if not (first and s == 0):
                        pe.wait_ge(exped, QT * (n - 1) + {0: 1, 1: 3, 2: 4}[bk])
                    for q, at in tiles:
                        dst = bank[bk][:, at:at + (q + 1) * P]
                        cols = slice(q * P, (q + 1) * P)
                        keys = slice(0, (q + 1) * P)
                        pe.matmul(dst, qT_hi[:, cols], kT_hi[:, b, keys], start=True, stop=False)
                        pe.matmul(bank[bk][:, at + q * P:at + (q + 1) * P], identr[:, :], mask[:, :],
                                  start=False, stop=False, skip_group_check=True)
                        pe.matmul(dst, qT_hi[:, cols], kT_lo[:, b, keys], start=False, stop=False)
                        mm = pe.matmul(dst, qT_lo[:, cols], kT_hi[:, b, keys], start=False, stop=True)
                    mm.then_inc(scored, 1)

            def queries(g, s, first):
                busy = not (first and s <= 6)
                if s == STEPS:
                    g, s = g + 1, 0
                b, h = s // HQ, s % HQ
                n = g * STEPS + s
                pe.wait_ge(wq_lo_ok, g * HQ + h + 1)
                if busy:
                    pe.wait_ge(o_added, n - 6)
                three(pe, bank[6][:, :], [
                    (wq_hi[:, c, h * D1:(h + 1) * D1], wq_lo[:, c, h * D1:(h + 1) * D1],
                     xT_hi[:, c, b * S:(b + 1) * S], xT_lo[:, c, b * S:(b + 1) * S]) for c in range(KC)]
                ).then_inc(projected, 1)

            def weigh(g, s, last):
                n = g * STEPS + s
                b = (s - 1) % STEPS // HQ
                pe.wait_ge(pT_lo_ok, 3 * n)
                pe.wait_ge(kv_lo_ok, pieces_before(g, s, last))
                hh, hl, lh = (v_hi, pT_hi), (v_hi, pT_lo), (v_lo, pT_hi)
                passes = [(0, hh)] + [(t, x) for t in range(1, QT) for x in (hh, hl, lh)] + [(0, hl), (0, lh)]
                for n, (t, (v, p)) in enumerate(passes):
                    mm = pe.matmul(bank[7][:, t * P:S], v[:, b, t * D1:(t + 1) * D1],
                                   p[:, T_AT[t]:T_AT[t] + (QT - t) * P], start=(n == 0),
                                   stop=(n == len(passes) - 1), skip_group_check=True)
                mm.then_inc(weighted, 1)

            def outputs(g, s, drained=False):
                m = g * STEPS + s - 5
                blk_steps = 2 * g * HQ
                k = (s - 5) // HQ
                q = (s - 5) % HQ
                b = k % 2
                pe.wait_ge(c_lo_ok, blk_steps + (k + 1) * HQ)
                pe.wait_ge(wo_lo_ok, g + (1 if k >= 0 else 0))
                if not drained:
                    pe.wait_ge(q_lo_ok, g * STEPS + s + 2)
                else:
                    pe.wait_ge(o_added, m)
                three(pe, bank[6][:, :], [
                    (cT_hi[:, b, h, q * P:(q + 1) * P], cT_lo[:, b, h, q * P:(q + 1) * P],
                     wo_hi[:, h, :], wo_lo[:, h, :]) for h in range(HQ)]).then_inc(o_done, 1)

            def keys_values(g, b, piece, before_step):
                pe.wait_ge(wu_lo_ok, g + 1)
                if before_step is not None:
                    pe.wait_ge(c_lo_ok, before_step)
                if piece == 0:
                    mm = three(pe, bank[7][:, :], [
                        (wu_hi[:, 0, c, :], wu_lo[:, 0, c, :], lat_hi[:, b, c, :], lat_lo[:, b, c, :])
                        for c in range(LC)])
                else:
                    for i in range(2):
                        t = 2 * (piece - 1) + i
                        mm = three(pe, bank[7][:, i * D1:(i + 1) * D1], [
                            (lat_hi[:, b, LC + c, t * P:(t + 1) * P], lat_lo[:, b, LC + c, t * P:(t + 1) * P],
                             wu_hi[:, 1, c, :], wu_lo[:, 1, c, :]) for c in range(LC)])
                mm.then_inc(kv_done, 1)

            def turn(g, s, first):
                n = g * STEPS + s
                pe.wait_ge(normed, QT * (n + 1))
                if not (first and s == 0):
                    pe.wait_ge(pT_lo_ok, 3 * n)
                for bk, tiles in TURNS:
                    for t, at in tiles:
                        for q in range(t, QT):
                            col = at + (q - t) * P
                            mm = pe.transpose(bank[bk][:, col:col + P],
                                              probs[:, PROB_AT[q] + t * P:PROB_AT[q] + (t + 1) * P], ident[:, :])
                    mm.then_inc(turned, 1)

            def step(g, s, first, last):
                scores(g, s, first)
                if not (last and s == STEPS - 1):
                    queries(g, s + 1, first)
                if not (first and s == 0):
                    weigh(g, s, last)
                if not (first and s < 5):
                    outputs(g, s, drained=last and s == STEPS - 1)
                p = kv_piece(s)
                if p and not (last and p[1]):
                    keys_values(g + 1 if p[1] else g, p[0], p[2], g * STEPS + s)
                turn(g, s, first)

            for piece in range(PIECES):
                if piece:
                    pe.wait_ge(kv_lo_ok, piece)
                keys_values(0, 0, piece, None)
            queries(0, 0, True)
            steps(pe, step)
            weigh(HK - 1, STEPS, True)
            for x in range(5):
                outputs(HK - 1, STEPS + x, drained=True)

        @block.scalar
        def _(act):
            nc.scalar.preload_act_table(ACT.Exp)

            def high(kind, g, h, start=False):
                raw, hi, _ = views(kind, h)
                if kind == "wu":
                    act.wait_ge(wu_in, 32 * (g + 1))
                    if not start:
                        act.wait_ge(kv_done, 2 * PIECES * g)
                    sem = wu_hi_ok
                elif kind == "wq":
                    act.wait_ge(wq_in, 16 * (g + 1))
                    if not start:
                        act.wait_ge(projected, g * STEPS - HQ + h + 1)
                    sem = wq_hi_ok
                else:
                    act.wait_ge(wo_in, 16 * (g + 1))
                    if not (isinstance(g, int) and g == 0):
                        act.wait_ge(o_done, g * STEPS)
                    sem = wo_hi_ok
                act.activation(hi, raw, ACT.Copy).then_inc(sem, 1)

            def kv_high(count, b, piece):
                act.wait_ge(kv_done, count)
                if piece == 0:
                    act.activation(kT_hi[:, b, :], bank[7][:, :], ACT.Copy).then_inc(kv_hi_ok, 1)
                else:
                    cols = slice((piece - 1) * 2 * D1, piece * 2 * D1)
                    act.activation(v_hi[:, b, cols], bank[7][:, 0:2 * D1], ACT.Copy).then_inc(kv_hi_ok, 1)

            def q_high(n):
                act.wait_ge(projected, n + 1)
                act.activation(qT_hi[:, :], bank[6][:, :], ACT.Copy, scale=SCALE).then_inc(q_hi_ok, 1)

            def c_high(g, s):
                n = g * STEPS + s
                k = (s - 1) // HQ
                b, h = k % 2, (s - 1) % HQ
                act.wait_ge(weighted, n)
                if not (isinstance(g, int) and 2 * g + k < 2):
                    act.wait_ge(o_done, (2 * g + k - 1) * HQ)
                act.activation(cT_hi[:, b, h, :], bank[7][:, :], ACT.Copy).then_inc(c_hi_ok, 1)

            def step(g, s, first, last):
                n = g * STEPS + s
                for x, (bk, q, at) in enumerate(ORDER):
                    act.wait_ge(maxed, QT * n + BANK_MAXED[q])
                    if x == 0 and not (first and s == 0):
                        act.wait_ge(inverted, n)
                        act.wait_ge(turned, 3 * n)
                    act.activation(probs[:, PROB_AT[q]:PROB_AT[q] + (q + 1) * P], bank[bk][:, at:at + (q + 1) * P],
                                   ACT.Exp, bias=negmax[:, q:q + 1], accum_out=den[:, q:q + 1]).then_inc(exped, 1)
                if not (last and s == STEPS - 1):
                    q_high(n + 1)
                if not (first and s == 0):
                    c_high(g, s)
                p = kv_piece(s)
                if p and not (last and p[1]):
                    kv_high(pieces_before(g, s, last) + 1, p[0], p[2])
                for kind, gg, h in split_points(g, s, last):
                    high(kind, gg, h)
                for x, (bk, at, width) in enumerate(T_BANK):
                    act.wait_ge(turned, 3 * n + x + 1)
                    if x == 0 and not (first and s == 0):
                        act.wait_ge(weighted, n)
                    act.activation(pT_hi[:, at:at + width], bank[bk][:, 0:width], ACT.Copy).then_inc(pT_hi_ok, 1)

            high("wu", 0, 0, True)
            for h in range(HQ):
                high("wq", 0, h, True)
            for piece in range(PIECES):
                kv_high(piece + 1, 0, piece)
            q_high(0)
            steps(act, step)
            c_high(HK - 1, STEPS)

        @block.vector
        def _(dve):
            def kv_low(count, b, piece):
                dve.wait_ge(kv_hi_ok, count)
                if piece == 0:
                    dve.tensor_tensor(kT_lo[:, b, :], bank[7][:, :], kT_hi[:, b, :].bitcast(F32), ALU.subtract
                                      ).then_inc(kv_lo_ok, 1)
                else:
                    cols = slice((piece - 1) * 2 * D1, piece * 2 * D1)
                    dve.tensor_tensor(v_lo[:, b, cols], bank[7][:, 0:2 * D1], v_hi[:, b, cols].bitcast(F32),
                                      ALU.subtract).then_inc(kv_lo_ok, 1)

            def q_low(n):
                dve.wait_ge(q_hi_ok, n + 1)
                dve.scalar_tensor_tensor(out=qT_lo[:, :], in0=bank[6][:, :], scalar=SCALE,
                                         in1=qT_hi[:, :].bitcast(F32), op0=ALU.mult, op1=ALU.subtract
                                         ).then_inc(q_lo_ok, 1)

            def c_low(g, s):
                k = (s - 1) // HQ
                b, h = k % 2, (s - 1) % HQ
                dve.wait_ge(c_hi_ok, g * STEPS + s)
                dve.tensor_tensor(cT_lo[:, b, h, :], bank[7][:, :], cT_hi[:, b, h, :].bitcast(F32), ALU.subtract
                                  ).then_inc(c_lo_ok, 1)

            def add_output(g, s):
                k, q = (s - 5) // HQ, (s - 5) % HQ
                tile = k % 2 * QT + q
                dve.wait_ge(o_done, g * STEPS + s - 4)
                dve.tensor_tensor(y1[:, tile, :], bank[6][:, :], y1[:, tile, :], ALU.add).then_inc(o_added, 1)

            def step(g, s, first, last):
                n = g * STEPS + s
                for x, (bk, q, at) in enumerate(ORDER):
                    dve.wait_ge(scored, 3 * n + bk + 1)
                    dve.tensor_reduce(negmax[:, q:q + 1], bank[bk][:, at:at + (q + 1) * P], AX_X, ALU.max,
                                      negate=True).then_inc(maxed, 1)
                if not (last and s == STEPS - 1):
                    q_low(n + 1)
                dve.wait_ge(exped, QT * (n + 1))
                if not (first and s == 0):
                    dve.wait_ge(normed, QT * n)
                dve.reciprocal(rden[:, :], den[:, :]).then_inc(inverted, 1)
                dve.wait_ge(inverted, n + 1)
                for q in (0, 1, 2, 3):
                    tile = probs[:, PROB_AT[q]:PROB_AT[q] + (q + 1) * P]
                    dve.tensor_scalar(tile, tile, rden[:, q:q + 1], None, ALU.mult).then_inc(normed, 1)
                if not (first and s == 0):
                    c_low(g, s)
                if not (first and s < 5):
                    add_output(g, s)
                p = kv_piece(s)
                if p and not (last and p[1]):
                    kv_low(pieces_before(g, s, last) + 1, p[0], p[2])
                for x, (bk, at, width) in enumerate(T_BANK):
                    dve.wait_ge(pT_hi_ok, 3 * n + x + 1)
                    dve.tensor_tensor(pT_lo[:, at:at + width], bank[bk][:, 0:width],
                                      pT_hi[:, at:at + width].bitcast(F32), ALU.subtract).then_inc(pT_lo_ok, 1)

            for piece in range(PIECES):
                kv_low(piece + 1, 0, piece)
            q_low(0)
            steps(dve, step)
            c_low(HK - 1, STEPS)
            for x in range(5):
                add_output(HK - 1, STEPS + x)


def compress(nc, st, sb, sems, bank, a, ident, identr, mask, xT_hi, xT_lo, y1, lat_hi, lat_lo, SUB):
    PAIR = 2 * LAT
    raw = sb(st, "wkv_raw", [P, KC, HK, PAIR])
    hi = sb(st, "wkv_hi", [P, KC, HK, 2, PAIR], F32R)
    lo = sb(st, "wkv_lo", [P, KC, HK, 2, PAIR], F32R)
    maskf = sb(st, "maskf", [P, P])
    (w_in, hi_ok, lo_ok, zeroed, masked, const_ok, done, out_hi, out_lo) = sems(
        st, "K_w_in K_w_hi K_w_lo K_zeroed K_masked K_const K_done K_out_hi K_out_lo")
    with nc.Block() as block:
        @block.sync
        def _(sp):
            sp.dma_start(raw[:, :, :, :], a["WkvT"].rearrange("(c p) (h n) -> p c h n", p=P, h=HK)).then_inc(w_in, 16)

        @block.gpsimd
        def _(pool):
            pool.memset(maskf[:, :], 0.0).then_inc(zeroed, 1)
            pool.memset(y1[:, :, :], 0.0).then_inc(zeroed, 1)
            pool.wait_ge(zeroed, 2)
            pool.affine_select(out=maskf[:, :], in_=maskf[:, :], compare_op=ALU.is_ge, fill=MASKED, base=0,
                               pattern=[[-1, P]], channel_multiplier=1).then_inc(masked, 1)

        def kept(buf, b, hk, rows):
            cols = slice(hk * (S // 8), (hk + 1) * (S // 8))
            return buf[rows, bass.ds(b, 1), :, cols].rearrange("p one c t -> p (one c) t")

        def tokens(bk, i, rows):
            return bk[rows, :].rearrange("p (t c two) -> p two c t", two=2, c=2 * LC)[:, i, :, :]

        @block.scalar
        def _(act):
            nc.scalar.preload_act_table(ACT.Exp)
            act.wait_ge(w_in, 16)
            for i in range(2):
                act.activation(hi[:, :, :, i, :], raw[:, :, :, :], ACT.Copy).then_inc(hi_ok, 1)
            act.activation(identr[:, :], ident[:, :], ACT.Copy).then_inc(const_ok, 1)
            act.wait_ge(masked, 1)
            act.activation(mask[:, :], maskf[:, :], ACT.Copy).then_inc(const_ok, 1)

            def job(b, hk):
                act.wait_ge(done, b * HK + hk + 1)
                for i in range(2):
                    rows = slice(i * PAIR, (i + 1) * PAIR)
                    settle(act)
                    act.activation(kept(lat_hi, b, hk, rows), tokens(bank[hk], i, rows), ACT.Copy).then_inc(out_hi, 1)
            with act.Fori(0, B) as b:
                for hk in range(HK):
                    job(b, hk)

        @block.vector
        def _(dve):
            dve.wait_ge(hi_ok, 2)
            for i in range(2):
                dve.tensor_tensor(lo[:, :, :, i, :], raw[:, :, :, :], hi[:, :, :, i, :].bitcast(F32), ALU.subtract
                                  ).then_inc(lo_ok, 1)
            with dve.Fori(0, B) as b:
                for hk in range(HK):
                    dve.wait_ge(out_hi, 2 * (b * HK + hk) + 2)
                    for i in range(2):
                        rows = slice(i * PAIR, (i + 1) * PAIR)
                        dve.tensor_tensor(kept(lat_lo, b, hk, rows), tokens(bank[hk], i, rows),
                                          kept(lat_hi, b, hk, rows).bitcast(F32), ALU.subtract).then_inc(out_lo, 1)

        @block.tensor
        def _(pe):
            pe.wait_ge(lo_ok, 2)

            def job(b, hk):
                if not (isinstance(b, int) and b == 0):
                    pe.wait_ge(out_lo, 2 * (b * HK + hk - HK) + 2)
                three(pe, bank[hk][:, :], [
                    (hi[:, c, hk, :, :].rearrange("p a n -> p (a n)"), lo[:, c, hk, :, :].rearrange("p a n -> p (a n)"),
                     xT_hi[:, c, b * S:(b + 1) * S], xT_lo[:, c, b * S:(b + 1) * S]) for c in range(KC)]
                ).then_inc(done, 1)
            for b in range(B):
                for hk in range(HK):
                    job(b, hk)


def cores_ffn(nc, st, sb, sems, bank, a, ident, neghalf, y1, x_mid, out):
    NS = R + E
    wb_raw = sb(st, "wb_raw", [P, KC, D])
    wb_hi = sb(st, "wb_hi", [P, KC, D], F32R)
    wb_lo = sb(st, "wb_lo", [P, KC, D], F32R)
    ar_raw = sb(st, "ar_raw", [P, KC, NS])
    ar_hi = sb(st, "ar_hi", [P, KC, NS], F32R)
    ar_lo = sb(st, "ar_lo", [P, KC, NS], F32R)
    cores = sb(st, "cores_T", [R, P])
    b_w = sb(st, "b_w", [R, D])
    cb = sb(st, "cores_b", [P, D])
    bb = sb(st, "b_base", [P, D])
    x = sb(st, "x_last", [P, NT, D])
    xn = sb(st, "xn_last", [P, D])
    tT_hi = sb(st, "eT_hi", [P, KC, P], F32R)
    tT_lo = sb(st, "eT_lo", [P, KC, P], F32R)
    y = sb(st, "y_last", [P, D])
    negmax = sb(st, "negmaxE", [P, 1])
    ex = sb(st, "expE", [P, E])
    den = sb(st, "denE", [P, 1])
    rden = sb(st, "rdenE", [P, 1])
    route = sb(st, "route", [P, E])
    z = sb(st, "z", [P, E, R])
    zT = sb(st, "zT", [P, P])
    stats0 = sb(st, "stats_y1", [P, NT, 6])
    mv0 = sb(st, "mv_y1", [P, NT, 2])
    veps0 = sb(st, "veps_y1", [P, NT])
    rstd0 = sb(st, "rstd_y1", [P, NT])
    half0 = sb(st, "neghalf_y1", [P, NT])
    stats = sb(st, "statsE", [P, 2, 6])
    mv = sb(st, "mvE", [P, 2, 2])
    veps = sb(st, "vepsE", [P, 2, 1])
    rstd = sb(st, "rstdE", [P, 2, 1])
    (x_in, w_in, small_in, wb_hi_ok, wb_lo_ok, ar_hi_ok, ar_lo_ok, cb_done, cb_ok, stat0, aggr0, eps0, half_ok,
     rstd0_ok, applied0, x3_ok, turned, tT_hi_ok, tT_lo_ok, small_done, maxed, exped, inverted, routed, z_ok, z_turned,
     zT_ok, out_done, y_ok, x4_ok, stored) = sems(
        st, "E_x_in E_w_in E_small_in E_wb_hi E_wb_lo E_ar_hi E_ar_lo E_cb_done E_cb E_stat0 E_aggr0 E_eps0 E_half "
            "E_rstd0 E_applied0 E_x3 E_turned E_tT_hi E_tT_lo E_small_done E_maxed E_exped E_inverted E_routed E_z "
            "E_z_turned E_zT E_out_done E_y E_x4 E_stored")
    stat, aggr, eps_ok, rstd_ok, applied = (sems(st, " ".join(f"E_{n}{k}" for k in (1, 2)))
                                            for n in ("stat", "aggr", "eps", "rstd", "applied"))
    out_v = out.rearrange("(t p) h -> p t h", p=P)

    def tile_of(buf, t):
        return buf[:, t, :] if isinstance(t, int) else buf[:, bass.ds(t, 1), :]

    def quads(b):
        return b[:, :].rearrange("p (c q) -> p c q", c=KC)

    def steps(eng, step):
        step(0, True, False)
        with eng.Fori(1, NT - 1) as t:
            step(t, False, False)
        step(NT - 1, False, True)

    with nc.Block() as block:
        @block.sync
        def _(sp):
            sp.dma_start(x[:, :, :], x_mid.rearrange("(t p) h -> p t h", p=P)).then_inc(x_in, 16)
            sp.dma_start(wb_raw[:, :, :], a["WbT"].rearrange("(c p) n -> p c n", p=P)).then_inc(w_in, 16)
            sp.dma_start(ar_raw[:, :, :], a["ArT"].rearrange("(c p) n -> p c n", p=P)).then_inc(small_in, 16)
            sp.dma_start(cores[:, :], a["coresT"]).then_inc(small_in, 16)
            sp.dma_start(b_w[:, :], a["BwT"]).then_inc(small_in, 16)
            sp.dma_start(bb[:, :], a["bb"].rearrange("(a n) -> a n", a=1).to_broadcast([P, D])).then_inc(small_in, 16)

            def store(t, first, last):
                sp.wait_ge(x4_ok, t + 1)
                sp.dma_start(tile_of(out_v, t), tile_of(x, t)).then_inc(stored, 16)
            steps(sp, store)
            sp.wait_ge(stored, 16 * NT)

        @block.gpsimd
        def _(pool):
            def power(n, t):
                pool.wait_ge(eps_ok[n], t + 1)
                settle(pool)
                pool.tensor_tensor(rstd[:, n, :], veps[:, n, :], neghalf[:, :], ALU.pow).then_inc(rstd_ok[n], 1)

            pool.memset(half0[:, :], -0.5).then_inc(half_ok, 1)
            pool.wait_ge(half_ok, 1)
            pool.wait_ge(eps0, 1)
            pool.tensor_tensor(rstd0[:, :], veps0[:, :], half0[:, :], ALU.pow).then_inc(rstd0_ok, 1)
            pool.wait_ge(wb_hi_ok, 1)
            pool.tensor_tensor(wb_lo[:, :, :], wb_raw[:, :, :], wb_hi[:, :, :].bitcast(F32), ALU.subtract
                               ).then_inc(wb_lo_ok, 1)
            power(0, 0)

            def step(t, first, last):
                if not last:
                    power(0, t + 1)
                power(1, t)
            steps(pool, step)

        @block.tensor
        def _(pe):
            def turn_x(t, first=False):
                pe.wait_ge(applied[0], t + 1)
                if not first:
                    pe.wait_ge(tT_lo_ok, t)
                for c in range(KC):
                    mm = pe.transpose(bank[1][:, c * P:(c + 1) * P], xn[:, c * P:(c + 1) * P], ident[:, :])
                mm.then_inc(turned, 1)

            pe.wait_ge(small_in, 64)
            pe.matmul(bank[4][:, :], cores[:, :], b_w[:, :], start=True, stop=True).then_inc(cb_done, 1)
            turn_x(0, True)
            pe.wait_ge(ar_lo_ok, 1)
            pe.wait_ge(wb_lo_ok, 1)
            pe.wait_ge(cb_ok, 1)

            def step(t, first, last):
                pe.wait_ge(tT_lo_ok, t + 1)
                if not first:
                    pe.wait_ge(z_ok, t)
                three(pe, bank[2][:, 0:NS], [(tT_hi[:, c, :], tT_lo[:, c, :], ar_hi[:, c, :], ar_lo[:, c, :])
                                             for c in range(KC)]).then_inc(small_done, 1)
                if not first:
                    pe.wait_ge(y_ok, t)
                three(pe, bank[0][:, :], [(tT_hi[:, c, :], tT_lo[:, c, :], wb_hi[:, c, :], wb_lo[:, c, :])
                                          for c in range(KC)], stop=False)
                pe.wait_ge(z_ok, t + 1)
                if not first:
                    pe.wait_ge(zT_ok, t)
                pe.transpose(bank[3][:, 0:P], z[:, :, :].rearrange("p e r -> p (e r)"), ident[:, :]
                             ).then_inc(z_turned, 1)
                if not last:
                    turn_x(t + 1)
                pe.wait_ge(zT_ok, t + 1)
                pe.matmul(bank[0][:, :], zT[:, :], cb[:, :], start=False, stop=True).then_inc(out_done, 1)
            steps(pe, step)

        @block.scalar
        def _(act):
            nc.scalar.preload_act_table(ACT.Exp)
            act.wait_ge(small_in, 64)
            act.activation(ar_hi[:, :, :], ar_raw[:, :, :], ACT.Copy).then_inc(ar_hi_ok, 1)
            act.wait_ge(w_in, 16)
            act.activation(wb_hi[:, :, :], wb_raw[:, :, :], ACT.Copy).then_inc(wb_hi_ok, 1)
            act.wait_ge(cb_done, 1)
            act.activation(cb[:, :], bank[4][:, :], ACT.Copy, scale=LORA_SCALE).then_inc(cb_ok, 1)

            def high(t):
                act.wait_ge(turned, t + 1)
                act.activation(tT_hi[:, :, :], quads(bank[1]), ACT.Copy).then_inc(tT_hi_ok, 1)

            high(0)

            def step(t, first, last):
                act.wait_ge(maxed, t + 1)
                if not first:
                    act.wait_ge(routed, t)
                act.activation(ex[:, :], bank[2][:, R:NS], ACT.Exp, bias=negmax[:, :], accum_out=den[:, :]
                               ).then_inc(exped, 1)
                act.wait_ge(z_turned, t + 1)
                if not first:
                    act.wait_ge(out_done, t)
                act.activation(zT[:, :], bank[3][:, 0:P], ACT.Copy).then_inc(zT_ok, 1)
                if not last:
                    high(t + 1)
            steps(act, step)

        @block.vector
        def _(dve):
            def statistics(n, t, src, ready, first):
                dve.wait_ge(ready, t + 1)
                if not first:
                    dve.wait_ge(aggr[n], t)
                settle(dve)
                dve.bn_stats(stats[:, n, :], src).then_inc(stat[n], 1)
                dve.wait_ge(stat[n], t + 1)
                if not first:
                    dve.wait_ge(applied[n], t)
                settle(dve)
                dve.bn_aggr(mv[:, n, :], stats[:, n, :]).then_inc(aggr[n], 1)
                dve.wait_ge(aggr[n], t + 1)
                if not first:
                    dve.wait_ge(rstd_ok[n], t)
                dve.tensor_scalar(veps[:, n, :], mv[:, n, 1:2], EPS, None, ALU.add).then_inc(eps_ok[n], 1)

            def front(t, first):
                if isinstance(t, int):
                    r, m = rstd0[:, t:t + 1], mv0[:, t, 0:1]
                else:
                    r, m = rstd0[:, bass.ds(t, 1)], mv0[:, bass.ds(t, 1), 0:1]
                dve.tensor_scalar(tile_of(y1, t), tile_of(y1, t), m, r, ALU.subtract, ALU.mult
                                  ).then_inc(applied0, 1)
                dve.wait_ge(applied0, t + 1)
                dve.tensor_tensor(tile_of(x, t), tile_of(x, t), tile_of(y1, t), ALU.add).then_inc(x3_ok, 1)
                statistics(0, t, tile_of(x, t), x3_ok, first)

            def input_norm(t, first):
                dve.wait_ge(rstd_ok[0], t + 1)
                if not first:
                    dve.wait_ge(turned, t)
                dve.tensor_scalar(xn[:, :], tile_of(x, t), mv[:, 0, 0:1], rstd[:, 0, :], ALU.subtract, ALU.mult
                                  ).then_inc(applied[0], 1)

            def low(t):
                dve.wait_ge(tT_hi_ok, t + 1)
                dve.tensor_tensor(tT_lo[:, :, :], quads(bank[1]), tT_hi[:, :, :].bitcast(F32), ALU.subtract
                                  ).then_inc(tT_lo_ok, 1)

            def last_residual(t):
                dve.wait_ge(rstd_ok[1], t + 1)
                dve.tensor_scalar(y[:, :], y[:, :], mv[:, 1, 0:1], rstd[:, 1, :], ALU.subtract, ALU.mult
                                  ).then_inc(applied[1], 1)
                dve.wait_ge(applied[1], t + 1)
                dve.tensor_tensor(tile_of(x, t), tile_of(x, t), y[:, :], ALU.add).then_inc(x4_ok, 1)

            for t in range(NT):
                dve.bn_stats(stats0[:, t, :], y1[:, t, :]).then_inc(stat0, 1)
            dve.wait_ge(stat0, NT)
            for t in range(NT):
                dve.bn_aggr(mv0[:, t, :], stats0[:, t, :]).then_inc(aggr0, 1)
            dve.wait_ge(aggr0, NT)
            dve.tensor_scalar(veps0[:, :], mv0[:, :, 1], EPS, None, ALU.add).then_inc(eps0, 1)
            dve.wait_ge(ar_hi_ok, 1)
            dve.tensor_tensor(ar_lo[:, :, :], ar_raw[:, :, :], ar_hi[:, :, :].bitcast(F32), ALU.subtract
                              ).then_inc(ar_lo_ok, 1)
            dve.wait_ge(rstd0_ok, 1)
            dve.wait_ge(x_in, 16)
            front(0, True)
            input_norm(0, True)
            low(0)

            def step(t, first, last):
                dve.wait_ge(small_done, t + 1)
                if not first:
                    dve.wait_ge(exped, t)
                dve.tensor_reduce(negmax[:, :], bank[2][:, R:NS], AX_X, ALU.max, negate=True).then_inc(maxed, 1)
                if not first:
                    last_residual(t - 1)
                if not last:
                    front(t + 1, False)
                dve.wait_ge(exped, t + 1)
                if not first:
                    dve.wait_ge(routed, t)
                dve.reciprocal(rden[:, :], den[:, :]).then_inc(inverted, 1)
                dve.wait_ge(inverted, t + 1)
                if not first:
                    dve.wait_ge(z_turned, t)
                dve.tensor_scalar(route[:, :], ex[:, :], rden[:, :], None, ALU.mult).then_inc(routed, 1)
                dve.wait_ge(routed, t + 1)
                dve.tensor_tensor(z[:, :, :], route[:, :, None].to_broadcast([P, E, R]),
                                  bank[2][:, None, 0:R].to_broadcast([P, E, R]), ALU.mult).then_inc(z_ok, 1)
                if not last:
                    input_norm(t + 1, False)
                dve.wait_ge(out_done, t + 1)
                if not first:
                    dve.wait_ge(x4_ok, t)
                dve.tensor_tensor(y[:, :], bank[0][:, :], bb[:, :], ALU.add).then_inc(y_ok, 1)
                statistics(1, t, y[:, :], y_ok, first)
                if not last:
                    low(t + 1)
            steps(dve, step)
            last_residual(NT - 1)


def kernel(**inputs):
    import numpy as _np
    import concourse.bacc as _bacc
    from concourse import mybir as _mybir
    from concourse.bass_utils import run_bass_kernel_spmd as _run

    g = {n: _np.asarray(v) for n, v in inputs.items()}
    kv = [g[f"L1_attn_W{n}_down"].reshape(HK, LAT, D) for n in "kv"]
    laid = {
        "x": g["L0_attn_x"].reshape(TOK, D),
        "qkvw": g["L0_attn_attn_qkvw"],
        "qkvb": g["L0_attn_attn_qkvb"],
        "qkvb_cols": g["L0_attn_attn_qkvb"].reshape(3 * KC, P).T,
        "ow": g["L0_attn_attn_ow"],
        "ob": g["L0_attn_attn_ob"],
        "gateT": g["L0_ffn_w_gate"].transpose(2, 0, 1),
        "upT": g["L0_ffn_w_up"].transpose(2, 0, 1),
        "downT": g["L0_ffn_w_down"].transpose(2, 0, 1),
        "WqT": g["L1_attn_Wq"].T,
        "WkvT": _np.stack(kv, axis=1).reshape(2 * NLAT, D).T,
        "WkupT": g["L1_attn_Wk_up"].T,
        "WvupT": g["L1_attn_Wv_up"].T,
        "WoT": g["L1_attn_Wo"].T,
        "WbT": g["L1_ffn_W_base"].T,
        "bb": g["L1_ffn_b_base"],
        "ArT": _np.concatenate([g["L1_ffn_A_w"], g["L1_ffn_router_w"]]).T,
        "BwT": g["L1_ffn_B_w"].T,
        "coresT": g["L1_ffn_cores"].reshape(E * R, R).T,
    }
    nc = _bacc.Bacc("TRN2", target_bir_lowering=False, num_devices=1)
    arrays, aps = {}, {}
    for name, v in laid.items():
        v = _np.ascontiguousarray(v)
        arrays[f"in_{name}"] = v
        aps[name] = nc.dram_tensor(f"in_{name}", v.shape, _mybir.dt.from_np(v.dtype), kind="ExternalInput").ap()
    out = nc.dram_tensor("out_0", (TOK, D), F32, kind="ExternalOutput").ap()
    program(nc, aps, out)
    r = _run(nc, [arrays], core_ids=[0])
    return r.results[0]["out_0"].reshape(B, S, D)
```

```python
from contextlib import ExitStack

import concourse.bass as bass
from concourse import mybir

F32 = mybir.dt.float32
F32R = mybir.dt.float32r
ACT = mybir.ActivationFunctionType
ALU = mybir.AluOpType
AX_X = mybir.AxisListType.X

P = 128
B, S, D = 2, 512, 512
TOK = B * S
NT = TOK // P
QT = S // P
KC = D // P
EPS = 1e-5

H0, HD0 = 32, 16
HPC = P // HD0

O8 = 8
DI = D // O8
DH = 1366 // O8
MAIN = P
REM = DH - MAIN
NHC = O8 + O8 // 2

H1, HK, D1 = 32, 8, 128
LAT = D1 // 4
REP = H1 // HK
NLAT = HK * LAT
LC = NLAT // P

R, E = 16, 8
LORA_SCALE = 32.0 / 16.0

TRIPLES = [(1, 2, 3), (1, 4, 5), (1, 7, 6), (2, 4, 6), (2, 5, 7), (3, 4, 7), (3, 6, 5)]
MASKED = -1.0e30


def octonion_table():
    s = {(0, 0, 0): 1}
    for i in range(1, 8):
        s[0, i, i] = 1
        s[i, 0, i] = 1
        s[i, i, 0] = -1
    for a, b, c in TRIPLES:
        for x, y, z in ((a, b, c), (b, c, a), (c, a, b)):
            s[x, y, z] = 1
            s[y, x, z] = -1
    return {(i, k): (j, v) for (j, i, k), v in s.items()}


OCT = octonion_table()


def settle(eng):
    eng.nop(nofuse=True)


def program(nc, a, out, stop="all"):
    with ExitStack() as whole:
        bank = [whole.enter_context(nc.psum_tensor(f"bank{i}", [P, 512], F32)) for i in range(8)]

        def sems(stack, names):
            got = [nc.alloc_semaphore(n) for n in names.split()]

            def clear():
                nc.clear_and_free_semaphores(got)
                nc.all_engine_barrier()
            stack.callback(clear)
            return got

        def sb(stack, name, shape, dt=F32):
            return stack.enter_context(nc.sbuf_tensor(name, shape, dt))

        ident = sb(whole, "ident", [P, P])
        neghalf = sb(whole, "neghalf", [P, 1])
        xT_hi = sb(whole, "xT_hi", [P, KC, TOK], F32R)
        xT_lo = sb(whole, "xT_lo", [P, KC, TOK], F32R)
        x_mid = nc.dram_tensor("x_mid", (TOK, D), F32, kind="Internal").ap()

        with ExitStack() as first:
            x_res = sb(first, "x_res", [P, NT, D])
            ctx0 = sb(first, "ctx0", [P, NT, D])
            with ExitStack() as st:
                qk = sb(st, "qk", [P, 4, KC, TOK], F32R)
                v0 = sb(st, "v0", [P, NT, D])
                with ExitStack() as tmp:
                    project_qkv(nc, tmp, sb, sems, bank, a, ident, neghalf, x_res, ctx0, xT_hi, xT_lo, qk, v0)
                if stop == "A":
                    dump(nc, whole, sems, out, qk[:, 0:2, :, :].bitcast(F32).rearrange("p a b c -> p (a b c)")[:, 0:4096])
                    return
                with ExitStack() as tmp:
                    attention0(nc, tmp, sb, sems, bank, ident, qk, v0, ctx0, xT_hi, xT_lo)
            if stop == "B":
                dump(nc, whole, sems, out, ctx0[:, :, :])
                return
            with ExitStack() as tmp:
                middle(nc, tmp, sb, sems, bank, a, ident, neghalf, x_res, ctx0, xT_hi, xT_lo, x_mid)
            if stop == "C":
                dump(nc, whole, sems, out, x_res[:, :, :])
                return
        y1 = sb(whole, "y1", [P, NT, D])
        with ExitStack() as tmp:
            attention1(nc, tmp, sb, sems, bank, a, ident, xT_hi, xT_lo, y1)
        if stop == "D":
            dump(nc, whole, sems, out, y1[:, :, :])
            return
        with ExitStack() as tmp:
            cores_ffn(nc, tmp, sb, sems, bank, a, ident, neghalf, y1, x_mid, out)


def dump(nc, st, sems, out, what):
    (s,) = sems(st, "dumped")
    with nc.Block() as block:
        @block.sync
        def _(sp):
            dst = out.rearrange("(t p) h -> p t h", p=P)
            src = what if len(what.shape) == 3 else what.rearrange("p (t h) -> p t h", t=NT)
            sp.dma_start(dst, src).then_inc(s, 16)
            sp.wait_ge(s, 16)


def project_qkv(nc, st, sb, sems, bank, a, ident, neghalf, x_res, ctx0, xT_hi, xT_lo, qk, v0):
    scale = HD0 ** -0.5
    w_hi = sb(st, "wqkv_hi", [P, KC, 3 * D], F32R)
    w_lo = sb(st, "wqkv_lo", [P, KC, 3 * D], F32R)
    raw = [ctx0[:, 0:KC, :], ctx0[:, KC:2 * KC, :], sb(st, "raw_v", [P, KC, D])[:, :, :]]
    bias = sb(st, "qkv_bias", [P, 3 * KC])
    bias_q = sb(st, "q_bias_scaled", [P, KC])
    v_bias = sb(st, "v_bias", [P, D])
    stats = sb(st, "statsA", [P, 6])
    mv = sb(st, "mvA", [P, 2])
    veps = sb(st, "vepsA", [P, 1])
    rstd = sb(st, "rstdA", [P, 1])
    xn = sb(st, "xnA", [P, 2, D])
    (x_in, w_in, small_in, ident_ok, zeroed, stat, aggr, eps_added, rstd_ok, normed, turned, xT_hi_ok, xT_lo_ok,
     w_hi_ok, w_lo_ok, qbias_ok, proj, out_hi, out_lo, v_out) = sems(
        st, "A_x_in A_w_in A_small_in A_ident A_zeroed A_stat A_aggr A_eps A_rstd A_normed A_turned A_xT_hi A_xT_lo "
            "A_w_hi A_w_lo A_qbias A_proj A_out_hi A_out_lo A_v_out")
    x_v = a["x"].rearrange("(t p) h -> p t h", p=P)
    w_v = a["qkvw"].rearrange("(c p) n -> p c n", p=P)
    w_sems = [w_in] + sems(st, "A_wk_in A_wv_in")
    NM = 2 * KC

    with nc.Block() as block:
        @block.sync
        def _(sp):
            sp.dma_start(x_res[:, :, :], x_v).then_inc(x_in, 16)
            for n in range(3):
                sp.dma_start(raw[n], w_v[:, :, n * D:(n + 1) * D]).then_inc(w_sems[n], 16)
            sp.dma_start(bias[:, :], a["qkvb_cols"]).then_inc(small_in, 16)
            sp.dma_start(v_bias[:, :], a["qkvb"][2 * D:3 * D].rearrange("(a n) -> a n", a=1).to_broadcast([P, D])
                         ).then_inc(small_in, 16)

        @block.gpsimd
        def _(pool):
            pool.memset(neghalf[:, :], -0.5).then_inc(zeroed, 1)
            pool.memset(ident[:, :], 0.0).then_inc(zeroed, 1)
            pool.wait_ge(zeroed, 2)
            pool.affine_select(out=ident[:, :], in_=ident[:, :], compare_op=ALU.not_equal, fill=1.0, base=0,
                               pattern=[[-1, P]], channel_multiplier=1).then_inc(ident_ok, 1)
            with pool.Fori(0, NT) as t:
                pool.wait_ge(aggr, t + 1)
                settle(pool)
                pool.tensor_scalar(veps[:, :], mv[:, 1:2], EPS, None, ALU.add).then_inc(eps_added, 1)
                pool.wait_ge(eps_added, t + 1)
                settle(pool)
                pool.tensor_tensor(rstd[:, :], veps[:, :], neghalf[:, :], ALU.pow).then_inc(rstd_ok, 1)

        @block.scalar
        def _(act):
            nc.scalar.preload_act_table(ACT.Exp)
            act.wait_ge(small_in, 32)
            act.activation(bias_q[:, :], bias[:, 0:KC], ACT.Copy, scale=scale).then_inc(qbias_ok, 1)
            for n in range(3):
                act.wait_ge(w_sems[n], 16)
                act.activation(w_hi[:, :, n * D:(n + 1) * D], raw[n], ACT.Copy,
                               scale=scale if n == 0 else 1.0).then_inc(w_hi_ok, 1)
            for t in range(NT):
                act.wait_ge(turned, t + 1)
                act.activation(xT_hi[:, :, t * P:(t + 1) * P], bank[t % 2][:, :].rearrange("p (c q) -> p c q", c=KC),
                               ACT.Copy).then_inc(xT_hi_ok, 1)
            act.wait_ge(qbias_ok, 1)
            for b in range(B):
                for m in range(NM):
                    j = b * NM + m
                    act.wait_ge(proj, j + 1)
                    dst = qk[:, 1 if m < KC else 2, m % KC, b * S:(b + 1) * S]
                    act.activation(dst, bank[2 + j % 4][:, :], ACT.Identity,
                                   bias=bias_q[:, m:m + 1] if m < KC else bias[:, m:m + 1]).then_inc(out_hi, 1)

        @block.vector
        def _(dve):
            dve.wait_ge(x_in, 16)
            for t in range(NT):
                if t:
                    dve.wait_ge(aggr, t)
                dve.bn_stats(stats[:, :], x_res[:, t, :]).then_inc(stat, 1)
                dve.wait_ge(stat, t + 1)
                if t:
                    dve.wait_ge(normed, t)
                dve.bn_aggr(mv[:, :], stats[:, :]).then_inc(aggr, 1)
                dve.wait_ge(rstd_ok, t + 1)
                if t >= 2:
                    dve.wait_ge(turned, t - 1)
                dve.tensor_scalar(xn[:, t % 2, :], x_res[:, t, :], mv[:, 0:1], rstd[:, :], ALU.subtract,
                                  ALU.mult).then_inc(normed, 1)
                if t < 3:
                    dve.wait_ge(w_hi_ok, t + 1)
                    dve.scalar_tensor_tensor(out=w_lo[:, :, t * D:(t + 1) * D], in0=raw[t],
                                             scalar=scale if t == 0 else 1.0,
                                             in1=w_hi[:, :, t * D:(t + 1) * D].bitcast(F32), op0=ALU.mult,
                                             op1=ALU.subtract).then_inc(w_lo_ok, 1)
                dve.wait_ge(xT_hi_ok, t + 1)
                dve.tensor_tensor(xT_lo[:, :, t * P:(t + 1) * P], bank[t % 2][:, :].rearrange("p (c q) -> p c q", c=KC),
                                  xT_hi[:, :, t * P:(t + 1) * P].bitcast(F32), ALU.subtract).then_inc(xT_lo_ok, 1)
            dve.wait_ge(qbias_ok, 1)
            for b in range(B):
                for m in range(NM):
                    j = b * NM + m
                    dve.wait_ge(out_hi, j + 1)
                    hi, lo = (1, 0) if m < KC else (2, 3)
                    cols = slice(b * S, (b + 1) * S)
                    dve.scalar_tensor_tensor(out=qk[:, lo, m % KC, cols], in0=bank[2 + j % 4][:, :],
                                             scalar=bias_q[:, m:m + 1] if m < KC else bias[:, m:m + 1],
                                             in1=qk[:, hi, m % KC, cols].bitcast(F32), op0=ALU.add,
                                             op1=ALU.subtract).then_inc(out_lo, 1)
            for t in range(NT):
                dve.wait_ge(proj, B * NM + t + 1)
                dve.tensor_tensor(v0[:, t, :], bank[6 + t % 2][:, :], v_bias[:, :], ALU.add).then_inc(v_out, 1)

        @block.tensor
        def _(pe):
            pe.wait_ge(ident_ok, 1)
            for t in range(NT):
                pe.wait_ge(normed, t + 1)
                if t >= 2:
                    pe.wait_ge(xT_lo_ok, t - 1)
                for c in range(KC):
                    mm = pe.transpose(bank[t % 2][:, c * P:(c + 1) * P], xn[:, t % 2, c * P:(c + 1) * P], ident[:, :])
                mm.then_inc(turned, 1)
            pe.wait_ge(w_lo_ok, 3)
            for b in range(B):
                pe.wait_ge(xT_lo_ok, (b + 1) * QT)
                for m in range(NM):
                    j = b * NM + m
                    if j >= 4:
                        pe.wait_ge(out_lo, j - 3)
                    three(pe, bank[2 + j % 4][:, :], [
                        (w_hi[:, c, m * P:(m + 1) * P], w_lo[:, c, m * P:(m + 1) * P],
                         xT_hi[:, c, b * S:(b + 1) * S], xT_lo[:, c, b * S:(b + 1) * S]) for c in range(KC)]
                    ).then_inc(proj, 1)
            for t in range(NT):
                if t >= 2:
                    pe.wait_ge(v_out, t - 1)
                three(pe, bank[6 + t % 2][:, :], [
                    (xT_hi[:, c, t * P:(t + 1) * P], xT_lo[:, c, t * P:(t + 1) * P],
                     w_hi[:, c, 2 * D:3 * D], w_lo[:, c, 2 * D:3 * D]) for c in range(KC)]).then_inc(proj, 1)


def three(pe, dst, chunks, stop=True):
    steps = [p for s_hi, s_lo, m_hi, m_lo in chunks for p in ((s_hi, m_hi), (s_hi, m_lo), (s_lo, m_hi))]
    for n, (s, m) in enumerate(steps):
        mm = pe.matmul(dst, s, m, start=(n == 0), stop=(stop and n == len(steps) - 1))
    return mm


def attention0(nc, st, sb, sems, bank, ident, qk, v0, ctx0, xT_hi, xT_lo):
    G = 4
    NB = QT
    TURNS = 4
    U = TURNS * NB * G
    LOOPS = B * H0 // (G * TURNS)
    BEHIND = 7
    FULL = 96
    ROWS = FULL + 2
    VW = 32
    both = [sb(st, f"stack{u}", [P, G, 2, S], F32R)[:, :, :, :] for u in range(TURNS // 2)]
    both += [buf[:, :, :].rearrange("p c (n s) -> p c n s", n=2) for buf in (xT_hi, xT_lo)]
    stack = [[buf[0:ROWS, h, :, :] for h in range(G)] for buf in both]
    zero_one = sb(st, "zero_one", [P, 2])
    vst = [sb(st, f"values{i}", [P, QT, G, VW]) for i in range(2)]
    pT = [sb(st, f"pT{i}", [P, G, S]) for i in range(2)]
    cT = sb(st, "ctxT", [P, S])
    mrow = sb(st, "max_rows", [2 * G, S], F32R)
    negmax = [sb(st, f"negmax{i}", [P, QT, G]) for i in range(2)]
    msplit = sb(st, "max_split", [P, QT, G, 2], F32R)
    rden = sb(st, "rden", [P, QT, G])
    (cleared, zeros_ok, ones_ok, stk0, stk1, stk2, stk3, scored, maxed, mhi_ok, msplit_ok, m_turned, mrow_ok, max_in, v_ok,
     rescored, exped, weighted, cT_ok, c_turned, inverted, normed) = sems(
        st, "B_cleared B_zeros B_ones B_stack0 B_stack1 B_stack2 B_stack3 B_scored B_maxed B_mhi B_msplit B_m_turned B_mrow "
            "B_max_in B_v B_rescored B_exped B_weighted B_cT B_c_turned B_inverted B_normed")
    stk = [stk0, stk1, stk2, stk3]

    def positive(n):
        return not isinstance(n, int) or n > 0

    def iterations(eng, blocks):
        for q in range(TURNS * NB):
            blocks(0, q, False)
        with eng.Fori(1, LOOPS) as i:
            for q in range(TURNS * NB):
                blocks(i, q, False)
        for q in range(BEHIND + 1):
            blocks(LOOPS, q, True)

    def earlier(i, q, n):
        if q >= n:
            return i, q - n
        return None if isinstance(i, int) and i == 0 else (i - 1, q - n + TURNS * NB)

    def columns(i, u):
        at = i * (TURNS // B * G * HD0) + u // B * G * HD0
        return slice(at, at + G * HD0) if isinstance(i, int) else bass.ds(at, G * HD0)

    with nc.Block() as block:
        @block.sync
        def _(sp):
            def load(i, u):
                chunk = slice(i, i + 1) if isinstance(i, int) else bass.ds(i, 1)
                if isinstance(i, int) and i == 0:
                    sp.wait_ge(zeros_ok, 2 * u + 2)
                else:
                    sp.wait_ge(rescored, i * U - U + (u + 1) * NB * G)
                    settle(sp)
                for h in range(G):
                    rows = slice((u // B * G + h) * HD0, (u // B * G + h + 1) * HD0)
                    cols = slice(u % B * S, (u % B + 1) * S)
                    for slot, pair in enumerate((slice(1, 3, 1), slice(1, 4, 2), slice(0, 3, 2))):
                        sp.dma_start(stack[u][h][slot * HD0:(slot + 1) * HD0, :, :].bitcast(F32),
                                     qk[rows, pair, chunk, cols].rearrange("p n c s -> p (n c) s").bitcast(F32)
                                     ).then_inc(stk[u], 16)

            def maxima(i, u):
                sp.wait_ge(mrow_ok, i * TURNS + u + 1)
                for h in range(G):
                    sp.dma_start(stack[u][h][FULL:ROWS, 0, :].bitcast(F32),
                                 mrow[2 * h:2 * h + 2, :].bitcast(F32)).then_inc(max_in, 16)

            for u in range(TURNS):
                load(0, u)
            for u in range(TURNS):
                maxima(0, u)
                if u:
                    load(1, u - 1)
            with sp.Fori(1, LOOPS - 1) as i:
                for u in range(TURNS):
                    maxima(i, u)
                    load(i + 1 if u else i, (u - 1) % TURNS)
            for u in range(TURNS):
                maxima(LOOPS - 1, u)
                if u == 0:
                    load(LOOPS - 1, TURNS - 1)
            sp.wait_ge(max_in, 16 * G * TURNS * LOOPS)

        @block.gpsimd
        def _(pool):
            pool.memset(zero_one[:, 0:1], 0.0).then_inc(cleared, 1)
            pool.memset(zero_one[:, 1:2], 1.0).then_inc(cleared, 1)
            for i in range(2):
                pool.memset(vst[i][:, :, :, :], 0.0).then_inc(cleared, 1)
            pool.wait_ge(cleared, 4)
            for i in range(2):
                pool.memset(vst[i][:, :, :, HD0:HD0 + 1], 1.0).then_inc(cleared, 1)

            def values(i, u):
                t = i * TURNS + u
                if positive(NB * (t - 1)):
                    pool.wait_ge(weighted, NB * (t - 1))
                    settle(pool)
                b = u % B
                src = v0[:, b * QT:(b + 1) * QT, columns(i, u)].rearrange("p t (h d) -> p t h d", h=G)
                pool.tensor_copy(vst[u % 2][:, :, :, 0:HD0], src).then_inc(v_ok, 1)

            for u in range(TURNS):
                values(0, u)
            with pool.Fori(1, LOOPS) as i:
                for u in range(TURNS):
                    values(i, u)

        @block.tensor
        def _(pe):
            def first_scores(i, q, h):
                n, u = i * U + q * G + h, q // NB
                if q % NB == 0 and h == 0:
                    pe.wait_ge(stk[u], (i + 1) * 16 * 3 * G)
                if positive(n - 3):
                    pe.wait_ge(maxed, n - 3)
                at = q % NB * P
                pe.matmul(bank[h][:, :], stack[u][h][0:FULL, 0, at:at + P], stack[u][h][0:FULL, 1, :],
                          start=True, stop=True).then_inc(scored, 1)

            def second_scores(i, q, h):
                n, u = i * U + q * G + h, q // NB
                if q % NB == 0 and h == 0:
                    if isinstance(i, int) and i == 0 and u == 0:
                        pe.wait_ge(ones_ok, TURNS)
                    pe.wait_ge(max_in, (i * TURNS + u + 1) * 16 * G)
                if positive(n - 1):
                    pe.wait_ge(exped, n - 1)
                at = q % NB * P
                pe.matmul(bank[4 + h % 2][:, :], stack[u][h][:, 1, at:at + P], stack[u][h][:, 0, :],
                          start=True, stop=True).then_inc(rescored, 1)

            def context(i, q):
                u, t = q // NB, q % NB
                pe.wait_ge(exped, i * U + (q + 1) * G)
                if t == 0:
                    pe.wait_ge(v_ok, i * TURNS + u + 1)
                    if positive(i * TURNS + u):
                        pe.wait_ge(cT_ok, i * TURNS + u)
                for h in range(G):
                    mm = pe.matmul(bank[6][h * VW:(h + 1) * VW, :], vst[u % 2][:, t, h, :], pT[q % 2][:, h, :],
                                   start=(t == 0), stop=(t == NB - 1))
                mm.then_inc(weighted, 1)

            def turn_maxima(i, u):
                t = i * TURNS + u
                pe.wait_ge(msplit_ok, t + 1)
                if positive(t - 2):
                    pe.wait_ge(normed, t - 2)
                if positive(t):
                    pe.wait_ge(mrow_ok, t)
                for q in range(QT):
                    mm = pe.transpose(bank[7][0:2 * G, q * P:(q + 1) * P],
                                      msplit[:, q, :, :].bitcast(F32).rearrange("p h n -> p (h n)"), ident[:, :])
                mm.then_inc(m_turned, 1)

            def turn_context(i, u, ends):
                t = i * TURNS + u
                pe.wait_ge(cT_ok, t + 1)
                if ends:
                    pe.wait_ge(mrow_ok, LOOPS * TURNS)
                else:
                    pe.wait_ge(mrow_ok, t + 3)
                if positive(t):
                    pe.wait_ge(normed, t)
                for q in range(QT):
                    mm = pe.transpose(bank[7][:, q * P:(q + 1) * P], cT[:, q * P:(q + 1) * P], ident[:, :])
                mm.then_inc(c_turned, 1)

            def blocks(i, q, follow):
                again, weigh = earlier(i, q, BEHIND), earlier(i, q, BEHIND + 1)

                def scores(h):
                    if not follow:
                        first_scores(i, q, h)
                    if again and not (follow and q >= BEHIND):
                        second_scores(*again, h)
                scores(0)
                scores(1)
                if weigh:
                    context(*weigh)
                done = earlier(i, q, NB)
                if q % NB == 0 and done and not (follow and q >= NB):
                    turn_maxima(done[0], done[1] // NB)
                done = earlier(i, q, BEHIND + 2 + NB)
                if q % NB == 1 and done:
                    turn_context(done[0], done[1] // NB, follow)
                scores(2)
                scores(3)
            iterations(pe, blocks)
            turn_context(LOOPS - 1, TURNS - 1, True)

        @block.vector
        def _(dve):
            for u in range(TURNS):
                if u:
                    dve.wait_ge(zeros_ok, 2 * u)
                dve.memset(both[u][0:FULL, :, 1, :].bitcast(F32), 0.0).then_inc(zeros_ok, 1)
            dve.wait_ge(cleared, 2)
            for u in range(TURNS):
                dve.tensor_copy(both[u][FULL:ROWS, :, 1, :], zero_one[FULL:ROWS, None, 1:2].to_broadcast([2, G, S])
                                ).then_inc(ones_ok, 1)

            def maximum(i, q, h):
                u = q // NB
                dve.wait_ge(scored, i * U + q * G + h + 1)
                if q % NB == 0 and h == 0 and positive(i * TURNS + u - 1):
                    dve.wait_ge(msplit_ok, i * TURNS + u - 1)
                dve.tensor_reduce(negmax[u % 2][:, q % NB, h:h + 1], bank[h][:, :], AX_X, ALU.max, negate=True
                                  ).then_inc(maxed, 1)

            def split_maxima(i, u):
                t = i * TURNS + u
                dve.wait_ge(maxed, (t + 1) * NB * G)
                if positive(t):
                    dve.wait_ge(m_turned, t)
                dve.tensor_copy(msplit[:, :, :, 0], negmax[u % 2][:, :, :]).then_inc(mhi_ok, 1)
                dve.wait_ge(mhi_ok, t + 1)
                dve.tensor_tensor(msplit[:, :, :, 1], negmax[u % 2][:, :, :], msplit[:, :, :, 0].bitcast(F32),
                                  ALU.subtract).then_inc(msplit_ok, 1)

            def normalise(i, u):
                t, b = i * TURNS + u, u % B
                dve.wait_ge(c_turned, t + 1)
                if positive(t):
                    dve.wait_ge(normed, t)
                heads = bank[7][:, :].rearrange("p (q h v) -> p q h v", q=QT, h=G)
                dve.reciprocal(rden[:, :, :], heads[:, :, :, HD0]).then_inc(inverted, 1)
                dve.wait_ge(inverted, t + 1)
                dst = ctx0[:, b * QT:(b + 1) * QT, columns(i, u)].rearrange("p q (h d) -> p q h d", h=G)
                settle(dve)
                dve.tensor_tensor(dst, heads[:, :, :, 0:HD0],
                                  rden[:, :, :, None].to_broadcast([P, QT, G, HD0]), ALU.mult).then_inc(normed, 1)

            def blocks(i, q, follow):
                if not follow:
                    for h in range(G):
                        maximum(i, q, h)
                    if q % NB == NB - 1:
                        split_maxima(i, q // NB)
                done = earlier(i, q, BEHIND + 2 + NB)
                if q % NB == 1 and done:
                    normalise(done[0], done[1] // NB)
            iterations(dve, blocks)
            normalise(LOOPS - 1, TURNS - 1)

        @block.scalar
        def _(act):
            nc.scalar.preload_act_table(ACT.Exp)
            act.wait_ge(cleared, 2)
            for u in range(TURNS):
                if u:
                    act.wait_ge(zeros_ok, 2 * u)
                act.activation(both[u][0:FULL, :, 0, :], zero_one[0:FULL, None, 0:1].to_broadcast([FULL, G, S]),
                               ACT.Copy).then_inc(zeros_ok, 1)

            def exponent(i, q, h):
                act.wait_ge(rescored, i * U + q * G + h + 1)
                if h == 0 and positive(i * (U // G) + q - 1):
                    act.wait_ge(weighted, i * (U // G) + q - 1)
                act.activation(pT[q % 2][:, h, :], bank[4 + h % 2][:, :], ACT.Exp).then_inc(exped, 1)

            def maxima_row(i, u):
                t = i * TURNS + u
                act.wait_ge(m_turned, t + 1)
                if positive(t):
                    act.wait_ge(max_in, 16 * G * t)
                act.activation(mrow[:, :], bank[7][0:2 * G, :], ACT.Copy).then_inc(mrow_ok, 1)

            def context_rows(i, u):
                t = i * TURNS + u
                act.wait_ge(weighted, NB * (t + 1))
                if positive(t):
                    act.wait_ge(c_turned, t)
                act.activation(cT[:, :], bank[6][:, :], ACT.Copy).then_inc(cT_ok, 1)

            def blocks(i, q, follow):
                again = earlier(i, q, BEHIND)
                exps = again and not (follow and q >= BEHIND)
                for h in range(G - 1):
                    if exps:
                        exponent(*again, h)
                done = earlier(i, q, BEHIND + NB)
                if q % NB == 3 and done:
                    context_rows(done[0], done[1] // NB)
                if exps:
                    exponent(*again, G - 1)
                done = earlier(i, q, NB)
                if q % NB == 0 and done and not (follow and q >= NB):
                    maxima_row(done[0], done[1] // NB)
            iterations(act, blocks)




def middle(nc, st, sb, sems, bank, a, ident, neghalf, x_res, ctx0, xT_hi, xT_lo, x_mid):
    ow_hi = sb(st, "ow_hi", [P, KC, D], F32R)
    ow_lo = sb(st, "ow_lo", [P, KC, D], F32R)
    m_gate = sb(st, "m_gate", [P, KC, O8, DH], F32R)
    m_up = sb(st, "m_up", [P, KC, O8, DH], F32R)
    m_down = sb(st, "m_down", [P, NHC, D], F32R)
    ob = sb(st, "ob", [P, D])
    scales = sb(st, "tern_scales", [P, 3])
    with ExitStack() as tmp:
        build_ternary(nc, tmp, sb, sems, bank, a, ow_hi, ow_lo, m_gate, m_up, m_down, ob, scales)

    cs = sb(st, "ctx_tile", [P, D])
    cT_hi = sb(st, "cT_hi", [P, KC, P], F32R)
    cT_lo = sb(st, "cT_lo", [P, KC, P], F32R)
    tT_hi = sb(st, "tT_hi", [P, KC, P], F32R)
    tT_lo = sb(st, "tT_lo", [P, KC, P], F32R)
    gact = sb(st, "gact", [P, 3, D])
    h = sb(st, "hidden", [P, NHC * P])
    hT_hi = sb(st, "hT_hi", [P, NHC, P], F32R)
    hT_lo = sb(st, "hT_lo", [P, NHC, P], F32R)
    y = sb(st, "y_attn", [P, D])
    y2 = sb(st, "y_ffn", [P, D])
    xn1 = sb(st, "xn1", [P, D])
    xn2 = sb(st, "xn2", [P, D])
    stats = sb(st, "statsC", [P, 4, 6])
    mv = sb(st, "mvC", [P, 4, 2])
    veps = sb(st, "vepsC", [P, 4, 1])
    rstd = sb(st, "rstdC", [P, 4, 1])
    (zeroed, cs_ok, c_turned, cT_hi_ok, cT_lo_ok, o_done, y_ok, x_turned, tT_hi_ok, tT_lo_ok, gu_done, act_ok, h_ok,
     h_turned, hT_hi_ok, hT_lo_ok, d_done, y2_ok, x2_turned, xT_hi_ok, xT_lo_ok, x1_ok, x2_ok,
     stored) = sems(
        st, "C_zeroed C_cs C_c_turned C_cT_hi C_cT_lo C_o_done C_y C_x_turned C_tT_hi C_tT_lo C_gu_done C_act C_h "
            "C_h_turned C_hT_hi C_hT_lo C_d_done C_y2 C_x2_turned C_xT_hi C_xT_lo C_x1 C_x2 C_stored")
    stat, aggr, eps_ok, rstd_ok, applied = (sems(st, " ".join(f"C_{n}{k}" for k in range(4)))
                                            for n in ("stat", "aggr", "eps", "rstd", "applied"))
    h_main = h[:, 0:O8 * P].rearrange("p (i d) -> p i d", i=O8)
    h_rem = h[:, O8 * P:].rearrange("p (i d) -> p i d", i=O8)
    mid_v = x_mid.rearrange("(t p) h -> p t h", p=P)
    HI = O8 // 2

    def tile_of(buf, t):
        return buf[:, t, :] if isinstance(t, int) else buf[:, bass.ds(t, 1), :]

    def columns_of(buf, t):
        return buf[:, :, t * P:(t + 1) * P] if isinstance(t, int) else buf[:, :, bass.ds(t * P, P)]

    def steps(eng, before, step):
        before()
        step(0, True, False)
        with eng.Fori(1, NT - 1) as t:
            step(t, False, False)
        step(NT - 1, False, True)

    def quads(b):
        return b[:, :].rearrange("p (c q) -> p c q", c=KC)

    with nc.Block() as block:
        @block.sync
        def _(sp):
            def store(t, first, last):
                sp.wait_ge(x2_ok, t + 1)
                sp.dma_start(tile_of(mid_v, t), tile_of(x_res, t)).then_inc(stored, 16)
            steps(sp, lambda: None, store)
            sp.wait_ge(stored, 16 * NT)

        @block.gpsimd
        def _(pool):
            def power(n, t):
                pool.wait_ge(eps_ok[n], t + 1)
                settle(pool)
                pool.tensor_tensor(rstd[:, n, :], veps[:, n, :], neghalf[:, :], ALU.pow).then_inc(rstd_ok[n], 1)

            def stage(t):
                if not (isinstance(t, int) and t == 0):
                    pool.wait_ge(c_turned, t)
                    settle(pool)
                pool.tensor_copy(cs[:, :], tile_of(ctx0, t)).then_inc(cs_ok, 1)

            def before():
                pool.memset(h[:, O8 * P:], 0.0).then_inc(zeroed, 1)
                stage(0)
                stage(1)
                power(0, 0)
                power(1, 0)

            def step(t, first, last, ahead=True):
                if not first:
                    power(2, t - 1)
                    power(3, t - 1)
                if ahead:
                    stage(t + 2)
                if not last:
                    power(0, t + 1)
                    power(1, t + 1)

            before()
            step(0, True, False)
            with pool.Fori(1, NT - 2) as t:
                step(t, False, False)
            step(NT - 2, False, False, False)
            step(NT - 1, False, True, False)
            power(2, NT - 1)
            power(3, NT - 1)

        @block.tensor
        def _(pe):
            def turn(src, dst, sem):
                for c in range(KC):
                    mm = pe.transpose(dst[:, c * P:(c + 1) * P], src[:, c * P:(c + 1) * P], ident[:, :])
                mm.then_inc(sem, 1)

            def turn_ctx(t, first):
                pe.wait_ge(cs_ok, t + 1)
                turn(cs, bank[0], c_turned)

            def project(t, first):
                pe.wait_ge(cT_lo_ok, t + 1)
                if not first:
                    pe.wait_ge(y2_ok, t - 1)
                three(pe, bank[1][:, :], [(cT_hi[:, c, :], cT_lo[:, c, :], ow_hi[:, c, :], ow_lo[:, c, :])
                                          for c in range(KC)]).then_inc(o_done, 1)

            def turn_x1(t):
                pe.wait_ge(applied[1], t + 1)
                turn(xn1, bank[0], x_turned)

            def turn_x2(t):
                pe.wait_ge(applied[3], t + 1)
                turn(xn2, bank[0], x2_turned)

            def before():
                turn_ctx(0, True)
                project(0, True)
                turn_x1(0)

            def gate_up(t, g, first):
                if not first:
                    pe.wait_ge(hT_lo_ok, 3 * t - 2 + g)
                    pe.wait_ge(h_ok, 3 * t - 2 + g)
                for m, b in ((m_gate, bank[2 + g]), (m_up, bank[5 + g])):
                    dst = b[:, :] if g < 2 else b[:, 0:O8 * REM]
                    mats = [m[:, c, g * HI:(g + 1) * HI, 0:MAIN] if g < 2 else m[:, c, :, MAIN:DH]
                            for c in range(KC)]
                    for n, (s, c) in enumerate((s, c) for c in range(KC) for s in (tT_hi, tT_lo)):
                        mm = pe.matmul(dst, s[:, c, :], mats[c], start=(n == 0), stop=(n == 2 * KC - 1))
                mm.then_inc(gu_done, 1)

            def turn_hidden(t, g):
                pe.wait_ge(h_ok, 3 * t + g + 1)
                for c in range(KC):
                    n = g * KC + c
                    mm = pe.transpose(bank[2 + g][:, c * P:(c + 1) * P], h[:, n * P:(n + 1) * P], ident[:, :])
                mm.then_inc(h_turned, 1)

            def down(t, g):
                pe.wait_ge(hT_lo_ok, 3 * t + g + 1)
                for n in range(g * KC, (g + 1) * KC):
                    for s in (hT_hi, hT_lo):
                        mm = pe.matmul(bank[1][:, :], s[:, n, :], m_down[:, n, :], start=(n == 0 and s is hT_hi),
                                       stop=(n == NHC - 1 and s is hT_lo))
                if g == 2:
                    mm.then_inc(d_done, 1)

            def step(t, first, last):
                pe.wait_ge(tT_lo_ok, t + 1)
                if not last:
                    turn_ctx(t + 1, first)
                gate_up(t, 0, first)
                if not last:
                    project(t + 1, first)
                gate_up(t, 1, first)
                if not first:
                    turn_x2(t - 1)
                turn_hidden(t, 0)
                gate_up(t, 2, first)
                turn_hidden(t, 1)
                if not last:
                    pe.wait_ge(y_ok, t + 2)
                    if not first:
                        pe.wait_ge(xT_lo_ok, t)
                    turn_x1(t + 1)
                else:
                    pe.wait_ge(y2_ok, t)
                down(t, 0)
                turn_hidden(t, 2)
                down(t, 1)
                down(t, 2)

            steps(pe, before, step)
            turn_x2(NT - 1)

        @block.scalar
        def _(act):
            nc.scalar.preload_act_table(ACT.Silu)

            def split_ctx(t, first):
                act.wait_ge(c_turned, t + 1)
                if not first:
                    act.wait_ge(o_done, t)
                act.activation(cT_hi[:, :, :], quads(bank[0]), ACT.Copy).then_inc(cT_hi_ok, 1)

            def split_x1(t, first):
                act.wait_ge(x_turned, t + 1)
                if not first:
                    act.wait_ge(gu_done, 3 * t)
                act.activation(tT_hi[:, :, :], quads(bank[0]), ACT.Copy).then_inc(tT_hi_ok, 1)

            def split_x2(t):
                act.wait_ge(x2_turned, t + 1)
                settle(act)
                act.activation(columns_of(xT_hi, t), quads(bank[0]), ACT.Copy).then_inc(xT_hi_ok, 1)

            def before():
                split_ctx(0, True)
                split_x1(0, True)

            def gate(t, g, first):
                n = D if g < 2 else O8 * REM
                act.wait_ge(gu_done, 3 * t + g + 1)
                if not first:
                    act.wait_ge(h_ok, 3 * t - 2 + g)
                act.activation(gact[:, g, 0:n], bank[2 + g][:, 0:n], ACT.Silu, scale=scales[:, 0:1]
                               ).then_inc(act_ok, 1)

            def split_hidden(t, g, first):
                act.wait_ge(h_turned, 3 * t + g + 1)
                if not first:
                    act.wait_ge(d_done, t)
                act.activation(hT_hi[:, g * KC:(g + 1) * KC, :], quads(bank[2 + g]), ACT.Copy).then_inc(hT_hi_ok, 1)

            def step(t, first, last):
                if not last:
                    split_ctx(t + 1, False)
                gate(t, 0, first)
                gate(t, 1, first)
                if not first:
                    split_x2(t - 1)
                split_hidden(t, 0, first)
                gate(t, 2, first)
                split_hidden(t, 1, first)
                if not last:
                    split_x1(t + 1, False)
                split_hidden(t, 2, first)
                act.wait_ge(d_done, t + 1)
                if not first:
                    act.wait_ge(applied[2], t)
                act.activation(y2[:, :], bank[1][:, :], ACT.Copy, scale=scales[:, 2:3]).then_inc(y2_ok, 1)

            steps(act, before, step)
            split_x2(NT - 1)

        @block.vector
        def _(dve):
            def statistics(n, t, src, ready, first):
                dve.wait_ge(ready, t + 1)
                if not first:
                    dve.wait_ge(aggr[n], t)
                    settle(dve)
                dve.bn_stats(stats[:, n, :], src).then_inc(stat[n], 1)
                dve.wait_ge(stat[n], t + 1)
                if not first:
                    dve.wait_ge(applied[n], t)
                settle(dve)
                dve.bn_aggr(mv[:, n, :], stats[:, n, :]).then_inc(aggr[n], 1)
                dve.wait_ge(aggr[n], t + 1)
                if not first:
                    dve.wait_ge(rstd_ok[n], t)
                dve.tensor_scalar(veps[:, n, :], mv[:, n, 1:2], EPS, None, ALU.add).then_inc(eps_ok[n], 1)

            def apply(n, t, dst, src):
                dve.wait_ge(rstd_ok[n], t + 1)
                dve.tensor_scalar(dst, src, mv[:, n, 0:1], rstd[:, n, :], ALU.subtract, ALU.mult
                                  ).then_inc(applied[n], 1)

            def attention_out(t, first):
                dve.wait_ge(o_done, t + 1)
                if not first:
                    dve.wait_ge(x1_ok, t)
                dve.tensor_tensor(y[:, :], bank[1][:, :], ob[:, :], ALU.add).then_inc(y_ok, 1)
                statistics(0, t, y[:, :], y_ok, first)

            def first_residual(t, first):
                apply(0, t, y[:, :], y[:, :])
                dve.wait_ge(applied[0], t + 1)
                dve.tensor_tensor(tile_of(x_res, t), tile_of(x_res, t), y[:, :], ALU.add).then_inc(x1_ok, 1)
                statistics(1, t, tile_of(x_res, t), x1_ok, first)

            def first_norm(t, first):
                if not first:
                    dve.wait_ge(x_turned, t)
                apply(1, t, xn1[:, :], tile_of(x_res, t))

            def low(sem_hi, t, dst, hi, src, sem):
                dve.wait_ge(sem_hi, t + 1)
                dve.tensor_tensor(dst, src, hi.bitcast(F32), ALU.subtract).then_inc(sem, 1)

            def second_residual(t, first):
                statistics(2, t, y2[:, :], y2_ok, first)
                apply(2, t, y2[:, :], y2[:, :])

                dve.wait_ge(applied[2], t + 1)
                dve.tensor_tensor(tile_of(x_res, t), tile_of(x_res, t), y2[:, :], ALU.add).then_inc(x2_ok, 1)
                statistics(3, t, tile_of(x_res, t), x2_ok, first)

            def second_norm(t, first):
                if not first:
                    dve.wait_ge(x2_turned, t)
                apply(3, t, xn2[:, :], tile_of(x_res, t))

            def before():
                low(cT_hi_ok, 0, cT_lo[:, :, :], cT_hi[:, :, :], quads(bank[0]), cT_lo_ok)
                attention_out(0, True)
                first_residual(0, True)
                first_norm(0, True)
                low(tT_hi_ok, 0, tT_lo[:, :, :], tT_hi[:, :, :], quads(bank[0]), tT_lo_ok)
                dve.wait_ge(zeroed, 1)

            def hidden(t, g, first):
                dve.wait_ge(act_ok, 3 * t + g + 1)
                if not first:
                    dve.wait_ge(h_turned, 3 * t - 2 + g)
                if g < 2:
                    dve.tensor_tensor(h_main[:, g * HI:(g + 1) * HI, :],
                                      gact[:, g, :].rearrange("p (i d) -> p i d", i=HI),
                                      bank[5 + g][:, :].rearrange("p (i d) -> p i d", i=HI), ALU.mult
                                      ).then_inc(h_ok, 1)
                else:
                    dve.tensor_tensor(h_rem[:, :, 0:REM],
                                      gact[:, g, 0:O8 * REM].rearrange("p (i d) -> p i d", i=O8),
                                      bank[5 + g][:, 0:O8 * REM].rearrange("p (i d) -> p i d", i=O8), ALU.mult
                                      ).then_inc(h_ok, 1)

            def low_hidden(t, g):
                low(hT_hi_ok, 3 * t + g, hT_lo[:, g * KC:(g + 1) * KC, :], hT_hi[:, g * KC:(g + 1) * KC, :],
                    quads(bank[2 + g]), hT_lo_ok)

            def step(t, first, last):
                if not last:
                    low(cT_hi_ok, t + 1, cT_lo[:, :, :], cT_hi[:, :, :], quads(bank[0]), cT_lo_ok)
                if not first:
                    second_residual(t - 1, isinstance(t, int) and t == 1)
                hidden(t, 0, first)
                if not first:
                    second_norm(t - 1, isinstance(t, int) and t == 1)
                if not last:
                    attention_out(t + 1, False)
                    first_residual(t + 1, False)
                hidden(t, 1, first)
                if not first:
                    low(xT_hi_ok, t - 1, columns_of(xT_lo, t - 1), columns_of(xT_hi, t - 1), quads(bank[0]), xT_lo_ok)
                if not last:
                    first_norm(t + 1, False)
                low_hidden(t, 0)
                hidden(t, 2, first)
                low_hidden(t, 1)
                if not last:
                    low(tT_hi_ok, t + 1, tT_lo[:, :, :], tT_hi[:, :, :], quads(bank[0]), tT_lo_ok)
                low_hidden(t, 2)

            before()
            step(0, True, False)
            step(1, False, False)
            with dve.Fori(2, NT - 1) as t:
                step(t, False, False)
            step(NT - 1, False, True)
            second_residual(NT - 1, False)
            second_norm(NT - 1, False)
            low(xT_hi_ok, NT - 1, columns_of(xT_lo, NT - 1), columns_of(xT_hi, NT - 1), quads(bank[0]), xT_lo_ok)


def build_ternary(nc, st, sb, sems, bank, a, ow_hi, ow_lo, m_gate, m_up, m_down, ob, scales):
    N_W = O8 * DH * DI
    ow_raw = sb(st, "ow_raw", [P, KC, D])
    raw = [sb(st, n, s) for n, s in (("gate_raw", [P, O8, DH]), ("up_raw", [P, O8, DH]),
                                     ("down_raw", [P, O8, DI]), ("down_rem_raw", [P, O8, DI]))]
    above = [sb(st, f"above{i}", list(r.shape)) for i, r in enumerate(raw)]
    ones = sb(st, "ones_sq", [P, P])
    sums = sb(st, "sums", [P, 4])
    means = sb(st, "means", [P, 4])
    half = sb(st, "half", [P, 2, 3])
    (w_in, ow_in, cleared, summed, totalled, means_ok, down_ok, half_ok, scales_ok, above_ok, minus_ok, ow_hi_ok,
     ow_lo_ok) = sems(st, "T_w_in T_ow_in T_cleared T_summed T_totalled T_means T_down_mean T_half T_scales "
                          "T_above T_minus T_ow_hi T_ow_lo")
    HALVES = (slice(0, DI), slice(DI, P))
    REMS = (slice(0, REM), slice(DI, DI + REM))
    SCALE_OF = (0, 1, 2, 2)

    with nc.Block() as block:
        @block.sync
        def _(sp):
            sp.wait_ge(cleared, 3)
            for rows in HALVES:
                sp.dma_start(raw[0][rows, :, :], a["gateT"]).then_inc(w_in, 16)
                sp.dma_start(raw[1][rows, :, :], a["upT"]).then_inc(w_in, 16)
            sp.dma_start(raw[2][:, :, :], a["downT"][0:MAIN]).then_inc(w_in, 16)
            for rows in REMS:
                sp.dma_start(raw[3][rows, :, :], a["downT"][MAIN:DH]).then_inc(w_in, 16)
            sp.dma_start(ow_raw[:, :, :], a["ow"].rearrange("(c p) n -> p c n", p=P)).then_inc(ow_in, 16)
            sp.dma_start(ob[:, :], a["ob"].rearrange("(a n) -> a n", a=1).to_broadcast([P, D])).then_inc(ow_in, 16)
            sp.wait_ge(ow_in, 32)

        @block.gpsimd
        def _(pool):
            pool.memset(raw[3][:, :, :], 0.0).then_inc(cleared, 1)
            pool.memset(sums[:, :], 0.0).then_inc(cleared, 1)
            pool.memset(ones[:, :], 1.0).then_inc(cleared, 1)
            pool.wait_ge(ow_hi_ok, 1)
            pool.tensor_tensor(ow_lo[:, :, :], ow_raw[:, :, :], ow_hi[:, :, :].bitcast(F32), ALU.subtract
                               ).then_inc(ow_lo_ok, 1)

        @block.tensor
        def _(pe):
            pe.wait_ge(summed, 4)
            pe.matmul(bank[0][:, 0:4], ones[:, :], sums[:, :], start=True, stop=True).then_inc(totalled, 1)

        def signed_copy(engine, dst, src, sign):
            if engine == "act":
                return nc.scalar.activation(dst, src, ACT.Copy, scale=-float(sign))
            return nc.vector.tensor_scalar(dst, src, -float(sign), None, ALU.mult)

        def octonion_in(eng, name, m, minus):
            for c in range(KC):
                for n, rows in enumerate(HALVES):
                    for k in range(O8):
                        j, sign = OCT[2 * c + n, k]
                        signed_copy(name, m[rows, c, k, :], minus[rows, j, :], sign)

        @block.scalar
        def _(act):
            act.wait_ge(ow_in, 32)
            act.activation(ow_hi[:, :, :], ow_raw[:, :, :], ACT.Copy).then_inc(ow_hi_ok, 1)
            act.wait_ge(minus_ok, 1)
            octonion_in(act, "act", m_up, above[1])

        @block.vector
        def _(dve):
            dve.wait_ge(cleared, 3)
            dve.wait_ge(w_in, 7 * 16)
            for n, rows in enumerate((P, P, P, DI)):
                dve.tensor_reduce(sums[0:rows, n:n + 1], raw[n][0:rows, :, :], mybir.AxisListType.XY, ALU.add,
                                  apply_absolute_value=True).then_inc(summed, 1)
            dve.wait_ge(totalled, 1)
            dve.tensor_scalar(means[:, 0:2], bank[0][:, 0:2], 0.5 / N_W, None, ALU.mult).then_inc(means_ok, 1)
            dve.tensor_scalar(means[:, 2:4], bank[0][:, 2:4], 1.0 / N_W, None, ALU.mult).then_inc(means_ok, 1)
            dve.wait_ge(means_ok, 2)
            dve.tensor_tensor(means[:, 2:3], means[:, 2:3], means[:, 3:4], ALU.add).then_inc(down_ok, 1)
            dve.wait_ge(down_ok, 1)
            dve.tensor_scalar(half[:, 0, :], means[:, 0:3], 0.5, None, ALU.mult).then_inc(half_ok, 1)
            dve.tensor_scalar(half[:, 1, :], means[:, 0:3], -0.5, None, ALU.mult).then_inc(half_ok, 1)
            dve.tensor_copy(scales[:, 0:2], means[:, 0:2]).then_inc(scales_ok, 1)
            dve.tensor_tensor(scales[:, 2:3], means[:, 1:2], means[:, 2:3], ALU.mult).then_inc(scales_ok, 1)
            dve.wait_ge(half_ok, 2)
            for n in (1, 0, 2, 3):
                s = SCALE_OF[n]
                dve.tensor_scalar(above[n][:, :, :], raw[n][:, :, :], half[:, 0, s:s + 1], None, ALU.is_gt
                                  ).then_inc(above_ok, 1)
            for n in (1, 0, 2, 3):
                s = SCALE_OF[n]
                dve.wait_ge(above_ok, 4)
                dve.scalar_tensor_tensor(out=above[n][:, :, :], in0=raw[n][:, :, :], scalar=half[:, 1, s:s + 1],
                                         in1=above[n][:, :, :], op0=ALU.is_lt, op1=ALU.subtract
                                         ).then_inc(minus_ok, 1)
            dve.wait_ge(minus_ok, 4)
            octonion_in(dve, "dve", m_gate, above[0])
            for i in range(O8):
                for k in range(O8):
                    j, sign = OCT[i, k]
                    signed_copy("dve", m_down[:, i, k * DI:(k + 1) * DI], above[2][:, j, :], sign)
                    rows = HALVES[i % 2]
                    signed_copy("dve", m_down[rows, O8 + i // 2, k * DI:(k + 1) * DI], above[3][rows, j, :], sign)


def attention1(nc, st, sb, sems, bank, a, ident, xT_hi, xT_lo, y1):
    SUB = NLAT // (2 * LAT)
    lat_hi = sb(st, "lat_hi", [P, B, 2 * LC, S], F32R)
    lat_lo = sb(st, "lat_lo", [P, B, 2 * LC, S], F32R)
    identr = sb(st, "identr", [P, P], F32R)
    mask = sb(st, "mask", [P, P], F32R)
    with ExitStack() as tmp:
        compress(nc, tmp, sb, sems, bank, a, ident, identr, mask, xT_hi, xT_lo, y1, lat_hi, lat_lo, SUB)

    HQ = REP
    W = HQ * D1
    STEPS = B * HQ
    wq_raw = sb(st, "wq_raw", [P, KC, W])
    wq_hi = sb(st, "wq_hi", [P, KC, W], F32R)
    wq_lo = sb(st, "wq_lo", [P, KC, W], F32R)
    wo_raw = sb(st, "wo_raw", [P, HQ, D])
    wo_hi = sb(st, "wo_hi", [P, HQ, D], F32R)
    wo_lo = sb(st, "wo_lo", [P, HQ, D], F32R)
    wu_raw = sb(st, "wu_raw", [P, 2, LC, D1])
    wu_hi = sb(st, "wu_hi", [P, 2, LC, D1], F32R)
    wu_lo = sb(st, "wu_lo", [P, 2, LC, D1], F32R)
    kT_hi = sb(st, "kT_hi", [P, B, S], F32R)
    kT_lo = sb(st, "kT_lo", [P, B, S], F32R)
    v_hi = sb(st, "v_hi", [P, B, S], F32R)
    v_lo = sb(st, "v_lo", [P, B, S], F32R)
    qT_hi = sb(st, "qT_hi", [P, S], F32R)
    qT_lo = sb(st, "qT_lo", [P, S], F32R)
    probs = sb(st, "probs_b", [P, 10 * P])
    pT_hi = sb(st, "pT_hi", [P, 10 * P], F32R)
    pT_lo = sb(st, "pT_lo", [P, 10 * P], F32R)
    cT_hi = sb(st, "c1T_hi", [P, B, HQ, S], F32R)
    cT_lo = sb(st, "c1T_lo", [P, B, HQ, S], F32R)
    negmax = sb(st, "negmax_b", [P, QT])
    den = sb(st, "den_b", [P, QT])
    rden = sb(st, "rden_b", [P, QT])
    (wq_in, wo_in, wu_in, wq_hi_ok, wq_lo_ok, wo_hi_ok, wo_lo_ok, wu_hi_ok, wu_lo_ok, kv_done, kv_hi_ok, kv_lo_ok,
     projected, q_hi_ok, q_lo_ok, scored, maxed, exped, inverted, normed, turned, pT_hi_ok, pT_lo_ok, weighted,
     c_hi_ok, c_lo_ok, o_done, o_added) = sems(
        st, "D_wq_in D_wo_in D_wu_in D_wq_hi D_wq_lo D_wo_hi D_wo_lo D_wu_hi D_wu_lo D_kv_done D_kv_hi D_kv_lo "
            "D_projected D_q_hi D_q_lo D_scored D_maxed D_exped D_inverted D_normed D_turned D_pT_hi D_pT_lo "
            "D_weighted D_c_hi D_c_lo D_o_done D_o_added")
    SCALE = D1 ** -0.5
    SCORES = ((0, ((3, 0),)), (1, ((2, 0), (0, 3 * P))), (2, ((1, 0),)))
    ORDER = [(b, q, at) for b, tiles in SCORES for q, at in tiles]
    BANK_MAXED = {3: 1, 2: 3, 0: 3, 1: 4}
    PROB_AT = [0, P, 3 * P, 6 * P]
    TURNS = ((3, ((0, 0),)), (4, ((1, 0), (3, 3 * P))), (5, ((2, 0),)))
    T_AT = {0: 0, 1: 4 * P, 3: 7 * P, 2: 8 * P}
    T_BANK = ((3, 0, 4 * P), (4, 4 * P, 4 * P), (5, 8 * P, 2 * P))
    PIECES = 3

    def kv_piece(s):
        if 1 <= s <= 3:
            return 1, False, s - 1
        if 5 <= s <= 7:
            return 0, True, s - 5
        return None

    def steps(eng, step):
        for s in range(STEPS):
            step(0, s, True, False)
        with eng.Fori(1, HK - 1) as g:
            for s in range(STEPS):
                step(g, s, False, False)
        for s in range(STEPS):
            step(HK - 1, s, False, True)

    def pieces_before(g, s, last):
        return 2 * PIECES * g + PIECES + max(0, min(s, 4) - 1) + (0 if last else max(0, s - 5))

    with nc.Block() as block:
        @block.sync
        def _(sp):
            wq_v = a["WqT"].rearrange("(c p) n -> p c n", p=P)
            wo_v = a["WoT"].rearrange("(h d) n -> d h n", d=D1)
            wk_v = a["WkupT"].rearrange("(c p) n -> p c n", p=P)
            wv_v = a["WvupT"].rearrange("(c p) n -> p c n", p=P)

            def part(v, axis, g, n):
                at = slice(g * n, (g + 1) * n) if isinstance(g, int) else bass.ds(g * n, n)
                return v[:, :, at] if axis == 2 else v[:, at, :]

            def load(g):
                if not (isinstance(g, int) and g == 0):
                    sp.wait_ge(wu_lo_ok, g)
                    settle(sp)
                sp.dma_start(wu_raw[:, 0, :, :], part(wk_v, 2, g, D1)).then_inc(wu_in, 16)
                sp.dma_start(wu_raw[:, 1, :, :], part(wv_v, 2, g, D1)).then_inc(wu_in, 16)
                if not (isinstance(g, int) and g == 0):
                    sp.wait_ge(wq_lo_ok, g * HQ)
                    settle(sp)
                sp.dma_start(wq_raw[:, :, :], part(wq_v, 2, g, W)).then_inc(wq_in, 16)
                if not (isinstance(g, int) and g == 0):
                    sp.wait_ge(wo_lo_ok, g)
                    settle(sp)
                sp.dma_start(wo_raw[:, :, :], part(wo_v, 1, g, HQ)).then_inc(wo_in, 16)

            load(0)
            with sp.Fori(1, HK) as g:
                load(g)
            sp.wait_ge(wo_in, 16 * HK)

        def split_points(g, s, last):
            out = []
            if s == 4 and not last:
                out.append(("wu", g + 1, 0))
            if s >= 4 and not last:
                out.append(("wq", g + 1, s - 4))
            if s == 4:
                out.append(("wo", g, 0))
            return out

        def views(kind, h):
            if kind == "wu":
                return wu_raw[:, :, :, :], wu_hi[:, :, :, :], wu_lo[:, :, :, :]
            if kind == "wo":
                return wo_raw[:, :, :], wo_hi[:, :, :], wo_lo[:, :, :]
            c = slice(h * D1, (h + 1) * D1)
            return wq_raw[:, :, c], wq_hi[:, :, c], wq_lo[:, :, c]

        @block.gpsimd
        def _(pool):
            def low(kind, g, h):
                raw, hi, lo = views(kind, h)
                done, sem = {"wu": (wu_hi_ok, wu_lo_ok), "wq": (wq_hi_ok, wq_lo_ok), "wo": (wo_hi_ok, wo_lo_ok)}[kind]
                pool.wait_ge(done, (g * HQ + h if kind == "wq" else g) + 1)
                pool.tensor_tensor(lo, raw, hi.bitcast(F32), ALU.subtract).then_inc(sem, 1)

            low("wu", 0, 0)
            for h in range(HQ):
                low("wq", 0, h)
            steps(pool, lambda g, s, first, last: [low(*x) for x in split_points(g, s, last)])

        @block.tensor
        def _(pe):
            def scores(g, s, first):
                b = s // HQ
                n = g * STEPS + s
                pe.wait_ge(q_lo_ok, n + 1)
                pe.wait_ge(kv_lo_ok, 2 * PIECES * g + (PIECES if b == 0 else 2 * PIECES))
                for bk, tiles in SCORES:
                    if not (first and s == 0):
                        pe.wait_ge(exped, QT * (n - 1) + {0: 1, 1: 3, 2: 4}[bk])
                    for q, at in tiles:
                        dst = bank[bk][:, at:at + (q + 1) * P]
                        cols = slice(q * P, (q + 1) * P)
                        keys = slice(0, (q + 1) * P)
                        pe.matmul(dst, qT_hi[:, cols], kT_hi[:, b, keys], start=True, stop=False)
                        pe.matmul(bank[bk][:, at + q * P:at + (q + 1) * P], identr[:, :], mask[:, :],
                                  start=False, stop=False, skip_group_check=True)
                        pe.matmul(dst, qT_hi[:, cols], kT_lo[:, b, keys], start=False, stop=False)
                        mm = pe.matmul(dst, qT_lo[:, cols], kT_hi[:, b, keys], start=False, stop=True)
                    mm.then_inc(scored, 1)

            def queries(g, s, first):
                busy = not (first and s <= 6)
                if s == STEPS:
                    g, s = g + 1, 0
                b, h = s // HQ, s % HQ
                n = g * STEPS + s
                pe.wait_ge(wq_lo_ok, g * HQ + h + 1)
                if busy:
                    pe.wait_ge(o_added, n - 6)
                three(pe, bank[6][:, :], [
                    (wq_hi[:, c, h * D1:(h + 1) * D1], wq_lo[:, c, h * D1:(h + 1) * D1],
                     xT_hi[:, c, b * S:(b + 1) * S], xT_lo[:, c, b * S:(b + 1) * S]) for c in range(KC)]
                ).then_inc(projected, 1)

            def weigh(g, s, last):
                n = g * STEPS + s
                b = (s - 1) % STEPS // HQ
                pe.wait_ge(pT_lo_ok, 3 * n)
                pe.wait_ge(kv_lo_ok, pieces_before(g, s, last))
                hh, hl, lh = (v_hi, pT_hi), (v_hi, pT_lo), (v_lo, pT_hi)
                passes = [(0, hh)] + [(t, x) for t in range(1, QT) for x in (hh, hl, lh)] + [(0, hl), (0, lh)]
                for n, (t, (v, p)) in enumerate(passes):
                    mm = pe.matmul(bank[7][:, t * P:S], v[:, b, t * D1:(t + 1) * D1],
                                   p[:, T_AT[t]:T_AT[t] + (QT - t) * P], start=(n == 0),
                                   stop=(n == len(passes) - 1), skip_group_check=True)
                mm.then_inc(weighted, 1)

            def outputs(g, s, drained=False):
                m = g * STEPS + s - 5
                blk_steps = 2 * g * HQ
                k = (s - 5) // HQ
                q = (s - 5) % HQ
                b = k % 2
                pe.wait_ge(c_lo_ok, blk_steps + (k + 1) * HQ)
                pe.wait_ge(wo_lo_ok, g + (1 if k >= 0 else 0))
                if not drained:
                    pe.wait_ge(q_lo_ok, g * STEPS + s + 2)
                else:
                    pe.wait_ge(o_added, m)
                three(pe, bank[6][:, :], [
                    (cT_hi[:, b, h, q * P:(q + 1) * P], cT_lo[:, b, h, q * P:(q + 1) * P],
                     wo_hi[:, h, :], wo_lo[:, h, :]) for h in range(HQ)]).then_inc(o_done, 1)

            def keys_values(g, b, piece, before_step):
                pe.wait_ge(wu_lo_ok, g + 1)
                if before_step is not None:
                    pe.wait_ge(c_lo_ok, before_step)
                if piece == 0:
                    mm = three(pe, bank[7][:, :], [
                        (wu_hi[:, 0, c, :], wu_lo[:, 0, c, :], lat_hi[:, b, c, :], lat_lo[:, b, c, :])
                        for c in range(LC)])
                else:
                    for i in range(2):
                        t = 2 * (piece - 1) + i
                        mm = three(pe, bank[7][:, i * D1:(i + 1) * D1], [
                            (lat_hi[:, b, LC + c, t * P:(t + 1) * P], lat_lo[:, b, LC + c, t * P:(t + 1) * P],
                             wu_hi[:, 1, c, :], wu_lo[:, 1, c, :]) for c in range(LC)])
                mm.then_inc(kv_done, 1)

            def turn(g, s, first):
                n = g * STEPS + s
                pe.wait_ge(normed, QT * (n + 1))
                if not (first and s == 0):
                    pe.wait_ge(pT_lo_ok, 3 * n)
                for bk, tiles in TURNS:
                    for t, at in tiles:
                        for q in range(t, QT):
                            col = at + (q - t) * P
                            mm = pe.transpose(bank[bk][:, col:col + P],
                                              probs[:, PROB_AT[q] + t * P:PROB_AT[q] + (t + 1) * P], ident[:, :])
                    mm.then_inc(turned, 1)

            def step(g, s, first, last):
                scores(g, s, first)
                if not (last and s == STEPS - 1):
                    queries(g, s + 1, first)
                if not (first and s == 0):
                    weigh(g, s, last)
                if not (first and s < 5):
                    outputs(g, s, drained=last and s == STEPS - 1)
                p = kv_piece(s)
                if p and not (last and p[1]):
                    keys_values(g + 1 if p[1] else g, p[0], p[2], g * STEPS + s)
                turn(g, s, first)

            for piece in range(PIECES):
                if piece:
                    pe.wait_ge(kv_lo_ok, piece)
                keys_values(0, 0, piece, None)
            queries(0, 0, True)
            steps(pe, step)
            weigh(HK - 1, STEPS, True)
            for x in range(5):
                outputs(HK - 1, STEPS + x, drained=True)

        @block.scalar
        def _(act):
            nc.scalar.preload_act_table(ACT.Exp)

            def high(kind, g, h, start=False):
                raw, hi, _ = views(kind, h)
                if kind == "wu":
                    act.wait_ge(wu_in, 32 * (g + 1))
                    if not start:
                        act.wait_ge(kv_done, 2 * PIECES * g)
                    sem = wu_hi_ok
                elif kind == "wq":
                    act.wait_ge(wq_in, 16 * (g + 1))
                    if not start:
                        act.wait_ge(projected, g * STEPS - HQ + h + 1)
                    sem = wq_hi_ok
                else:
                    act.wait_ge(wo_in, 16 * (g + 1))
                    if not (isinstance(g, int) and g == 0):
                        act.wait_ge(o_done, g * STEPS)
                    sem = wo_hi_ok
                act.activation(hi, raw, ACT.Copy).then_inc(sem, 1)

            def kv_high(count, b, piece):
                act.wait_ge(kv_done, count)
                if piece == 0:
                    act.activation(kT_hi[:, b, :], bank[7][:, :], ACT.Copy).then_inc(kv_hi_ok, 1)
                else:
                    cols = slice((piece - 1) * 2 * D1, piece * 2 * D1)
                    act.activation(v_hi[:, b, cols], bank[7][:, 0:2 * D1], ACT.Copy).then_inc(kv_hi_ok, 1)

            def q_high(n):
                act.wait_ge(projected, n + 1)
                act.activation(qT_hi[:, :], bank[6][:, :], ACT.Copy, scale=SCALE).then_inc(q_hi_ok, 1)

            def c_high(g, s):
                n = g * STEPS + s
                k = (s - 1) // HQ
                b, h = k % 2, (s - 1) % HQ
                act.wait_ge(weighted, n)
                if h == 0 and not (isinstance(g, int) and g == 0):
                    act.wait_ge(o_done, (2 * g + k - 1) * HQ)
                act.activation(cT_hi[:, b, h, :], bank[7][:, :], ACT.Copy).then_inc(c_hi_ok, 1)

            def step(g, s, first, last):
                n = g * STEPS + s
                for x, (bk, q, at) in enumerate(ORDER):
                    act.wait_ge(maxed, QT * n + BANK_MAXED[q])
                    if x == 0 and not (first and s == 0):
                        act.wait_ge(inverted, n)
                        act.wait_ge(turned, 3 * n)
                    act.activation(probs[:, PROB_AT[q]:PROB_AT[q] + (q + 1) * P], bank[bk][:, at:at + (q + 1) * P],
                                   ACT.Exp, bias=negmax[:, q:q + 1], accum_out=den[:, q:q + 1]).then_inc(exped, 1)
                if not (last and s == STEPS - 1):
                    q_high(n + 1)
                if not (first and s == 0):
                    c_high(g, s)
                p = kv_piece(s)
                if p and not (last and p[1]):
                    kv_high(pieces_before(g, s, last) + 1, p[0], p[2])
                for kind, gg, h in split_points(g, s, last):
                    high(kind, gg, h)
                for x, (bk, at, width) in enumerate(T_BANK):
                    act.wait_ge(turned, 3 * n + x + 1)
                    if x == 0 and not (first and s == 0):
                        act.wait_ge(weighted, n)
                    act.activation(pT_hi[:, at:at + width], bank[bk][:, 0:width], ACT.Copy).then_inc(pT_hi_ok, 1)

            high("wu", 0, 0, True)
            for h in range(HQ):
                high("wq", 0, h, True)
            for piece in range(PIECES):
                kv_high(piece + 1, 0, piece)
            q_high(0)
            steps(act, step)
            c_high(HK - 1, STEPS)

        @block.vector
        def _(dve):
            def kv_low(count, b, piece):
                dve.wait_ge(kv_hi_ok, count)
                if piece == 0:
                    dve.tensor_tensor(kT_lo[:, b, :], bank[7][:, :], kT_hi[:, b, :].bitcast(F32), ALU.subtract
                                      ).then_inc(kv_lo_ok, 1)
                else:
                    cols = slice((piece - 1) * 2 * D1, piece * 2 * D1)
                    dve.tensor_tensor(v_lo[:, b, cols], bank[7][:, 0:2 * D1], v_hi[:, b, cols].bitcast(F32),
                                      ALU.subtract).then_inc(kv_lo_ok, 1)

            def q_low(n):
                dve.wait_ge(q_hi_ok, n + 1)
                dve.scalar_tensor_tensor(out=qT_lo[:, :], in0=bank[6][:, :], scalar=SCALE,
                                         in1=qT_hi[:, :].bitcast(F32), op0=ALU.mult, op1=ALU.subtract
                                         ).then_inc(q_lo_ok, 1)

            def c_low(g, s):
                k = (s - 1) // HQ
                b, h = k % 2, (s - 1) % HQ
                dve.wait_ge(c_hi_ok, g * STEPS + s)
                dve.tensor_tensor(cT_lo[:, b, h, :], bank[7][:, :], cT_hi[:, b, h, :].bitcast(F32), ALU.subtract
                                  ).then_inc(c_lo_ok, 1)

            def add_output(g, s):
                k, q = (s - 5) // HQ, (s - 5) % HQ
                tile = k % 2 * QT + q
                dve.wait_ge(o_done, g * STEPS + s - 4)
                dve.tensor_tensor(y1[:, tile, :], bank[6][:, :], y1[:, tile, :], ALU.add).then_inc(o_added, 1)

            def step(g, s, first, last):
                n = g * STEPS + s
                for x, (bk, q, at) in enumerate(ORDER):
                    dve.wait_ge(scored, 3 * n + bk + 1)
                    dve.tensor_reduce(negmax[:, q:q + 1], bank[bk][:, at:at + (q + 1) * P], AX_X, ALU.max,
                                      negate=True).then_inc(maxed, 1)
                if not (last and s == STEPS - 1):
                    q_low(n + 1)
                dve.wait_ge(exped, QT * (n + 1))
                if not (first and s == 0):
                    dve.wait_ge(normed, QT * n)
                dve.reciprocal(rden[:, :], den[:, :]).then_inc(inverted, 1)
                dve.wait_ge(inverted, n + 1)
                for q in (0, 1, 2, 3):
                    tile = probs[:, PROB_AT[q]:PROB_AT[q] + (q + 1) * P]
                    dve.tensor_scalar(tile, tile, rden[:, q:q + 1], None, ALU.mult).then_inc(normed, 1)
                if not (first and s == 0):
                    c_low(g, s)
                if not (first and s < 5):
                    add_output(g, s)
                p = kv_piece(s)
                if p and not (last and p[1]):
                    kv_low(pieces_before(g, s, last) + 1, p[0], p[2])
                for x, (bk, at, width) in enumerate(T_BANK):
                    dve.wait_ge(pT_hi_ok, 3 * n + x + 1)
                    dve.tensor_tensor(pT_lo[:, at:at + width], bank[bk][:, 0:width],
                                      pT_hi[:, at:at + width].bitcast(F32), ALU.subtract).then_inc(pT_lo_ok, 1)

            for piece in range(PIECES):
                kv_low(piece + 1, 0, piece)
            q_low(0)
            steps(dve, step)
            c_low(HK - 1, STEPS)
            for x in range(5):
                add_output(HK - 1, STEPS + x)


def compress(nc, st, sb, sems, bank, a, ident, identr, mask, xT_hi, xT_lo, y1, lat_hi, lat_lo, SUB):
    PAIR = 2 * LAT
    raw = sb(st, "wkv_raw", [P, KC, HK, PAIR])
    hi = sb(st, "wkv_hi", [P, KC, HK, 2, PAIR], F32R)
    lo = sb(st, "wkv_lo", [P, KC, HK, 2, PAIR], F32R)
    maskf = sb(st, "maskf", [P, P])
    (w_in, hi_ok, lo_ok, zeroed, masked, const_ok, done, out_hi, out_lo) = sems(
        st, "K_w_in K_w_hi K_w_lo K_zeroed K_masked K_const K_done K_out_hi K_out_lo")
    with nc.Block() as block:
        @block.sync
        def _(sp):
            sp.dma_start(raw[:, :, :, :], a["WkvT"].rearrange("(c p) (h n) -> p c h n", p=P, h=HK)).then_inc(w_in, 16)

        @block.gpsimd
        def _(pool):
            pool.memset(maskf[:, :], 0.0).then_inc(zeroed, 1)
            pool.memset(y1[:, :, :], 0.0).then_inc(zeroed, 1)
            pool.wait_ge(zeroed, 2)
            pool.affine_select(out=maskf[:, :], in_=maskf[:, :], compare_op=ALU.is_ge, fill=MASKED, base=0,
                               pattern=[[-1, P]], channel_multiplier=1).then_inc(masked, 1)

        def kept(buf, b, hk, rows):
            cols = slice(hk * (S // 8), (hk + 1) * (S // 8))
            return buf[rows, bass.ds(b, 1), :, cols].rearrange("p one c t -> p (one c) t")

        def tokens(bk, i, rows):
            return bk[rows, :].rearrange("p (t c two) -> p two c t", two=2, c=2 * LC)[:, i, :, :]

        @block.scalar
        def _(act):
            nc.scalar.preload_act_table(ACT.Exp)
            act.wait_ge(w_in, 16)
            for i in range(2):
                act.activation(hi[:, :, :, i, :], raw[:, :, :, :], ACT.Copy).then_inc(hi_ok, 1)
            act.activation(identr[:, :], ident[:, :], ACT.Copy).then_inc(const_ok, 1)
            act.wait_ge(masked, 1)
            act.activation(mask[:, :], maskf[:, :], ACT.Copy).then_inc(const_ok, 1)

            def job(b, hk):
                act.wait_ge(done, b * HK + hk + 1)
                for i in range(2):
                    rows = slice(i * PAIR, (i + 1) * PAIR)
                    settle(act)
                    act.activation(kept(lat_hi, b, hk, rows), tokens(bank[hk], i, rows), ACT.Copy).then_inc(out_hi, 1)
            with act.Fori(0, B) as b:
                for hk in range(HK):
                    job(b, hk)

        @block.vector
        def _(dve):
            dve.wait_ge(hi_ok, 2)
            for i in range(2):
                dve.tensor_tensor(lo[:, :, :, i, :], raw[:, :, :, :], hi[:, :, :, i, :].bitcast(F32), ALU.subtract
                                  ).then_inc(lo_ok, 1)
            with dve.Fori(0, B) as b:
                for hk in range(HK):
                    dve.wait_ge(out_hi, 2 * (b * HK + hk) + 2)
                    for i in range(2):
                        rows = slice(i * PAIR, (i + 1) * PAIR)
                        dve.tensor_tensor(kept(lat_lo, b, hk, rows), tokens(bank[hk], i, rows),
                                          kept(lat_hi, b, hk, rows).bitcast(F32), ALU.subtract).then_inc(out_lo, 1)

        @block.tensor
        def _(pe):
            pe.wait_ge(lo_ok, 2)

            def job(b, hk):
                if not (isinstance(b, int) and b == 0):
                    pe.wait_ge(out_lo, 2 * (b * HK + hk - HK) + 2)
                three(pe, bank[hk][:, :], [
                    (hi[:, c, hk, :, :].rearrange("p a n -> p (a n)"), lo[:, c, hk, :, :].rearrange("p a n -> p (a n)"),
                     xT_hi[:, c, b * S:(b + 1) * S], xT_lo[:, c, b * S:(b + 1) * S]) for c in range(KC)]
                ).then_inc(done, 1)
            for b in range(B):
                for hk in range(HK):
                    job(b, hk)


def cores_ffn(nc, st, sb, sems, bank, a, ident, neghalf, y1, x_mid, out):
    NS = R + E
    wb_raw = sb(st, "wb_raw", [P, KC, D])
    wb_hi = sb(st, "wb_hi", [P, KC, D], F32R)
    wb_lo = sb(st, "wb_lo", [P, KC, D], F32R)
    ar_raw = sb(st, "ar_raw", [P, KC, NS])
    ar_hi = sb(st, "ar_hi", [P, KC, NS], F32R)
    ar_lo = sb(st, "ar_lo", [P, KC, NS], F32R)
    cores = sb(st, "cores_T", [R, P])
    b_w = sb(st, "b_w", [R, D])
    cb = sb(st, "cores_b", [P, D])
    bb = sb(st, "b_base", [P, D])
    x = sb(st, "x_last", [P, NT, D])
    xn = sb(st, "xn_last", [P, D])
    tT_hi = [sb(st, f"eT_hi{i}", [P, KC, P], F32R) for i in range(2)]
    tT_lo = [sb(st, f"eT_lo{i}", [P, KC, P], F32R) for i in range(2)]
    y = sb(st, "y_last", [P, D])
    negmax = sb(st, "negmaxE", [P, 1])
    ex = sb(st, "expE", [P, E])
    den = sb(st, "denE", [P, 1])
    rden = sb(st, "rdenE", [P, 1])
    route = sb(st, "route", [P, E])
    z = sb(st, "z", [P, E, R])
    zT = sb(st, "zT", [P, P])
    stats0 = sb(st, "stats_y1", [P, NT, 6])
    mv0 = sb(st, "mv_y1", [P, NT, 2])
    veps0 = sb(st, "veps_y1", [P, NT])
    rstd0 = sb(st, "rstd_y1", [P, NT])
    half0 = sb(st, "neghalf_y1", [P, NT])
    nmr0 = sb(st, "shift_y1", [P, NT])
    stats = sb(st, "statsE", [P, 2, 6])
    mv = sb(st, "mvE", [P, 2, 2])
    veps = sb(st, "vepsE", [P, 2, 1])
    rstd = sb(st, "rstdE", [P, 2, 1])
    (x_in, x_rest_in, nmr_ok, w_in, small_in, wb_hi_ok, wb_lo_ok, ar_hi_ok, ar_lo_ok, cb_done, cb_ok, stat0, aggr0, eps0, half_ok,
     rstd0_ok, applied0, x3_ok, turned, tT_hi_ok, tT_lo_ok, small_done, maxed, exped, inverted, routed, z_ok, z_turned,
     zT_ok, out_done, y_ok, x4_ok, stored) = sems(
        st, "E_x_in E_x_rest_in E_nmr E_w_in E_small_in E_wb_hi E_wb_lo E_ar_hi E_ar_lo E_cb_done E_cb E_stat0 E_aggr0 E_eps0 E_half "
            "E_rstd0 E_applied0 E_x3 E_turned E_tT_hi E_tT_lo E_small_done E_maxed E_exped E_inverted E_routed E_z "
            "E_z_turned E_zT E_out_done E_y E_x4 E_stored")
    stat, aggr, eps_ok, rstd_ok, applied = (sems(st, " ".join(f"E_{n}{k}" for k in (1, 2)))
                                            for n in ("stat", "aggr", "eps", "rstd", "applied"))
    out_v = out.rearrange("(t p) h -> p t h", p=P)

    def tile_of(buf, t):
        return buf[:, t, :] if isinstance(t, int) else buf[:, bass.ds(t, 1), :]

    def quads(b):
        return b[:, :].rearrange("p (c q) -> p c q", c=KC)

    def steps(eng, step):
        for odd in range(2):
            step(odd, odd, True)
        with eng.Fori(1, NT // 2 - 1) as i:
            for odd in range(2):
                step(2 * i + odd, odd, True)
        for odd in range(2):
            step(NT - 2 + odd, odd, False)

    def tile(t, n):
        return isinstance(t, int) and t == n

    with nc.Block() as block:
        @block.sync
        def _(sp):
            mid_v = x_mid.rearrange("(t p) h -> p t h", p=P)
            sp.dma_start(x[:, 0:2, :], mid_v[:, 0:2, :]).then_inc(x_in, 16)
            sp.dma_start(wb_raw[:, :, :], a["WbT"].rearrange("(c p) n -> p c n", p=P)).then_inc(w_in, 16)
            sp.dma_start(ar_raw[:, :, :], a["ArT"].rearrange("(c p) n -> p c n", p=P)).then_inc(small_in, 16)
            sp.dma_start(cores[:, :], a["coresT"]).then_inc(small_in, 16)
            sp.dma_start(b_w[:, :], a["BwT"]).then_inc(small_in, 16)
            sp.dma_start(bb[:, :], a["bb"].rearrange("(a n) -> a n", a=1).to_broadcast([P, D])).then_inc(small_in, 16)
            sp.dma_start(x[:, 2:NT, :], mid_v[:, 2:NT, :]).then_inc(x_rest_in, 16)

            def store(t, odd, ahead):
                sp.wait_ge(x4_ok, t + 1)
                sp.dma_start(tile_of(out_v, t), tile_of(x, t)).then_inc(stored, 16)
            steps(sp, store)
            sp.wait_ge(stored, 16 * NT)

        @block.gpsimd
        def _(pool):
            def power(n, t):
                pool.wait_ge(eps_ok[n], t + 1)
                settle(pool)
                pool.tensor_tensor(rstd[:, n, :], veps[:, n, :], neghalf[:, :], ALU.pow).then_inc(rstd_ok[n], 1)

            pool.memset(half0[:, :], -0.5).then_inc(half_ok, 1)
            pool.wait_ge(half_ok, 1)
            pool.wait_ge(eps0, 1)
            pool.tensor_tensor(rstd0[:, :], veps0[:, :], half0[:, :], ALU.pow).then_inc(rstd0_ok, 1)
            power(0, 0)
            power(0, 1)

            def add(t):
                pool.wait_ge(applied[1], t + 1)
                settle(pool)
                pool.tensor_tensor(tile_of(x, t), tile_of(x, t), y[:, :], ALU.add).then_inc(x4_ok, 1)

            def step(t, odd, ahead):
                if not tile(t, 0):
                    power(1, t - 1)
                if ahead:
                    power(0, t + 2)
                if not tile(t, 0):
                    add(t - 1)
            steps(pool, step)
            power(1, NT - 1)
            add(NT - 1)

        @block.tensor
        def _(pe):
            def turn_x(t, first=False):
                pe.wait_ge(applied[0], t + 1)
                if not first:
                    pe.wait_ge(tT_lo_ok, t)
                for c in range(KC):
                    mm = pe.transpose(bank[1][:, c * P:(c + 1) * P], xn[:, c * P:(c + 1) * P], ident[:, :])
                mm.then_inc(turned, 1)

            pe.wait_ge(small_in, 64)
            pe.matmul(bank[4][:, :], cores[:, :], b_w[:, :], start=True, stop=True).then_inc(cb_done, 1)
            turn_x(0, True)
            pe.wait_ge(ar_lo_ok, 1)
            pe.wait_ge(wb_lo_ok, 1)
            pe.wait_ge(cb_ok, 1)

            def step(t, odd, ahead):
                hi, lo = tT_hi[odd], tT_lo[odd]
                pe.wait_ge(tT_lo_ok, t + 1)
                if not tile(t, 0):
                    pe.wait_ge(z_ok, t)
                three(pe, bank[2][:, 0:NS], [(hi[:, c, :], lo[:, c, :], ar_hi[:, c, :], ar_lo[:, c, :])
                                             for c in range(KC)]).then_inc(small_done, 1)
                if not tile(t, NT - 1):
                    turn_x(t + 1)
                if not tile(t, 0):
                    pe.wait_ge(y_ok, t)
                three(pe, bank[0][:, :], [(hi[:, c, :], lo[:, c, :], wb_hi[:, c, :], wb_lo[:, c, :])
                                          for c in range(KC)], stop=False)
                pe.wait_ge(z_ok, t + 1)
                if not tile(t, 0):
                    pe.wait_ge(zT_ok, t)
                pe.transpose(bank[3][:, 0:P], z[:, :, :].rearrange("p e r -> p (e r)"), ident[:, :]
                             ).then_inc(z_turned, 1)
                pe.wait_ge(zT_ok, t + 1)
                pe.matmul(bank[0][:, :], zT[:, :], cb[:, :], start=False, stop=True).then_inc(out_done, 1)
            steps(pe, step)

        @block.scalar
        def _(act):
            nc.scalar.preload_act_table(ACT.Exp)
            act.wait_ge(small_in, 64)
            act.activation(ar_hi[:, :, :], ar_raw[:, :, :], ACT.Copy).then_inc(ar_hi_ok, 1)
            act.wait_ge(w_in, 16)
            act.activation(wb_hi[:, :, :], wb_raw[:, :, :], ACT.Copy).then_inc(wb_hi_ok, 1)
            act.wait_ge(cb_done, 1)
            act.activation(cb[:, :], bank[4][:, :], ACT.Copy, scale=LORA_SCALE).then_inc(cb_ok, 1)

            act.wait_ge(nmr_ok, 1)
            for t in range(NT):
                act.activation(y1[:, t, :], y1[:, t, :], ACT.Identity, scale=rstd0[:, t:t + 1], bias=nmr0[:, t:t + 1]
                               ).then_inc(applied0, 1)

            def high(t, odd):
                act.wait_ge(turned, t + 1)
                if not (isinstance(t, int) and t < 2):
                    act.wait_ge(out_done, t - 1)
                act.activation(tT_hi[odd][:, :, :], quads(bank[1]), ACT.Copy).then_inc(tT_hi_ok, 1)

            high(0, 0)

            def step(t, odd, ahead):
                act.wait_ge(maxed, t + 1)
                if not tile(t, 0):
                    act.wait_ge(routed, t)
                act.activation(ex[:, :], bank[2][:, R:NS], ACT.Exp, bias=negmax[:, :], accum_out=den[:, :]
                               ).then_inc(exped, 1)
                if not tile(t, NT - 1):
                    high(t + 1, 1 - odd)
                act.wait_ge(z_turned, t + 1)
                if not tile(t, 0):
                    act.wait_ge(out_done, t)
                act.activation(zT[:, :], bank[3][:, 0:P], ACT.Copy).then_inc(zT_ok, 1)
            steps(act, step)

        @block.vector
        def _(dve):
            def statistics(n, t, src, ready, first):
                dve.wait_ge(ready, t + 1)
                if not first:
                    dve.wait_ge(aggr[n], t)
                settle(dve)
                dve.bn_stats(stats[:, n, :], src).then_inc(stat[n], 1)
                dve.wait_ge(stat[n], t + 1)
                if not first:
                    dve.wait_ge(applied[n], t)
                settle(dve)
                dve.bn_aggr(mv[:, n, :], stats[:, n, :]).then_inc(aggr[n], 1)
                dve.wait_ge(aggr[n], t + 1)
                if not first:
                    dve.wait_ge(rstd_ok[n], t)
                dve.tensor_scalar(veps[:, n, :], mv[:, n, 1:2], EPS, None, ALU.add).then_inc(eps_ok[n], 1)

            def front(t, first):
                dve.tensor_tensor(tile_of(x, t), tile_of(x, t), tile_of(y1, t), ALU.add).then_inc(x3_ok, 1)
                statistics(0, t, tile_of(x, t), x3_ok, first)

            def input_norm(t, first):
                dve.wait_ge(rstd_ok[0], t + 1)
                if not first:
                    dve.wait_ge(turned, t)
                dve.tensor_scalar(xn[:, :], tile_of(x, t), mv[:, 0, 0:1], rstd[:, 0, :], ALU.subtract, ALU.mult
                                  ).then_inc(applied[0], 1)

            def low(t, odd):
                dve.wait_ge(tT_hi_ok, t + 1)
                dve.tensor_tensor(tT_lo[odd][:, :, :], quads(bank[1]), tT_hi[odd][:, :, :].bitcast(F32), ALU.subtract
                                  ).then_inc(tT_lo_ok, 1)

            def output(t, first):
                dve.wait_ge(out_done, t + 1)
                if not first:
                    dve.wait_ge(x4_ok, t)
                dve.tensor_tensor(y[:, :], bank[0][:, :], bb[:, :], ALU.add).then_inc(y_ok, 1)
                statistics(1, t, y[:, :], y_ok, first)

            def normalise(t):
                dve.wait_ge(rstd_ok[1], t + 1)
                dve.tensor_scalar(y[:, :], y[:, :], mv[:, 1, 0:1], rstd[:, 1, :], ALU.subtract, ALU.mult
                                  ).then_inc(applied[1], 1)

            for t in range(NT):
                dve.bn_stats(stats0[:, t, :], y1[:, t, :]).then_inc(stat0, 1)
            dve.wait_ge(stat0, NT)
            for t in range(NT):
                dve.bn_aggr(mv0[:, t, :], stats0[:, t, :]).then_inc(aggr0, 1)
            dve.wait_ge(aggr0, NT)
            dve.tensor_scalar(veps0[:, :], mv0[:, :, 1], EPS, None, ALU.add).then_inc(eps0, 1)
            dve.wait_ge(ar_hi_ok, 1)
            dve.tensor_tensor(ar_lo[:, :, :], ar_raw[:, :, :], ar_hi[:, :, :].bitcast(F32), ALU.subtract
                              ).then_inc(ar_lo_ok, 1)
            dve.wait_ge(rstd0_ok, 1)
            dve.scalar_tensor_tensor(out=nmr0[:, :], in0=mv0[:, :, 0], scalar=-1.0, in1=rstd0[:, :], op0=ALU.mult,
                                     op1=ALU.mult).then_inc(nmr_ok, 1)
            dve.wait_ge(x_in, 16)
            dve.wait_ge(applied0, 1)
            front(0, True)
            dve.wait_ge(wb_hi_ok, 1)
            dve.tensor_tensor(wb_lo[:, :, :], wb_raw[:, :, :], wb_hi[:, :, :].bitcast(F32), ALU.subtract
                              ).then_inc(wb_lo_ok, 1)
            input_norm(0, True)
            low(0, 0)
            dve.wait_ge(applied0, NT)
            front(1, False)
            input_norm(1, False)

            def step(t, odd, ahead):
                dve.wait_ge(small_done, t + 1)
                if not tile(t, 0):
                    dve.wait_ge(exped, t)
                dve.tensor_reduce(negmax[:, :], bank[2][:, R:NS], AX_X, ALU.max, negate=True).then_inc(maxed, 1)
                if not tile(t, 0):
                    output(t - 1, tile(t, 1))
                dve.wait_ge(exped, t + 1)
                if not tile(t, 0):
                    dve.wait_ge(routed, t)
                dve.reciprocal(rden[:, :], den[:, :]).then_inc(inverted, 1)
                dve.wait_ge(inverted, t + 1)
                if not tile(t, 0):
                    dve.wait_ge(z_turned, t)
                dve.tensor_scalar(route[:, :], ex[:, :], rden[:, :], None, ALU.mult).then_inc(routed, 1)
                dve.wait_ge(routed, t + 1)
                dve.tensor_tensor(z[:, :, :], route[:, :, None].to_broadcast([P, E, R]),
                                  bank[2][:, None, 0:R].to_broadcast([P, E, R]), ALU.mult).then_inc(z_ok, 1)
                if not tile(t, NT - 1):
                    low(t + 1, 1 - odd)
                if tile(t, 0):
                    dve.wait_ge(x_rest_in, 16)
                if ahead:
                    front(t + 2, False)
                if not tile(t, 0):
                    normalise(t - 1)
                if ahead:
                    input_norm(t + 2, False)

            steps(dve, step)
            output(NT - 1, False)
            normalise(NT - 1)


def kernel(**inputs):
    import numpy as _np
    import concourse.bacc as _bacc
    from concourse import mybir as _mybir
    from concourse.bass_utils import run_bass_kernel_spmd as _run

    g = {n: _np.asarray(v) for n, v in inputs.items()}
    kv = [g[f"L1_attn_W{n}_down"].reshape(HK, LAT, D) for n in "kv"]
    laid = {
        "x": g["L0_attn_x"].reshape(TOK, D),
        "qkvw": g["L0_attn_attn_qkvw"],
        "qkvb": g["L0_attn_attn_qkvb"],
        "qkvb_cols": g["L0_attn_attn_qkvb"].reshape(3 * KC, P).T,
        "ow": g["L0_attn_attn_ow"],
        "ob": g["L0_attn_attn_ob"],
        "gateT": g["L0_ffn_w_gate"].transpose(2, 0, 1),
        "upT": g["L0_ffn_w_up"].transpose(2, 0, 1),
        "downT": g["L0_ffn_w_down"].transpose(2, 0, 1),
        "WqT": g["L1_attn_Wq"].T,
        "WkvT": _np.stack(kv, axis=1).reshape(2 * NLAT, D).T,
        "WkupT": g["L1_attn_Wk_up"].T,
        "WvupT": g["L1_attn_Wv_up"].T,
        "WoT": g["L1_attn_Wo"].T,
        "WbT": g["L1_ffn_W_base"].T,
        "bb": g["L1_ffn_b_base"],
        "ArT": _np.concatenate([g["L1_ffn_A_w"], g["L1_ffn_router_w"]]).T,
        "BwT": g["L1_ffn_B_w"].T,
        "coresT": g["L1_ffn_cores"].reshape(E * R, R).T,
    }
    nc = _bacc.Bacc("TRN2", target_bir_lowering=False, num_devices=1)
    arrays, aps = {}, {}
    for name, v in laid.items():
        v = _np.ascontiguousarray(v)
        arrays[f"in_{name}"] = v
        aps[name] = nc.dram_tensor(f"in_{name}", v.shape, _mybir.dt.from_np(v.dtype), kind="ExternalInput").ap()
    out = nc.dram_tensor("out_0", (TOK, D), F32, kind="ExternalOutput").ap()
    program(nc, aps, out)
    r = _run(nc, [arrays], core_ids=[0])
    return r.results[0]["out_0"].reshape(B, S, D)
```

```python
from contextlib import ExitStack

import concourse.bass as bass
from concourse import mybir

F32 = mybir.dt.float32
F32R = mybir.dt.float32r
ACT = mybir.ActivationFunctionType
ALU = mybir.AluOpType
AX_X = mybir.AxisListType.X

P = 128
B, S, D = 2, 512, 512
TOK = B * S
NT = TOK // P
QT = S // P
KC = D // P
EPS = 1e-5

H0, HD0 = 32, 16
HPC = P // HD0

O8 = 8
DI = D // O8
DH = 1366 // O8
MAIN = P
REM = DH - MAIN
NHC = O8 + O8 // 2

GATE_AT, UP_AT, DOWN_AT, REM_AT, ABOVE_AT = (n * DH * O8 if n < 3 else 2 * DH * O8 + (n - 2) * D for n in range(5))
TERN = ABOVE_AT + DH * O8

H1, HK, D1 = 32, 8, 128
LAT = D1 // 4
REP = H1 // HK
NLAT = HK * LAT
LC = NLAT // P

R, E = 16, 8
LORA_SCALE = 32.0 / 16.0

TRIPLES = [(1, 2, 3), (1, 4, 5), (1, 7, 6), (2, 4, 6), (2, 5, 7), (3, 4, 7), (3, 6, 5)]
MASKED = -1.0e30


def ternary_parts(tern):
    return [tern[:, at:at + O8 * n].rearrange("p (j n) -> p j n", j=O8)
            for at, n in ((GATE_AT, DH), (UP_AT, DH), (DOWN_AT, DI), (REM_AT, DI))]


def octonion_table():
    s = {(0, 0, 0): 1}
    for i in range(1, 8):
        s[0, i, i] = 1
        s[i, 0, i] = 1
        s[i, i, 0] = -1
    for a, b, c in TRIPLES:
        for x, y, z in ((a, b, c), (b, c, a), (c, a, b)):
            s[x, y, z] = 1
            s[y, x, z] = -1
    return {(i, k): (j, v) for (j, i, k), v in s.items()}


OCT = octonion_table()


def settle(eng):
    eng.nop(nofuse=True)


def program(nc, a, out):
    with ExitStack() as whole:
        bank = [whole.enter_context(nc.psum_tensor(f"bank{i}", [P, 512], F32)) for i in range(8)]

        held = {}

        def sems(stack, names):
            got = [nc.alloc_semaphore(n) for n in names.split()]
            if id(stack) not in held:
                held[id(stack)] = []
                stack.callback(clear, id(stack))
            held[id(stack)] += got
            return got

        def clear(stage):
            nc.clear_and_free_semaphores(held.pop(stage))
            nc.all_engine_barrier()

        def sb(stack, name, shape, dt=F32):
            return stack.enter_context(nc.sbuf_tensor(name, shape, dt))

        ident = sb(whole, "ident", [P, P])
        neghalf = sb(whole, "neghalf", [P, 1])
        xT_hi = sb(whole, "xT_hi", [P, KC, TOK], F32R)
        xT_lo = sb(whole, "xT_lo", [P, KC, TOK], F32R)
        x_mid = nc.dram_tensor("x_mid", (TOK, D), F32, kind="Internal").ap()

        with ExitStack() as first:
            tern = sb(first, "ternary", [P, TERN])
            scales = sb(first, "tern_scales", [P, 3])
            ctx0 = sb(first, "ctx0", [P, NT, D])
            with ExitStack() as st:
                qk = sb(st, "qk", [P, 4, KC, TOK], F32R)
                v0 = sb(st, "v0", [P, NT, D])
                with ExitStack() as tmp:
                    project_qkv(nc, tmp, sb, sems, bank, a, ident, neghalf, tern, ctx0, xT_hi, xT_lo, qk, v0)
                with ExitStack() as tmp:
                    attention0(nc, tmp, sb, sems, bank, a, ident, qk, v0, ctx0, xT_hi, xT_lo, tern, scales)
            with ExitStack() as tmp:
                x_res = sb(tmp, "x_res", [P, NT, D])
                middle(nc, tmp, sb, sems, bank, a, ident, neghalf, x_res, ctx0, xT_hi, xT_lo, x_mid, tern, scales)
        y1 = sb(whole, "y1", [P, NT, D])
        with ExitStack() as tmp:
            attention1(nc, tmp, sb, sems, bank, a, ident, xT_hi, xT_lo, y1)
        with ExitStack() as tmp:
            cores_ffn(nc, tmp, sb, sems, bank, a, ident, neghalf, y1, x_mid, out)


def project_qkv(nc, st, sb, sems, bank, a, ident, neghalf, spare, ctx0, xT_hi, xT_lo, qk, v0):
    x_res = v0
    scale = HD0 ** -0.5
    w_hi = sb(st, "wqkv_hi", [P, KC, 3 * D], F32R)
    w_lo = sb(st, "wqkv_lo", [P, KC, 3 * D], F32R)
    raw = [ctx0[:, 0:KC, :], ctx0[:, KC:2 * KC, :], spare[:, 0:KC * D].rearrange("p (c n) -> p c n", c=KC)]
    bias = sb(st, "qkv_bias", [P, 3 * KC])
    bias_q = sb(st, "q_bias_scaled", [P, KC])
    v_bias = sb(st, "v_bias", [P, D])
    stats = sb(st, "statsA", [P, NT, 6])
    mv = sb(st, "mvA", [P, NT, 2])
    veps = sb(st, "vepsA", [P, NT])
    rstd = sb(st, "rstdA", [P, NT])
    half = sb(st, "neghalfA", [P, QT])
    xn = spare[:, KC * D:(KC + 2) * D].rearrange("p (t n) -> p t n", t=2)
    (x_in, w_in, small_in, ident_ok, zeroed, stat, aggr, eps_added, rstd_ok, normed, turned, xT_hi_ok, xT_lo_ok,
     w_hi_ok, w_lo_ok, wk_lo_ok, x2_in, qbias_ok, proj, out_hi, out_lo, v_out) = sems(
        st, "A_x_in A_w_in A_small_in A_ident A_zeroed A_stat A_aggr A_eps A_rstd A_normed A_turned A_xT_hi A_xT_lo "
            "A_w_hi A_w_lo A_wk_lo A_x2_in A_qbias A_proj A_out_hi A_out_lo A_v_out")
    x_v = a["x"].rearrange("(t p) h -> p t h", p=P)
    w_v = a["qkvw"].rearrange("(c p) n -> p c n", p=P)
    w_sems = [w_in] + sems(st, "A_wk_in A_wv_in")
    NM = 2 * KC

    with nc.Block() as block:
        @block.sync
        def _(sp):
            for b, loaded in enumerate((x_in, x2_in)):
                sp.dma_start(x_res[:, b * QT:(b + 1) * QT, :], x_v[:, b * QT:(b + 1) * QT, :]).then_inc(loaded, 16)
            for n in range(3):
                sp.dma_start(raw[n], w_v[:, :, n * D:(n + 1) * D]).then_inc(w_sems[n], 16)
            sp.dma_start(bias[:, :], a["qkvb_cols"]).then_inc(small_in, 16)
            sp.dma_start(v_bias[:, :], a["qkvb"][2 * D:3 * D].rearrange("(a n) -> a n", a=1).to_broadcast([P, D])
                         ).then_inc(small_in, 16)

        @block.gpsimd
        def _(pool):
            pool.memset(neghalf[:, :], -0.5).then_inc(zeroed, 1)
            pool.memset(half[:, :], -0.5).then_inc(zeroed, 1)
            pool.memset(ident[:, :], 0.0).then_inc(zeroed, 1)
            pool.wait_ge(zeroed, 3)
            pool.affine_select(out=ident[:, :], in_=ident[:, :], compare_op=ALU.not_equal, fill=1.0, base=0,
                               pattern=[[-1, P]], channel_multiplier=1).then_inc(ident_ok, 1)
            for b in range(B):
                of = slice(b * QT, (b + 1) * QT)
                pool.wait_ge(eps_added, b + 1)
                pool.tensor_tensor(rstd[:, of], veps[:, of], half[:, :], ALU.pow).then_inc(rstd_ok, 1)
            for n in (1, 2):
                pool.wait_ge(w_hi_ok, n + 1)
                pool.tensor_tensor(w_lo[:, :, n * D:(n + 1) * D], raw[n], w_hi[:, :, n * D:(n + 1) * D].bitcast(F32),
                                   ALU.subtract).then_inc(wk_lo_ok, 1)

        @block.scalar
        def _(act):
            nc.scalar.preload_act_table(ACT.Exp)

            def high_weights(n):
                act.wait_ge(w_sems[n], 16)
                act.activation(w_hi[:, :, n * D:(n + 1) * D], raw[n], ACT.Copy,
                               scale=scale if n == 0 else 1.0).then_inc(w_hi_ok, 1)

            def high(t):
                act.wait_ge(turned, t + 1)
                act.activation(xT_hi[:, :, t * P:(t + 1) * P], bank[t % 2][:, :].rearrange("p (c q) -> p c q", c=KC),
                               ACT.Copy).then_inc(xT_hi_ok, 1)

            def out(b, m):
                j = b * NM + m
                act.wait_ge(proj, j + 1)
                dst = qk[:, 1 if m < KC else 2, m % KC, b * S:(b + 1) * S]
                act.activation(dst, bank[2 + j % 4][:, :], ACT.Identity,
                               bias=bias_q[:, m:m + 1] if m < KC else bias[:, m:m + 1]).then_inc(out_hi, 1)

            for t in range(QT):
                if t:
                    high_weights(t - 1)
                high(t)
            act.wait_ge(small_in, 32)
            act.activation(bias_q[:, :], bias[:, 0:KC], ACT.Copy, scale=scale).then_inc(qbias_ok, 1)
            act.wait_ge(qbias_ok, 1)
            for b in range(B):
                for m in range(NM):
                    out(b, m)
                    if b == 0 and m < QT:
                        high(QT + m)

        @block.vector
        def _(dve):
            for b, loaded in enumerate((x_in, x2_in)):
                of = slice(b * QT, (b + 1) * QT)
                dve.wait_ge(loaded, 16)
                for t in range(b * QT, (b + 1) * QT):
                    dve.bn_stats(stats[:, t, :], x_res[:, t, :]).then_inc(stat, 1)
                dve.wait_ge(stat, (b + 1) * QT)
                for t in range(b * QT, (b + 1) * QT):
                    dve.bn_aggr(mv[:, t, :], stats[:, t, :]).then_inc(aggr, 1)
                dve.wait_ge(aggr, (b + 1) * QT)
                dve.tensor_scalar(veps[:, of], mv[:, of, 1], EPS, None, ALU.add).then_inc(eps_added, 1)

            def normalise(t):
                dve.wait_ge(rstd_ok, t // QT + 1)
                if t >= 2:
                    dve.wait_ge(turned, t - 1)
                dve.tensor_scalar(xn[:, t % 2, :], x_res[:, t, :], mv[:, t, 0:1], rstd[:, t:t + 1], ALU.subtract,
                                  ALU.mult).then_inc(normed, 1)

            def low(t):
                dve.wait_ge(xT_hi_ok, t + 1)
                dve.tensor_tensor(xT_lo[:, :, t * P:(t + 1) * P], bank[t % 2][:, :].rearrange("p (c q) -> p c q", c=KC),
                                  xT_hi[:, :, t * P:(t + 1) * P].bitcast(F32), ALU.subtract).then_inc(xT_lo_ok, 1)

            def out(b, m):
                j = b * NM + m
                dve.wait_ge(out_hi, j + 1)
                hi, lo = (1, 0) if m < KC else (2, 3)
                cols = slice(b * S, (b + 1) * S)
                dve.scalar_tensor_tensor(out=qk[:, lo, m % KC, cols], in0=bank[2 + j % 4][:, :],
                                         scalar=bias_q[:, m:m + 1] if m < KC else bias[:, m:m + 1],
                                         in1=qk[:, hi, m % KC, cols].bitcast(F32), op0=ALU.add,
                                         op1=ALU.subtract).then_inc(out_lo, 1)

            normalise(0)
            for t in range(QT):
                normalise(t + 1)
                low(t)
            dve.wait_ge(w_hi_ok, 1)
            for m in range(KC):
                of = slice(m * P, (m + 1) * P)
                dve.scalar_tensor_tensor(out=w_lo[:, :, of], in0=raw[0][:, :, of], scalar=scale,
                                         in1=w_hi[:, :, of].bitcast(F32), op0=ALU.mult, op1=ALU.subtract
                                         ).then_inc(w_lo_ok, 1)
            normalise(QT + 1)
            dve.wait_ge(qbias_ok, 1)
            for b in range(B):
                for m in range(NM):
                    out(b, m)
                    if b == 0 and m < QT:
                        low(QT + m)
                        if m + 2 < QT:
                            normalise(QT + m + 2)
            dve.wait_ge(normed, NT)
            for t in range(NT):
                dve.wait_ge(proj, B * NM + t + 1)
                dve.tensor_tensor(v0[:, t, :], bank[6 + t % 2][:, :], v_bias[:, :], ALU.add).then_inc(v_out, 1)

        @block.tensor
        def _(pe):
            pe.wait_ge(ident_ok, 1)

            def turn(t):
                pe.wait_ge(normed, t + 1)
                if t >= 2:
                    pe.wait_ge(xT_lo_ok, t - 1)
                for c in range(KC):
                    mm = pe.transpose(bank[t % 2][:, c * P:(c + 1) * P], xn[:, t % 2, c * P:(c + 1) * P], ident[:, :])
                mm.then_inc(turned, 1)

            for t in range(QT):
                turn(t)
            for b in range(B):
                pe.wait_ge(xT_lo_ok, (b + 1) * QT)
                for m in range(NM):
                    j = b * NM + m
                    if b == 0 and m < KC:
                        pe.wait_ge(w_lo_ok, m + 1)
                    if b == 0 and m == KC:
                        pe.wait_ge(wk_lo_ok, 1)
                    if j >= 4:
                        pe.wait_ge(out_lo, j - 3)
                    three(pe, bank[2 + j % 4][:, :], [
                        (w_hi[:, c, m * P:(m + 1) * P], w_lo[:, c, m * P:(m + 1) * P],
                         xT_hi[:, c, b * S:(b + 1) * S], xT_lo[:, c, b * S:(b + 1) * S]) for c in range(KC)]
                    ).then_inc(proj, 1)
                    if b == 0 and m < QT:
                        turn(QT + m)
            pe.wait_ge(wk_lo_ok, 2)
            for t in range(NT):
                if t >= 2:
                    pe.wait_ge(v_out, t - 1)
                three(pe, bank[6 + t % 2][:, :], [
                    (xT_hi[:, c, t * P:(t + 1) * P], xT_lo[:, c, t * P:(t + 1) * P],
                     w_hi[:, c, 2 * D:3 * D], w_lo[:, c, 2 * D:3 * D]) for c in range(KC)]).then_inc(proj, 1)


def three(pe, dst, chunks, start=True, stop=True):
    steps = [p for s_hi, s_lo, m_hi, m_lo in chunks for p in ((s_hi, m_hi), (s_hi, m_lo), (s_lo, m_hi))]
    for n, (s, m) in enumerate(steps):
        mm = pe.matmul(dst, s, m, start=(start and n == 0), stop=(stop and n == len(steps) - 1))
    return mm


def attention0(nc, st, sb, sems, bank, a, ident, qk, v0, ctx0, xT_hi, xT_lo, tern, scales):
    parts = ternary_parts(tern)
    N_W = O8 * DH * DI
    SCALE_OF = (0, 1, 2, 2)
    ones_sq = sb(st, "ones_sq", [P, P])
    sums = sb(st, "sums", [P, 4])
    means = sb(st, "means", [P, 4])
    half = sb(st, "half", [P, 2, 3])
    t_cleared, w_in, summed, totalled, means_ok, down_ok, half_ok, scales_ok, above_ok, minus_ok = sems(
        st, "T_cleared T_w_in T_summed T_totalled T_means T_down_mean T_half T_scales T_above T_minus")
    G = 4
    NB = QT
    TURNS = 4
    U = TURNS * NB * G
    LOOPS = B * H0 // (G * TURNS)
    BEHIND = 7
    FULL = 96
    ROWS = FULL + 2
    VW = 32
    both = [sb(st, f"stack{u}", [P, G, 2, S], F32R)[:, :, :, :] for u in range(TURNS // 2)]
    both += [buf[:, :, :].rearrange("p c (n s) -> p c n s", n=2) for buf in (xT_hi, xT_lo)]
    stack = [[buf[0:ROWS, h, :, :] for h in range(G)] for buf in both]
    zero_one = sb(st, "zero_one", [P, 2])
    vst = [sb(st, f"values{i}", [P, QT, G, VW]) for i in range(2)]
    pT = [sb(st, f"pT{i}", [P, G, S]) for i in range(2)]
    cT = sb(st, "ctxT", [P, S])
    mrow = sb(st, "max_rows", [2 * G, S], F32R)
    negmax = [sb(st, f"negmax{i}", [P, QT, G]) for i in range(2)]
    msplit = sb(st, "max_split", [P, QT, G, 2], F32R)
    rden = sb(st, "rden", [P, QT, G])
    (cleared, zeros_ok, ones_ok, scored, maxed, mhi_ok, msplit_ok, m_turned, mrow_ok, max_in, v_ok,
     rescored, exped, weighted, cT_ok, c_turned, inverted, normed) = sems(
        st, "B_cleared B_zeros B_ones B_scored B_maxed B_mhi B_msplit B_m_turned B_mrow "
            "B_max_in B_v B_rescored B_exped B_weighted B_cT B_c_turned B_inverted B_normed")
    stk = [sems(st, " ".join(f"B_stack{u}_{h}" for h in range(G))) for u in range(TURNS)]

    def positive(n):
        return not isinstance(n, int) or n > 0

    def iterations(eng, blocks):
        for q in range(TURNS * NB):
            blocks(0, q, False)
        with eng.Fori(1, LOOPS) as i:
            for q in range(TURNS * NB):
                blocks(i, q, False)
        for q in range(BEHIND + 1):
            blocks(LOOPS, q, True)

    def earlier(i, q, n):
        if q >= n:
            return i, q - n
        return None if isinstance(i, int) and i == 0 else (i - 1, q - n + TURNS * NB)

    def columns(i, u):
        at = i * (TURNS // B * G * HD0) + u // B * G * HD0
        return slice(at, at + G * HD0) if isinstance(i, int) else bass.ds(at, G * HD0)

    with nc.Block() as block:
        @block.sync
        def _(sp):
            def load(i, u):
                chunk = slice(i, i + 1) if isinstance(i, int) else bass.ds(i, 1)
                if isinstance(i, int) and i == 0:
                    sp.wait_ge(zeros_ok, 2 * u + 2)
                else:
                    sp.wait_ge(rescored, i * U - U + (u + 1) * NB * G)
                    settle(sp)
                for h in range(G):
                    rows = slice((u // B * G + h) * HD0, (u // B * G + h + 1) * HD0)
                    cols = slice(u % B * S, (u % B + 1) * S)
                    for slot, pair in enumerate((slice(1, 3, 1), slice(1, 4, 2), slice(0, 3, 2))):
                        sp.dma_start(stack[u][h][slot * HD0:(slot + 1) * HD0, :, :].bitcast(F32),
                                     qk[rows, pair, chunk, cols].rearrange("p n c s -> p (n c) s").bitcast(F32)
                                     ).then_inc(stk[u][h], 16)

            def maxima(i, u):
                sp.wait_ge(mrow_ok, i * TURNS + u + 1)
                for h in range(G):
                    sp.dma_start(stack[u][h][FULL:ROWS, 0, :].bitcast(F32),
                                 mrow[2 * h:2 * h + 2, :].bitcast(F32)).then_inc(max_in, 16)

            def load_weights():
                sp.wait_ge(t_cleared, 3)
                for rows in (slice(0, DI), slice(DI, P)):
                    sp.dma_start(parts[0][rows, :, :], a["gateT"]).then_inc(w_in, 16)
                    sp.dma_start(parts[1][rows, :, :], a["upT"]).then_inc(w_in, 16)
                sp.dma_start(parts[2][:, :, :], a["downT"][0:MAIN]).then_inc(w_in, 16)
                for rows in (slice(0, REM), slice(DI, DI + REM)):
                    sp.dma_start(parts[3][rows, :, :], a["downT"][MAIN:DH]).then_inc(w_in, 16)

            for u in range(TURNS - 1):
                load(0, u)
            for u in range(TURNS):
                maxima(0, u)
                load(1 if u else 0, (u - 1) % TURNS)
                if u == 1:
                    load_weights()
            with sp.Fori(1, LOOPS - 1) as i:
                for u in range(TURNS):
                    maxima(i, u)
                    load(i + 1 if u else i, (u - 1) % TURNS)
            for u in range(TURNS):
                maxima(LOOPS - 1, u)
                if u == 0:
                    load(LOOPS - 1, TURNS - 1)
            sp.wait_ge(max_in, 16 * G * TURNS * LOOPS)

        @block.gpsimd
        def _(pool):
            pool.memset(zero_one[:, 0:1], 0.0).then_inc(cleared, 1)
            pool.memset(zero_one[:, 1:2], 1.0).then_inc(cleared, 1)
            for i in range(2):
                pool.memset(vst[i][:, :, :, :], 0.0).then_inc(cleared, 1)
            pool.wait_ge(cleared, 4)
            for i in range(2):
                pool.memset(vst[i][:, :, :, HD0:HD0 + 1], 1.0).then_inc(cleared, 1)

            pool.memset(parts[3][:, :, :], 0.0).then_inc(t_cleared, 1)
            pool.memset(sums[:, :], 0.0).then_inc(t_cleared, 1)
            pool.memset(ones_sq[:, :], 1.0).then_inc(t_cleared, 1)

            def values(i, u):
                t = i * TURNS + u
                if positive(NB * (t - 1)):
                    pool.wait_ge(weighted, NB * (t - 1))
                    settle(pool)
                b = u % B
                src = v0[:, b * QT:(b + 1) * QT, columns(i, u)].rearrange("p t (h d) -> p t h d", h=G)
                pool.tensor_copy(vst[u % 2][:, :, :, 0:HD0], src).then_inc(v_ok, 1)

            for u in range(TURNS):
                values(0, u)
            with pool.Fori(1, LOOPS) as i:
                for u in range(TURNS):
                    values(i, u)

        @block.tensor
        def _(pe):
            def first_scores(i, q, h):
                n, u = i * U + q * G + h, q // NB
                if q % NB == 0:
                    pe.wait_ge(stk[u][h], (i + 1) * 16 * 3)
                if positive(n - 3):
                    pe.wait_ge(maxed, n - 3)
                at = q % NB * P
                pe.matmul(bank[h][:, :], stack[u][h][0:FULL, 0, at:at + P], stack[u][h][0:FULL, 1, :],
                          start=True, stop=True).then_inc(scored, 1)

            def second_scores(i, q, h):
                n, u = i * U + q * G + h, q // NB
                if q % NB == 0 and h == 0:
                    if isinstance(i, int) and i == 0 and u == 0:
                        pe.wait_ge(ones_ok, TURNS)
                    pe.wait_ge(max_in, (i * TURNS + u + 1) * 16 * G)
                if positive(n - 1):
                    pe.wait_ge(exped, n - 1)
                at = q % NB * P
                pe.matmul(bank[4 + h % 2][:, :], stack[u][h][:, 1, at:at + P], stack[u][h][:, 0, :],
                          start=True, stop=True).then_inc(rescored, 1)

            def context(i, q):
                u, t = q // NB, q % NB
                pe.wait_ge(exped, i * U + (q + 1) * G)
                if t == 0:
                    pe.wait_ge(v_ok, i * TURNS + u + 1)
                    if positive(i * TURNS + u):
                        pe.wait_ge(cT_ok, i * TURNS + u)
                for h in range(G):
                    mm = pe.matmul(bank[6][h * VW:(h + 1) * VW, :], vst[u % 2][:, t, h, :], pT[q % 2][:, h, :],
                                   start=(t == 0), stop=(t == NB - 1))
                mm.then_inc(weighted, 1)

            def turn_maxima(i, u):
                t = i * TURNS + u
                pe.wait_ge(msplit_ok, t + 1)
                if positive(t - 2):
                    pe.wait_ge(normed, t - 2)
                if positive(t):
                    pe.wait_ge(mrow_ok, t)
                for q in range(QT):
                    mm = pe.transpose(bank[7][0:2 * G, q * P:(q + 1) * P],
                                      msplit[:, q, :, :].bitcast(F32).rearrange("p h n -> p (h n)"), ident[:, :])
                mm.then_inc(m_turned, 1)

            def turn_context(i, u, ends):
                t = i * TURNS + u
                pe.wait_ge(cT_ok, t + 1)
                if ends:
                    pe.wait_ge(mrow_ok, LOOPS * TURNS)
                else:
                    pe.wait_ge(mrow_ok, t + 3)
                if positive(t):
                    pe.wait_ge(normed, t)
                for q in range(QT):
                    mm = pe.transpose(bank[7][:, q * P:(q + 1) * P], cT[:, q * P:(q + 1) * P], ident[:, :])
                mm.then_inc(c_turned, 1)

            def blocks(i, q, follow):
                again, weigh = earlier(i, q, BEHIND), earlier(i, q, BEHIND + 1)

                def first(h):
                    if not follow:
                        first_scores(i, q, h)

                def second(h):
                    if again and not (follow and q >= BEHIND):
                        second_scores(*again, h)
                first(0)
                second(0)
                first(1)
                second(1)
                if weigh:
                    context(*weigh)
                second(2)
                first(2)
                first(3)
                second(3)
                done = earlier(i, q, NB)
                if q % NB == 0 and done and not (follow and q >= NB):
                    turn_maxima(done[0], done[1] // NB)
                done = earlier(i, q, BEHIND + 2 + NB)
                if q % NB == 1 and done:
                    turn_context(done[0], done[1] // NB, follow)
                if follow and q == 3:
                    pe.wait_ge(summed, 4)
                    pe.matmul(bank[0][:, 0:4], ones_sq[:, :], sums[:, :], start=True, stop=True).then_inc(totalled, 1)
            iterations(pe, blocks)
            turn_context(LOOPS - 1, TURNS - 1, True)

        @block.vector
        def _(dve):
            for u in range(TURNS):
                if u:
                    dve.wait_ge(zeros_ok, 2 * u)
                dve.memset(both[u][0:FULL, :, 1, :].bitcast(F32), 0.0).then_inc(zeros_ok, 1)
            dve.wait_ge(cleared, 2)
            for u in range(TURNS):
                dve.tensor_copy(both[u][FULL:ROWS, :, 1, :], zero_one[FULL:ROWS, None, 1:2].to_broadcast([2, G, S])
                                ).then_inc(ones_ok, 1)

            def maximum(i, q, h):
                u = q // NB
                dve.wait_ge(scored, i * U + q * G + h + 1)
                if q % NB == 0 and h == 0 and positive(i * TURNS + u - 1):
                    dve.wait_ge(msplit_ok, i * TURNS + u - 1)
                dve.tensor_reduce(negmax[u % 2][:, q % NB, h:h + 1], bank[h][:, :], AX_X, ALU.max, negate=True
                                  ).then_inc(maxed, 1)

            def split_maxima(i, u):
                t = i * TURNS + u
                dve.wait_ge(maxed, (t + 1) * NB * G)
                if positive(t):
                    dve.wait_ge(m_turned, t)
                dve.tensor_copy(msplit[:, :, :, 0], negmax[u % 2][:, :, :]).then_inc(mhi_ok, 1)
                dve.wait_ge(mhi_ok, t + 1)
                dve.tensor_tensor(msplit[:, :, :, 1], negmax[u % 2][:, :, :], msplit[:, :, :, 0].bitcast(F32),
                                  ALU.subtract).then_inc(msplit_ok, 1)

            def normalise(i, u):
                t, b = i * TURNS + u, u % B
                dve.wait_ge(c_turned, t + 1)
                if positive(t):
                    dve.wait_ge(normed, t)
                heads = bank[7][:, :].rearrange("p (q h v) -> p q h v", q=QT, h=G)
                dve.reciprocal(rden[:, :, :], heads[:, :, :, HD0]).then_inc(inverted, 1)
                dve.wait_ge(inverted, t + 1)
                dst = ctx0[:, b * QT:(b + 1) * QT, columns(i, u)].rearrange("p q (h d) -> p q h d", h=G)
                settle(dve)
                dve.tensor_tensor(dst, heads[:, :, :, 0:HD0],
                                  rden[:, :, :, None].to_broadcast([P, QT, G, HD0]), ALU.mult).then_inc(normed, 1)

            def magnitudes():
                dve.wait_ge(t_cleared, 3)
                dve.wait_ge(w_in, 7 * 16)
                for n, rows in enumerate((P, P, P, DI)):
                    dve.tensor_reduce(sums[0:rows, n:n + 1], parts[n][0:rows, :, :], mybir.AxisListType.XY, ALU.add,
                                      apply_absolute_value=True).then_inc(summed, 1)

            def set_scales():
                dve.wait_ge(totalled, 1)
                dve.tensor_scalar(means[:, 0:2], bank[0][:, 0:2], 0.5 / N_W, None, ALU.mult).then_inc(means_ok, 1)
                dve.tensor_scalar(means[:, 2:4], bank[0][:, 2:4], 1.0 / N_W, None, ALU.mult).then_inc(means_ok, 1)
                dve.wait_ge(means_ok, 2)
                dve.tensor_tensor(means[:, 2:3], means[:, 2:3], means[:, 3:4], ALU.add).then_inc(down_ok, 1)
                dve.wait_ge(down_ok, 1)
                dve.tensor_scalar(half[:, 0, :], means[:, 0:3], 0.5, None, ALU.mult).then_inc(half_ok, 1)
                dve.tensor_scalar(half[:, 1, :], means[:, 0:3], -0.5, None, ALU.mult).then_inc(half_ok, 1)
                dve.tensor_copy(scales[:, 0:2], means[:, 0:2]).then_inc(scales_ok, 1)
                dve.tensor_tensor(scales[:, 2:3], means[:, 1:2], means[:, 2:3], ALU.mult).then_inc(scales_ok, 1)
                dve.wait_ge(half_ok, 2)

            def ternary(n):
                s, part = SCALE_OF[n], parts[n]
                width = part.shape[2]
                above = tern[:, ABOVE_AT:ABOVE_AT + O8 * width].rearrange("p (j n) -> p j n", j=O8)
                if n:
                    dve.wait_ge(minus_ok, n)
                dve.tensor_scalar(above, part, half[:, 0, s:s + 1], None, ALU.is_gt).then_inc(above_ok, 1)
                dve.wait_ge(above_ok, n + 1)
                dve.scalar_tensor_tensor(out=part, in0=part, scalar=half[:, 1, s:s + 1], in1=above, op0=ALU.is_lt,
                                         op1=ALU.subtract).then_inc(minus_ok, 1)

            def blocks(i, q, follow):
                if follow and q == 0:
                    magnitudes()
                elif follow and q == 3:
                    set_scales()
                    ternary(0)
                    ternary(1)
                elif follow and q == BEHIND:
                    ternary(2)
                    ternary(3)
                if not follow:
                    for h in range(G):
                        maximum(i, q, h)
                    if q % NB == NB - 1:
                        split_maxima(i, q // NB)
                done = earlier(i, q, BEHIND + 2 + NB)
                if q % NB == 1 and done:
                    normalise(done[0], done[1] // NB)
            iterations(dve, blocks)
            normalise(LOOPS - 1, TURNS - 1)

        @block.scalar
        def _(act):
            nc.scalar.preload_act_table(ACT.Exp)
            act.wait_ge(cleared, 2)
            for u in range(TURNS):
                if u:
                    act.wait_ge(zeros_ok, 2 * u)
                act.activation(both[u][0:FULL, :, 0, :], zero_one[0:FULL, None, 0:1].to_broadcast([FULL, G, S]),
                               ACT.Copy).then_inc(zeros_ok, 1)

            def exponent(i, q, h):
                act.wait_ge(rescored, i * U + q * G + h + 1)
                if h == 0 and positive(i * (U // G) + q - 1):
                    act.wait_ge(weighted, i * (U // G) + q - 1)
                act.activation(pT[q % 2][:, h, :], bank[4 + h % 2][:, :], ACT.Exp).then_inc(exped, 1)

            def maxima_row(i, u):
                t = i * TURNS + u
                act.wait_ge(m_turned, t + 1)
                if positive(t):
                    act.wait_ge(max_in, 16 * G * t)
                act.activation(mrow[:, :], bank[7][0:2 * G, :], ACT.Copy).then_inc(mrow_ok, 1)

            def context_rows(i, u):
                t = i * TURNS + u
                act.wait_ge(weighted, NB * (t + 1))
                if positive(t):
                    act.wait_ge(c_turned, t)
                act.activation(cT[:, :], bank[6][:, :], ACT.Copy).then_inc(cT_ok, 1)

            def blocks(i, q, follow):
                again = earlier(i, q, BEHIND)
                exps = again and not (follow and q >= BEHIND)
                for h in range(G):
                    if exps:
                        exponent(*again, h)
                done = earlier(i, q, BEHIND + NB)
                if q % NB == 3 and done:
                    context_rows(done[0], done[1] // NB)
                done = earlier(i, q, NB)
                if q % NB == 0 and done and not (follow and q >= NB):
                    maxima_row(done[0], done[1] // NB)
            iterations(act, blocks)




def middle(nc, st, sb, sems, bank, a, ident, neghalf, x_res, ctx0, xT_hi, xT_lo, x_mid, tern,
           scales):
    ow_hi = sb(st, "ow_hi", [P, KC, D], F32R)
    ow_lo = sb(st, "ow_lo", [P, KC, D], F32R)
    m_gate = sb(st, "m_gate", [P, KC, O8, DH], F32R)
    m_up = sb(st, "m_up", [P, KC, O8, DH], F32R)
    m_down = sb(st, "m_down", [P, NHC, D], F32R)
    ob = sb(st, "ob", [P, D])
    ow_raw = sb(st, "ow_raw", [P, KC, D])
    gate, up, down_main, down_rem = ternary_parts(tern)
    HALVES = (slice(0, DI), slice(DI, P))
    into = {"gate": [], "up": [], "down": [], "rem": []}
    for i in range(O8):
        rows = HALVES[i % 2]
        for k in range(O8):
            j, sign = OCT[i, k]
            into["gate"].append((m_gate[rows, i // 2, k, :], gate[rows, j, :], -float(sign)))
            into["up"].append((m_up[rows, i // 2, k, :], up[rows, j, :], -float(sign)))
            cols = slice(k * DI, (k + 1) * DI)
            into["down"].append((m_down[:, i, cols], down_main[:, j, :], -float(sign)))
            into["rem"].append((m_down[rows, O8 + i // 2, cols], down_rem[rows, j, :], -float(sign)))
    DOWN_BY_POOL, REM_BY_ACT = 30, 28
    by_pool = into["down"][:DOWN_BY_POOL]
    by_act = into["up"] + into["rem"][:REM_BY_ACT]
    by_dve = into["gate"] + into["down"][DOWN_BY_POOL:] + into["rem"][REM_BY_ACT:]

    cs = sb(st, "ctx_tile", [P, D])
    cT_hi = sb(st, "cT_hi", [P, KC, P], F32R)
    cT_lo = sb(st, "cT_lo", [P, KC, P], F32R)
    tT_hi = sb(st, "tT_hi", [P, KC, P], F32R)
    tT_lo = sb(st, "tT_lo", [P, KC, P], F32R)
    gact = tern[:, 0:3 * D].rearrange("p (g n) -> p g n", g=3)
    h = tern[:, 3 * D:3 * D + NHC * P]
    y2 = tern[:, 3 * D + NHC * P:4 * D + NHC * P]
    y, xn1 = (tern[:, n:n + D] for n in (ABOVE_AT, ABOVE_AT + D))
    hT_hi = sb(st, "hT_hi", [P, NHC, P], F32R)
    hT_lo = sb(st, "hT_lo", [P, NHC, P], F32R)
    xn2 = sb(st, "xn2", [P, D])
    stats = sb(st, "statsC", [P, 4, 6])
    mv = sb(st, "mvC", [P, 4, 2])
    veps = sb(st, "vepsC", [P, 4, 1])
    rstd = sb(st, "rstdC", [P, 4, 1])
    (zeroed, cs_ok, c_turned, cT_hi_ok, cT_lo_ok, o_done, y_ok, x_turned, tT_hi_ok, tT_lo_ok, gu_done, act_ok, h_ok,
     h_turned, hT_hi_ok, hT_lo_ok, d_done, y2_ok, x2_turned, xT_hi_ok, xT_lo_ok, x1_ok, x2_ok,
     stored, ow_in, x_in, ow_hi_ok, ow_lo_ok, gate_ok, up_ok, pool_copied, act_copied,
     dve_copied) = sems(
        st, "C_zeroed C_cs C_c_turned C_cT_hi C_cT_lo C_o_done C_y C_x_turned C_tT_hi C_tT_lo C_gu_done C_act C_h "
            "C_h_turned C_hT_hi C_hT_lo C_d_done C_y2 C_x2_turned C_xT_hi C_xT_lo C_x1 C_x2 C_stored "
            "C_ow_in C_x_in C_ow_hi C_ow_lo C_gate C_up C_pool_copied C_act_copied C_dve_copied")
    stat, aggr, eps_ok, rstd_ok, applied = (sems(st, " ".join(f"C_{n}{k}" for k in range(4)))
                                            for n in ("stat", "aggr", "eps", "rstd", "applied"))
    h_main = h[:, 0:O8 * P].rearrange("p (i d) -> p i d", i=O8)
    h_rem = h[:, O8 * P:].rearrange("p (i d) -> p i d", i=O8)
    mid_v = x_mid.rearrange("(t p) h -> p t h", p=P)
    HI = O8 // 2

    def tile_of(buf, t):
        return buf[:, t, :] if isinstance(t, int) else buf[:, bass.ds(t, 1), :]

    def columns_of(buf, t):
        return buf[:, :, t * P:(t + 1) * P] if isinstance(t, int) else buf[:, :, bass.ds(t * P, P)]

    def steps(eng, before, step):
        before()
        step(0, True, False)
        with eng.Fori(1, NT - 1) as t:
            step(t, False, False)
        step(NT - 1, False, True)

    def quads(b):
        return b[:, :].rearrange("p (c q) -> p c q", c=KC)

    with nc.Block() as block:
        @block.sync
        def _(sp):
            sp.dma_start(ow_raw[:, :, :], a["ow"].rearrange("(c p) n -> p c n", p=P)).then_inc(ow_in, 16)
            sp.dma_start(ob[:, :], a["ob"].rearrange("(a n) -> a n", a=1).to_broadcast([P, D])).then_inc(x_in, 16)
            sp.dma_start(x_res[:, :, :], a["x"].rearrange("(t p) h -> p t h", p=P)).then_inc(x_in, 16)

            def store(t, first, last):
                sp.wait_ge(x2_ok, t + 1)
                sp.dma_start(tile_of(mid_v, t), tile_of(x_res, t)).then_inc(stored, 16)
            steps(sp, lambda: None, store)
            sp.wait_ge(stored, 16 * NT)

        @block.gpsimd
        def _(pool):
            def power(n, t):
                pool.wait_ge(eps_ok[n], t + 1)
                settle(pool)
                pool.tensor_tensor(rstd[:, n, :], veps[:, n, :], neghalf[:, :], ALU.pow).then_inc(rstd_ok[n], 1)

            def stage(t):
                if not (isinstance(t, int) and t == 0):
                    pool.wait_ge(c_turned, t)
                    settle(pool)
                pool.tensor_copy(cs[:, :], tile_of(ctx0, t)).then_inc(cs_ok, 1)

            def copies(n, m):
                for dst, src, sign in by_pool[n:m]:
                    last = pool.tensor_scalar(dst, src, sign, None, ALU.mult)
                return last

            def before():
                stage(0)
                copies(0, 14)
                power(0, 0)
                copies(14, 20)
                power(1, 0)
                stage(1)
                copies(20, DOWN_BY_POOL).then_inc(pool_copied, 1)
                pool.wait_ge(pool_copied, 1)
                pool.wait_ge(act_copied, 1)
                pool.wait_ge(dve_copied, 1)
                pool.memset(h[:, O8 * P:], 0.0).then_inc(zeroed, 1)

            def step(t, first, last, ahead=True):
                if not first:
                    power(2, t - 1)
                    power(3, t - 1)
                if ahead:
                    stage(t + 2)
                if not last:
                    power(0, t + 1)
                    power(1, t + 1)

            before()
            step(0, True, False)
            with pool.Fori(1, NT - 2) as t:
                step(t, False, False)
            step(NT - 2, False, False, False)
            step(NT - 1, False, True, False)
            power(2, NT - 1)
            power(3, NT - 1)

        @block.tensor
        def _(pe):
            def turn(src, dst, sem):
                for c in range(KC):
                    mm = pe.transpose(dst[:, c * P:(c + 1) * P], src[:, c * P:(c + 1) * P], ident[:, :])
                mm.then_inc(sem, 1)

            def turn_ctx(t, first):
                pe.wait_ge(cs_ok, t + 1)
                turn(cs, bank[0], c_turned)

            def project(t, first):
                pe.wait_ge(cT_lo_ok, t + 1)
                if not first:
                    pe.wait_ge(y2_ok, t - 1)
                three(pe, bank[1][:, :], [(cT_hi[:, c, :], cT_lo[:, c, :], ow_hi[:, c, :], ow_lo[:, c, :])
                                          for c in range(KC)]).then_inc(o_done, 1)

            def turn_x1(t):
                pe.wait_ge(applied[1], t + 1)
                turn(xn1, bank[0], x_turned)

            def turn_x2(t):
                pe.wait_ge(applied[3], t + 1)
                turn(xn2, bank[0], x2_turned)

            def before():
                turn_ctx(0, True)
                pe.wait_ge(ow_lo_ok, 1)
                project(0, True)
                turn_x1(0)
                pe.wait_ge(gate_ok, 1)
                pe.wait_ge(up_ok, 1)

            def gate_up(t, g, first):
                if not first:
                    pe.wait_ge(hT_lo_ok, 3 * t - 2 + g)
                    pe.wait_ge(h_ok, 3 * t - 2 + g)
                for m, b in ((m_gate, bank[2 + g]), (m_up, bank[5 + g])):
                    dst = b[:, :] if g < 2 else b[:, 0:O8 * REM]
                    mats = [m[:, c, g * HI:(g + 1) * HI, 0:MAIN] if g < 2 else m[:, c, :, MAIN:DH]
                            for c in range(KC)]
                    for n, (s, c) in enumerate((s, c) for c in range(KC) for s in (tT_hi, tT_lo)):
                        mm = pe.matmul(dst, s[:, c, :], mats[c], start=(n == 0), stop=(n == 2 * KC - 1))
                mm.then_inc(gu_done, 1)

            def turn_hidden(t, g):
                pe.wait_ge(h_ok, 3 * t + g + 1)
                for c in range(KC):
                    n = g * KC + c
                    mm = pe.transpose(bank[2 + g][:, c * P:(c + 1) * P], h[:, n * P:(n + 1) * P], ident[:, :])
                mm.then_inc(h_turned, 1)

            def down(t, g):
                pe.wait_ge(hT_lo_ok, 3 * t + g + 1)
                for n in range(g * KC, (g + 1) * KC):
                    for s in (hT_hi, hT_lo):
                        mm = pe.matmul(bank[1][:, :], s[:, n, :], m_down[:, n, :], start=(n == 0 and s is hT_hi),
                                       stop=(n == NHC - 1 and s is hT_lo))
                if g == 2:
                    mm.then_inc(d_done, 1)

            def step(t, first, last):
                pe.wait_ge(tT_lo_ok, t + 1)
                if not last:
                    turn_ctx(t + 1, first)
                gate_up(t, 0, first)
                if not last:
                    project(t + 1, first)
                gate_up(t, 1, first)
                if not first:
                    turn_x2(t - 1)
                turn_hidden(t, 0)
                gate_up(t, 2, first)
                turn_hidden(t, 1)
                if not last:
                    pe.wait_ge(y_ok, t + 2)
                    if not first:
                        pe.wait_ge(xT_lo_ok, t)
                    turn_x1(t + 1)
                else:
                    pe.wait_ge(y2_ok, t)
                if first:
                    for copied in (pool_copied, act_copied, dve_copied):
                        pe.wait_ge(copied, 1)
                down(t, 0)
                turn_hidden(t, 2)
                down(t, 1)
                down(t, 2)

            steps(pe, before, step)
            turn_x2(NT - 1)

        @block.scalar
        def _(act):
            nc.scalar.preload_act_table(ACT.Silu)

            def split_ctx(t, first):
                act.wait_ge(c_turned, t + 1)
                if not first:
                    act.wait_ge(o_done, t)
                act.activation(cT_hi[:, :, :], quads(bank[0]), ACT.Copy).then_inc(cT_hi_ok, 1)

            def split_x1(t, first):
                act.wait_ge(x_turned, t + 1)
                if not first:
                    act.wait_ge(gu_done, 3 * t)
                act.activation(tT_hi[:, :, :], quads(bank[0]), ACT.Copy).then_inc(tT_hi_ok, 1)

            def split_x2(t):
                act.wait_ge(x2_turned, t + 1)
                settle(act)
                act.activation(columns_of(xT_hi, t), quads(bank[0]), ACT.Copy).then_inc(xT_hi_ok, 1)

            def copies(n, m):
                for dst, src, sign in by_act[n:m]:
                    last = act.activation(dst, src, ACT.Copy, scale=sign)
                return last

            def before():
                copies(0, 16)
                act.wait_ge(ow_in, 16)
                act.activation(ow_hi[:, :, :], ow_raw[:, :, :], ACT.Copy).then_inc(ow_hi_ok, 1)
                split_ctx(0, True)
                copies(16, len(into["up"])).then_inc(up_ok, 1)
                split_x1(0, True)
                copies(64, len(by_act)).then_inc(act_copied, 1)

            def gate(t, g, first):
                n = D if g < 2 else O8 * REM
                act.wait_ge(gu_done, 3 * t + g + 1)
                if not first:
                    act.wait_ge(h_ok, 3 * t - 2 + g)
                act.activation(gact[:, g, 0:n], bank[2 + g][:, 0:n], ACT.Silu, scale=scales[:, 0:1]
                               ).then_inc(act_ok, 1)

            def split_hidden(t, g, first):
                act.wait_ge(h_turned, 3 * t + g + 1)
                if not first:
                    act.wait_ge(d_done, t)
                act.activation(hT_hi[:, g * KC:(g + 1) * KC, :], quads(bank[2 + g]), ACT.Copy).then_inc(hT_hi_ok, 1)

            def step(t, first, last):
                if not last:
                    split_ctx(t + 1, False)
                gate(t, 0, first)
                gate(t, 1, first)
                if not first:
                    split_x2(t - 1)
                split_hidden(t, 0, first)
                gate(t, 2, first)
                split_hidden(t, 1, first)
                if not last:
                    split_x1(t + 1, False)
                split_hidden(t, 2, first)
                act.wait_ge(d_done, t + 1)
                if not first:
                    act.wait_ge(applied[2], t)
                act.activation(y2[:, :], bank[1][:, :], ACT.Copy, scale=scales[:, 2:3]).then_inc(y2_ok, 1)

            steps(act, before, step)
            split_x2(NT - 1)

        @block.vector
        def _(dve):
            def statistics(n, t, src, ready, first):
                dve.wait_ge(ready, t + 1)
                if not first:
                    dve.wait_ge(aggr[n], t)
                    settle(dve)
                dve.bn_stats(stats[:, n, :], src).then_inc(stat[n], 1)
                dve.wait_ge(stat[n], t + 1)
                if not first:
                    dve.wait_ge(applied[n], t)
                settle(dve)
                dve.bn_aggr(mv[:, n, :], stats[:, n, :]).then_inc(aggr[n], 1)
                dve.wait_ge(aggr[n], t + 1)
                if not first:
                    dve.wait_ge(rstd_ok[n], t)
                dve.tensor_scalar(veps[:, n, :], mv[:, n, 1:2], EPS, None, ALU.add).then_inc(eps_ok[n], 1)

            def apply(n, t, dst, src):
                dve.wait_ge(rstd_ok[n], t + 1)
                dve.tensor_scalar(dst, src, mv[:, n, 0:1], rstd[:, n, :], ALU.subtract, ALU.mult
                                  ).then_inc(applied[n], 1)

            def attention_out(t, first):
                dve.wait_ge(o_done, t + 1)
                if not first:
                    dve.wait_ge(x1_ok, t)
                dve.tensor_tensor(y[:, :], bank[1][:, :], ob[:, :], ALU.add).then_inc(y_ok, 1)
                statistics(0, t, y[:, :], y_ok, first)

            def first_residual(t, first):
                apply(0, t, y[:, :], y[:, :])
                dve.wait_ge(applied[0], t + 1)
                dve.tensor_tensor(tile_of(x_res, t), tile_of(x_res, t), y[:, :], ALU.add).then_inc(x1_ok, 1)
                statistics(1, t, tile_of(x_res, t), x1_ok, first)

            def first_norm(t, first):
                if not first:
                    dve.wait_ge(x_turned, t)
                apply(1, t, xn1[:, :], tile_of(x_res, t))

            def low(sem_hi, t, dst, hi, src, sem):
                dve.wait_ge(sem_hi, t + 1)
                dve.tensor_tensor(dst, src, hi.bitcast(F32), ALU.subtract).then_inc(sem, 1)

            def second_residual(t, first):
                statistics(2, t, y2[:, :], y2_ok, first)
                apply(2, t, y2[:, :], y2[:, :])

                dve.wait_ge(applied[2], t + 1)
                dve.tensor_tensor(tile_of(x_res, t), tile_of(x_res, t), y2[:, :], ALU.add).then_inc(x2_ok, 1)
                statistics(3, t, tile_of(x_res, t), x2_ok, first)

            def second_norm(t, first):
                if not first:
                    dve.wait_ge(x2_turned, t)
                apply(3, t, xn2[:, :], tile_of(x_res, t))

            def copies(n, m):
                for dst, src, sign in by_dve[n:m]:
                    last = dve.tensor_scalar(dst, src, sign, None, ALU.mult)
                return last

            def before():
                copies(0, 34)
                dve.wait_ge(ow_hi_ok, 1)
                dve.tensor_tensor(ow_lo[:, :, :], ow_raw[:, :, :], ow_hi[:, :, :].bitcast(F32), ALU.subtract
                                  ).then_inc(ow_lo_ok, 1)
                low(cT_hi_ok, 0, cT_lo[:, :, :], cT_hi[:, :, :], quads(bank[0]), cT_lo_ok)
                copies(34, len(into["gate"])).then_inc(gate_ok, 1)
                dve.wait_ge(x_in, 32)
                attention_out(0, True)
                copies(64, 74)
                first_residual(0, True)
                copies(74, 84)
                first_norm(0, True)
                copies(84, 100)
                low(tT_hi_ok, 0, tT_lo[:, :, :], tT_hi[:, :, :], quads(bank[0]), tT_lo_ok)
                copies(100, len(by_dve)).then_inc(dve_copied, 1)
                dve.wait_ge(zeroed, 1)

            def hidden(t, g, first):
                dve.wait_ge(act_ok, 3 * t + g + 1)
                if not first:
                    dve.wait_ge(h_turned, 3 * t - 2 + g)
                if g < 2:
                    dve.tensor_tensor(h_main[:, g * HI:(g + 1) * HI, :],
                                      gact[:, g, :].rearrange("p (i d) -> p i d", i=HI),
                                      bank[5 + g][:, :].rearrange("p (i d) -> p i d", i=HI), ALU.mult
                                      ).then_inc(h_ok, 1)
                else:
                    dve.tensor_tensor(h_rem[:, :, 0:REM],
                                      gact[:, g, 0:O8 * REM].rearrange("p (i d) -> p i d", i=O8),
                                      bank[5 + g][:, 0:O8 * REM].rearrange("p (i d) -> p i d", i=O8), ALU.mult
                                      ).then_inc(h_ok, 1)

            def low_hidden(t, g):
                low(hT_hi_ok, 3 * t + g, hT_lo[:, g * KC:(g + 1) * KC, :], hT_hi[:, g * KC:(g + 1) * KC, :],
                    quads(bank[2 + g]), hT_lo_ok)

            def step(t, first, last):
                if not last:
                    low(cT_hi_ok, t + 1, cT_lo[:, :, :], cT_hi[:, :, :], quads(bank[0]), cT_lo_ok)
                if not first:
                    second_residual(t - 1, isinstance(t, int) and t == 1)
                hidden(t, 0, first)
                if not first:
                    second_norm(t - 1, isinstance(t, int) and t == 1)
                if not last:
                    attention_out(t + 1, False)
                    first_residual(t + 1, False)
                hidden(t, 1, first)
                if not first:
                    low(xT_hi_ok, t - 1, columns_of(xT_lo, t - 1), columns_of(xT_hi, t - 1), quads(bank[0]), xT_lo_ok)
                if not last:
                    first_norm(t + 1, False)
                low_hidden(t, 0)
                hidden(t, 2, first)
                low_hidden(t, 1)
                if not last:
                    low(tT_hi_ok, t + 1, tT_lo[:, :, :], tT_hi[:, :, :], quads(bank[0]), tT_lo_ok)
                low_hidden(t, 2)

            before()
            step(0, True, False)
            step(1, False, False)
            with dve.Fori(2, NT - 1) as t:
                step(t, False, False)
            step(NT - 1, False, True)
            second_residual(NT - 1, False)
            second_norm(NT - 1, False)
            low(xT_hi_ok, NT - 1, columns_of(xT_lo, NT - 1), columns_of(xT_hi, NT - 1), quads(bank[0]), xT_lo_ok)



def attention1(nc, st, sb, sems, bank, a, ident, xT_hi, xT_lo, y1):
    SUB = NLAT // (2 * LAT)
    lat_hi = sb(st, "lat_hi", [P, B, 2 * LC, S], F32R)
    lat_lo = sb(st, "lat_lo", [P, B, 2 * LC, S], F32R)
    mask = sb(st, "mask", [P, P])
    HQ = REP
    W = HQ * D1
    STEPS = B * HQ
    wq_raw = sb(st, "wq_raw", [P, KC, W])
    wq_hi = sb(st, "wq_hi", [P, KC, W], F32R)
    wq_lo = sb(st, "wq_lo", [P, KC, W], F32R)
    wo_raw = sb(st, "wo_raw", [P, HQ, D])
    wo_hi = sb(st, "wo_hi", [P, HQ, D], F32R)
    wo_lo = sb(st, "wo_lo", [P, HQ, D], F32R)
    wu_raw = sb(st, "wu_raw", [P, 2, LC, D1])
    wu_hi = sb(st, "wu_hi", [P, 2, LC, D1], F32R)
    wu_lo = sb(st, "wu_lo", [P, 2, LC, D1], F32R)
    (wq_in, wo_in, wu_in, wq_hi_ok, wq_lo_ok, wo_hi_ok, wo_lo_ok, wu_hi_ok, wu_lo_ok, kv_done, projected,
     o_done) = sems(
        st, "D_wq_in D_wo_in D_wu_in D_wq_hi D_wq_lo D_wo_hi D_wo_lo D_wu_hi D_wu_lo D_kv_done D_projected D_o_done")
    PIECES = 3

    def load(sp, g):
        def part(name, axis, n):
            v = a[name].rearrange("(c p) n -> p c n" if axis == 2 else "(h d) n -> d h n", **{"p" if axis == 2 else "d": P})
            at = slice(g * n, (g + 1) * n) if isinstance(g, int) else bass.ds(g * n, n)
            return v[:, :, at] if axis == 2 else v[:, at, :]

        again = not (isinstance(g, int) and g == 0)
        if again:
            sp.wait_ge(wu_lo_ok, g)
            settle(sp)
        sp.dma_start(wu_raw[:, 0, :, :], part("WkupT", 2, D1)).then_inc(wu_in, 16)
        sp.dma_start(wu_raw[:, 1, :, :], part("WvupT", 2, D1)).then_inc(wu_in, 16)
        if again:
            sp.wait_ge(wq_lo_ok, g * HQ)
            settle(sp)
        sp.dma_start(wq_raw[:, :, :], part("WqT", 2, W)).then_inc(wq_in, 16)
        if again:
            sp.wait_ge(wo_lo_ok, g)
            settle(sp)
        sp.dma_start(wo_raw[:, :, :], part("WoT", 1, HQ)).then_inc(wo_in, 16)

    def views(kind, h):
        if kind == "wu":
            return wu_raw[:, :, :, :], wu_hi[:, :, :, :], wu_lo[:, :, :, :]
        if kind == "wo":
            return wo_raw[:, :, :], wo_hi[:, :, :], wo_lo[:, :, :]
        c = slice(h * D1, (h + 1) * D1)
        return wq_raw[:, :, c], wq_hi[:, :, c], wq_lo[:, :, c]

    def high(act, kind, g, h, start=False):
        raw, hi, _ = views(kind, h)
        if kind == "wu":
            act.wait_ge(wu_in, 32 * (g + 1))
            if not start:
                act.wait_ge(kv_done, 2 * PIECES * g)
            sem = wu_hi_ok
        elif kind == "wq":
            act.wait_ge(wq_in, 16 * (g + 1))
            if not start:
                act.wait_ge(projected, g * STEPS - HQ + h + 1)
            sem = wq_hi_ok
        else:
            act.wait_ge(wo_in, 16 * (g + 1))
            if not (isinstance(g, int) and g == 0):
                act.wait_ge(o_done, g * STEPS)
            sem = wo_hi_ok
        act.activation(hi, raw, ACT.Copy).then_inc(sem, 1)

    def low(pool, kind, g, h):
        raw, hi, lo = views(kind, h)
        done, sem = {"wu": (wu_hi_ok, wu_lo_ok), "wq": (wq_hi_ok, wq_lo_ok), "wo": (wo_hi_ok, wo_lo_ok)}[kind]
        pool.wait_ge(done, (g * HQ + h if kind == "wq" else g) + 1)
        pool.tensor_tensor(lo, raw, hi.bitcast(F32), ALU.subtract).then_inc(sem, 1)

    with ExitStack() as tmp:
        compress(nc, tmp, sb, sems, bank, a, ident, mask, xT_hi, xT_lo, y1, lat_hi, lat_lo, SUB, HQ, load,
                 high, low)

    kT_hi = sb(st, "kT_hi", [P, B, S], F32R)
    kT_lo = sb(st, "kT_lo", [P, B, S], F32R)
    v_hi = sb(st, "v_hi", [P, B, S], F32R)
    v_lo = sb(st, "v_lo", [P, B, S], F32R)
    qT_hi = sb(st, "qT_hi", [P, S], F32R)
    qT_lo = sb(st, "qT_lo", [P, S], F32R)
    probs = sb(st, "probs_b", [P, 10 * P])
    pT_hi = sb(st, "pT_hi", [P, 10 * P], F32R)
    pT_lo = sb(st, "pT_lo", [P, 10 * P], F32R)
    cT_hi = sb(st, "c1T_hi", [P, B, HQ, S], F32R)
    cT_lo = sb(st, "c1T_lo", [P, B, HQ, S], F32R)
    negmax = sb(st, "negmax_b", [P, QT])
    den = sb(st, "den_b", [P, QT])
    rden = sb(st, "rden_b", [P, QT])
    (kv_hi_ok, kv_lo_ok, q_hi_ok, q_lo_ok, scored, masked, maxed, exped, inverted, normed, turned, pT_hi_ok, pT_lo_ok,
     weighted, c_hi_ok, c_lo_ok, o_added) = sems(
        st, "D_kv_hi D_kv_lo D_q_hi D_q_lo D_scored D_masked D_maxed D_exped D_inverted D_normed D_turned D_pT_hi D_pT_lo "
            "D_weighted D_c_hi D_c_lo D_o_added")
    SCALE = D1 ** -0.5
    SCORES = ((0, ((3, 0),)), (1, ((2, 0), (0, 3 * P))), (2, ((1, 0),)))
    ORDER = [(b, q, at) for b, tiles in SCORES for q, at in tiles]
    BANK_MAXED = {3: 1, 2: 3, 0: 3, 1: 4}
    PROB_AT = [0, P, 3 * P, 6 * P]
    TURNS = ((3, ((0, 0),)), (4, ((1, 0), (3, 3 * P))), (5, ((2, 0),)))
    T_AT = {0: 0, 1: 4 * P, 3: 7 * P, 2: 8 * P}
    T_BANK = ((3, 0, 4 * P), (4, 4 * P, 4 * P), (5, 8 * P, 2 * P))

    def out_bank(s, drained):
        return bank[0] if drained and s >= STEPS and (s - STEPS) % 2 == 0 else bank[6]

    def kv_piece(s):
        if 1 <= s <= 3:
            return 1, False, s - 1
        if 5 <= s <= 7:
            return 0, True, s - 5
        return None

    def steps(eng, step):
        for s in range(STEPS):
            step(0, s, True, False)
        with eng.Fori(1, HK - 1) as g:
            for s in range(STEPS):
                step(g, s, False, False)
        for s in range(STEPS):
            step(HK - 1, s, False, True)

    def pieces_before(g, s, last):
        return 2 * PIECES * g + PIECES + max(0, min(s, 4) - 1) + (0 if last else max(0, s - 5))

    with nc.Block() as block:
        @block.sync
        def _(sp):
            with sp.Fori(1, HK) as g:
                load(sp, g)
            sp.wait_ge(wo_in, 16 * HK)

        def split_points(g, s, last):
            out = []
            if s == 4 and not last:
                out.append(("wu", g + 1, 0))
            if s >= 4 and not last:
                out.append(("wq", g + 1, s - 4))
            if s == 4:
                out.append(("wo", g, 0))
            return out

        @block.gpsimd
        def _(pool):
            steps(pool, lambda g, s, first, last: [low(pool, *x) for x in split_points(g, s, last)])

        @block.tensor
        def _(pe):
            def scores(g, s, first):
                b = s // HQ
                n = g * STEPS + s
                pe.wait_ge(q_lo_ok, n + 1)
                pe.wait_ge(kv_lo_ok, 2 * PIECES * g + (PIECES if b == 0 else 2 * PIECES))
                for bk, tiles in SCORES:
                    if not (first and s == 0):
                        pe.wait_ge(exped, QT * (n - 1) + {0: 1, 1: 3, 2: 4}[bk])
                    for q, at in tiles:
                        dst = bank[bk][:, at:at + (q + 1) * P]
                        cols = slice(q * P, (q + 1) * P)
                        keys = slice(0, (q + 1) * P)
                        pe.matmul(dst, qT_hi[:, cols], kT_hi[:, b, keys], start=True, stop=False)
                        pe.matmul(dst, qT_hi[:, cols], kT_lo[:, b, keys], start=False, stop=False)
                        mm = pe.matmul(dst, qT_lo[:, cols], kT_hi[:, b, keys], start=False, stop=True)
                    mm.then_inc(scored, 1)

            def queries(g, s, first):
                busy = not (first and s <= 6)
                if s == STEPS:
                    g, s = g + 1, 0
                b, h = s // HQ, s % HQ
                n = g * STEPS + s
                pe.wait_ge(wq_lo_ok, g * HQ + h + 1)
                if busy:
                    pe.wait_ge(o_added, n - 6)
                three(pe, bank[6][:, :], [
                    (wq_hi[:, c, h * D1:(h + 1) * D1], wq_lo[:, c, h * D1:(h + 1) * D1],
                     xT_hi[:, c, b * S:(b + 1) * S], xT_lo[:, c, b * S:(b + 1) * S]) for c in range(KC)]
                ).then_inc(projected, 1)

            def weigh(g, s, last):
                n = g * STEPS + s
                b = (s - 1) % STEPS // HQ
                pe.wait_ge(pT_lo_ok, 3 * n)
                pe.wait_ge(kv_lo_ok, pieces_before(g, s, last))
                hh, hl, lh = (v_hi, pT_hi), (v_hi, pT_lo), (v_lo, pT_hi)
                passes = [(0, hh)] + [(t, x) for t in range(1, QT) for x in (hh, hl, lh)] + [(0, hl), (0, lh)]
                for n, (t, (v, p)) in enumerate(passes):
                    mm = pe.matmul(bank[7][:, t * P:S], v[:, b, t * D1:(t + 1) * D1],
                                   p[:, T_AT[t]:T_AT[t] + (QT - t) * P], start=(n == 0),
                                   stop=(n == len(passes) - 1), skip_group_check=True)
                mm.then_inc(weighted, 1)

            def outputs(g, s, drained=False):
                m = g * STEPS + s - 5
                blk_steps = 2 * g * HQ
                k = (s - 5) // HQ
                q = (s - 5) % HQ
                b = k % 2
                pe.wait_ge(c_lo_ok, blk_steps + (k + 1) * HQ)
                pe.wait_ge(wo_lo_ok, g + (1 if k >= 0 else 0))
                if not drained:
                    pe.wait_ge(q_lo_ok, g * STEPS + s + 2)
                else:
                    pe.wait_ge(o_added, m if s == STEPS - 1 else m - 1)
                three(pe, out_bank(s, drained)[:, :], [
                    (cT_hi[:, b, h, q * P:(q + 1) * P], cT_lo[:, b, h, q * P:(q + 1) * P],
                     wo_hi[:, h, :], wo_lo[:, h, :]) for h in range(HQ)]).then_inc(o_done, 1)

            def keys_values(g, b, piece, before_step):
                pe.wait_ge(wu_lo_ok, g + 1)
                if before_step is not None:
                    pe.wait_ge(c_lo_ok, before_step)
                if piece == 0:
                    mm = three(pe, bank[7][:, :], [
                        (wu_hi[:, 0, c, :], wu_lo[:, 0, c, :], lat_hi[:, b, c, :], lat_lo[:, b, c, :])
                        for c in range(LC)])
                else:
                    for i in range(2):
                        t = 2 * (piece - 1) + i
                        mm = three(pe, bank[7][:, i * D1:(i + 1) * D1], [
                            (lat_hi[:, b, LC + c, t * P:(t + 1) * P], lat_lo[:, b, LC + c, t * P:(t + 1) * P],
                             wu_hi[:, 1, c, :], wu_lo[:, 1, c, :]) for c in range(LC)])
                mm.then_inc(kv_done, 1)

            def turn(g, s, first):
                n = g * STEPS + s
                pe.wait_ge(normed, QT * (n + 1))
                if not (first and s == 0):
                    pe.wait_ge(pT_lo_ok, 3 * n)
                for bk, tiles in TURNS:
                    for t, at in tiles:
                        for q in range(t, QT):
                            col = at + (q - t) * P
                            mm = pe.transpose(bank[bk][:, col:col + P],
                                              probs[:, PROB_AT[q] + t * P:PROB_AT[q] + (t + 1) * P], ident[:, :])
                    mm.then_inc(turned, 1)

            def step(g, s, first, last):
                scores(g, s, first)
                if not (last and s == STEPS - 1):
                    queries(g, s + 1, first)
                if not (first and s == 0):
                    weigh(g, s, last)
                if not (first and s < 5):
                    outputs(g, s, drained=last and s == STEPS - 1)
                p = kv_piece(s)
                if p and not (last and p[1]):
                    keys_values(g + 1 if p[1] else g, p[0], p[2], g * STEPS + s)
                turn(g, s, first)

            for piece in range(PIECES):
                if piece:
                    pe.wait_ge(kv_lo_ok, piece)
                keys_values(0, 0, piece, None)
            queries(0, 0, True)
            steps(pe, step)
            weigh(HK - 1, STEPS, True)
            for x in range(5):
                outputs(HK - 1, STEPS + x, drained=True)

        @block.scalar
        def _(act):
            nc.scalar.preload_act_table(ACT.Exp)

            def kv_high(count, b, piece):
                act.wait_ge(kv_done, count)
                if piece == 0:
                    act.activation(kT_hi[:, b, :], bank[7][:, :], ACT.Copy).then_inc(kv_hi_ok, 1)
                else:
                    cols = slice((piece - 1) * 2 * D1, piece * 2 * D1)
                    act.activation(v_hi[:, b, cols], bank[7][:, 0:2 * D1], ACT.Copy).then_inc(kv_hi_ok, 1)

            def q_high(n):
                act.wait_ge(projected, n + 1)
                act.activation(qT_hi[:, :], bank[6][:, :], ACT.Copy, scale=SCALE).then_inc(q_hi_ok, 1)

            def c_high(g, s):
                n = g * STEPS + s
                k = (s - 1) // HQ
                b, h = k % 2, (s - 1) % HQ
                act.wait_ge(weighted, n)
                if h == 0 and not (isinstance(g, int) and g == 0):
                    act.wait_ge(o_done, (2 * g + k - 1) * HQ)
                act.activation(cT_hi[:, b, h, :], bank[7][:, :], ACT.Copy).then_inc(c_hi_ok, 1)

            def step(g, s, first, last):
                n = g * STEPS + s
                for x, (bk, q, at) in enumerate(ORDER):
                    act.wait_ge(maxed, QT * n + BANK_MAXED[q])
                    if x == 0 and not (first and s == 0):
                        act.wait_ge(inverted, n)
                        act.wait_ge(turned, 3 * n)
                    if x == QT - 2 and not (last and s == STEPS - 1):
                        q_high(n + 1)
                    act.activation(probs[:, PROB_AT[q]:PROB_AT[q] + (q + 1) * P], bank[bk][:, at:at + (q + 1) * P],
                                   ACT.Exp, bias=negmax[:, q:q + 1], accum_out=den[:, q:q + 1]).then_inc(exped, 1)
                if not (first and s == 0):
                    c_high(g, s)
                p = kv_piece(s)
                if p and not (last and p[1]):
                    kv_high(pieces_before(g, s, last) + 1, p[0], p[2])
                for kind, gg, h in split_points(g, s, last):
                    high(act, kind, gg, h)
                for x, (bk, at, width) in enumerate(T_BANK):
                    act.wait_ge(turned, 3 * n + x + 1)
                    if x == 0 and not (first and s == 0):
                        act.wait_ge(weighted, n)
                    act.activation(pT_hi[:, at:at + width], bank[bk][:, 0:width], ACT.Copy).then_inc(pT_hi_ok, 1)

            for piece in range(PIECES):
                kv_high(piece + 1, 0, piece)
            q_high(0)
            steps(act, step)
            c_high(HK - 1, STEPS)

        @block.vector
        def _(dve):
            def kv_low(count, b, piece):
                dve.wait_ge(kv_hi_ok, count)
                if piece == 0:
                    dve.tensor_tensor(kT_lo[:, b, :], bank[7][:, :], kT_hi[:, b, :].bitcast(F32), ALU.subtract
                                      ).then_inc(kv_lo_ok, 1)
                else:
                    cols = slice((piece - 1) * 2 * D1, piece * 2 * D1)
                    dve.tensor_tensor(v_lo[:, b, cols], bank[7][:, 0:2 * D1], v_hi[:, b, cols].bitcast(F32),
                                      ALU.subtract).then_inc(kv_lo_ok, 1)

            def q_low(n):
                dve.wait_ge(q_hi_ok, n + 1)
                dve.scalar_tensor_tensor(out=qT_lo[:, :], in0=bank[6][:, :], scalar=SCALE,
                                         in1=qT_hi[:, :].bitcast(F32), op0=ALU.mult, op1=ALU.subtract
                                         ).then_inc(q_lo_ok, 1)

            def c_low(g, s):
                k = (s - 1) // HQ
                b, h = k % 2, (s - 1) % HQ
                dve.wait_ge(c_hi_ok, g * STEPS + s)
                dve.tensor_tensor(cT_lo[:, b, h, :], bank[7][:, :], cT_hi[:, b, h, :].bitcast(F32), ALU.subtract
                                  ).then_inc(c_lo_ok, 1)

            def add_output(g, s, drained=False):
                k, q = (s - 5) // HQ, (s - 5) % HQ
                tile = k % 2 * QT + q
                dve.wait_ge(o_done, g * STEPS + s - 4)
                dve.tensor_tensor(y1[:, tile, :], out_bank(s, drained)[:, :], y1[:, tile, :], ALU.add
                                  ).then_inc(o_added, 1)

            def step(g, s, first, last):
                n = g * STEPS + s
                for bk, q, at in ORDER:
                    dve.wait_ge(scored, 3 * n + bk + 1)
                    diagonal = bank[bk][:, at + q * P:at + (q + 1) * P]
                    dve.tensor_tensor(diagonal, diagonal, mask[:, :], ALU.add).then_inc(masked, 1)
                for x, (bk, q, at) in enumerate(ORDER):
                    dve.wait_ge(masked, QT * n + x + 1)
                    dve.tensor_reduce(negmax[:, q:q + 1], bank[bk][:, at:at + (q + 1) * P], AX_X, ALU.max,
                                      negate=True).then_inc(maxed, 1)
                if not (last and s == STEPS - 1):
                    q_low(n + 1)
                dve.wait_ge(exped, QT * (n + 1))
                if not (first and s == 0):
                    dve.wait_ge(normed, QT * n)
                dve.reciprocal(rden[:, :], den[:, :]).then_inc(inverted, 1)
                dve.wait_ge(inverted, n + 1)
                for q in (0, 1, 2, 3):
                    tile = probs[:, PROB_AT[q]:PROB_AT[q] + (q + 1) * P]
                    dve.tensor_scalar(tile, tile, rden[:, q:q + 1], None, ALU.mult).then_inc(normed, 1)
                if not (first and s == 0):
                    c_low(g, s)
                if not (first and s < 5):
                    add_output(g, s)
                p = kv_piece(s)
                if p and not (last and p[1]):
                    kv_low(pieces_before(g, s, last) + 1, p[0], p[2])
                for x, (bk, at, width) in enumerate(T_BANK):
                    dve.wait_ge(pT_hi_ok, 3 * n + x + 1)
                    dve.tensor_tensor(pT_lo[:, at:at + width], bank[bk][:, 0:width],
                                      pT_hi[:, at:at + width].bitcast(F32), ALU.subtract).then_inc(pT_lo_ok, 1)

            for piece in range(PIECES):
                kv_low(piece + 1, 0, piece)
            q_low(0)
            steps(dve, step)
            c_low(HK - 1, STEPS)
            for x in range(5):
                add_output(HK - 1, STEPS + x, True)


def compress(nc, st, sb, sems, bank, a, ident, mask, xT_hi, xT_lo, y1, lat_hi, lat_lo, SUB, HQ, load, high,
             low):
    PAIR = 2 * LAT
    raw = sb(st, "wkv_raw", [P, KC, HK, PAIR])
    hi = sb(st, "wkv_hi", [P, KC, HK, 2, PAIR], F32R)
    lo = sb(st, "wkv_lo", [P, KC, HK, 2, PAIR], F32R)
    w_in = sems(st, " ".join(f"K_w_in{c}" for c in range(KC)))
    (hi_ok, lo_ok, zeroed, masked, done, out_hi, out_lo) = sems(
        st, "K_w_hi K_w_lo K_zeroed K_masked K_done K_out_hi K_out_lo")
    with nc.Block() as block:
        @block.sync
        def _(sp):
            for c in range(KC):
                sp.dma_start(raw[:, c, :, :], a["WkvT"][c * P:(c + 1) * P].rearrange("p (h n) -> p h n", h=HK)
                             ).then_inc(w_in[c], 16)
            load(sp, 0)

        @block.gpsimd
        def _(pool):
            pool.memset(mask[:, :], 0.0).then_inc(zeroed, 1)
            pool.memset(y1[:, :, :], 0.0).then_inc(zeroed, 1)
            pool.wait_ge(zeroed, 2)
            pool.affine_select(out=mask[:, :], in_=mask[:, :], compare_op=ALU.is_ge, fill=MASKED, base=0,
                               pattern=[[-1, P]], channel_multiplier=1).then_inc(masked, 1)
            low(pool, "wu", 0, 0)
            for h in range(HQ):
                low(pool, "wq", 0, h)

        def kept(buf, b, hk, rows):
            cols = slice(hk * (S // 8), (hk + 1) * (S // 8))
            return buf[rows, bass.ds(b, 1), :, cols].rearrange("p one c t -> p (one c) t")

        def tokens(bk, i, rows):
            return bk[rows, :].rearrange("p (t c two) -> p two c t", two=2, c=2 * LC)[:, i, :, :]

        @block.scalar
        def _(act):
            nc.scalar.preload_act_table(ACT.Exp)
            for c in range(KC):
                act.wait_ge(w_in[c], 16)
                for i in range(2):
                    act.activation(hi[:, c, :, i, :], raw[:, c, :, :], ACT.Copy).then_inc(hi_ok, 1)
            high(act, "wu", 0, 0, True)
            for h in range(HQ):
                high(act, "wq", 0, h, True)

            def job(b, hk):
                act.wait_ge(done, b * HK + hk + 1)
                for i in range(2):
                    rows = slice(i * PAIR, (i + 1) * PAIR)
                    settle(act)
                    act.activation(kept(lat_hi, b, hk, rows), tokens(bank[hk], i, rows), ACT.Copy).then_inc(out_hi, 1)
            with act.Fori(0, B) as b:
                for hk in range(HK):
                    job(b, hk)

        @block.vector
        def _(dve):
            for c in range(KC):
                for i in range(2):
                    dve.wait_ge(hi_ok, 2 * c + i + 1)
                    dve.tensor_tensor(lo[:, c, :, i, :], raw[:, c, :, :], hi[:, c, :, i, :].bitcast(F32), ALU.subtract
                                      ).then_inc(lo_ok, 1)
            with dve.Fori(0, B) as b:
                for hk in range(HK):
                    dve.wait_ge(out_hi, 2 * (b * HK + hk) + 2)
                    for i in range(2):
                        rows = slice(i * PAIR, (i + 1) * PAIR)
                        dve.tensor_tensor(kept(lat_lo, b, hk, rows), tokens(bank[hk], i, rows),
                                          kept(lat_hi, b, hk, rows).bitcast(F32), ALU.subtract).then_inc(out_lo, 1)

        @block.tensor
        def _(pe):
            def job(b, hk):
                if not (isinstance(b, int) and b == 0):
                    pe.wait_ge(out_lo, 2 * (b * HK + hk - HK) + 2)
                for c in range(KC):
                    if b == 0 and hk == 0:
                        pe.wait_ge(lo_ok, 2 * (c + 1))
                    mm = three(pe, bank[hk][:, :], [
                        (hi[:, c, hk, :, :].rearrange("p a n -> p (a n)"),
                         lo[:, c, hk, :, :].rearrange("p a n -> p (a n)"),
                         xT_hi[:, c, b * S:(b + 1) * S], xT_lo[:, c, b * S:(b + 1) * S])],
                        start=(c == 0), stop=(c == KC - 1))
                mm.then_inc(done, 1)
            for b in range(B):
                for hk in range(HK):
                    job(b, hk)


def cores_ffn(nc, st, sb, sems, bank, a, ident, neghalf, y1, x_mid, out):
    NS = R + E
    wb_raw = sb(st, "wb_raw", [P, KC, D])
    wb_hi = sb(st, "wb_hi", [P, KC, D], F32R)
    wb_lo = sb(st, "wb_lo", [P, KC, D], F32R)
    ar_raw = sb(st, "ar_raw", [P, KC, NS])
    ar_hi = sb(st, "ar_hi", [P, KC, NS], F32R)
    ar_lo = sb(st, "ar_lo", [P, KC, NS], F32R)
    cores = sb(st, "cores_T", [R, P])
    b_w = sb(st, "b_w", [R, D])
    cb = sb(st, "cores_b", [P, D])
    bb = sb(st, "b_base", [P, D])
    x = sb(st, "x_last", [P, NT, D])
    xn = sb(st, "xn_last", [P, D])
    tT_hi = [sb(st, f"eT_hi{i}", [P, KC, P], F32R) for i in range(2)]
    tT_lo = [sb(st, f"eT_lo{i}", [P, KC, P], F32R) for i in range(2)]
    y = sb(st, "y_last", [P, D])
    negmax = sb(st, "negmaxE", [P, 1])
    ex = sb(st, "expE", [P, E])
    den = sb(st, "denE", [P, 1])
    rden = sb(st, "rdenE", [P, 1])
    route = sb(st, "route", [P, E])
    z = sb(st, "z", [P, E, R])
    zT = sb(st, "zT", [P, P])
    stats0 = sb(st, "stats_y1", [P, NT, 6])
    mv0 = sb(st, "mv_y1", [P, NT, 2])
    veps0 = sb(st, "veps_y1", [P, NT])
    rstd0 = sb(st, "rstd_y1", [P, NT])
    half0 = sb(st, "neghalf_y1", [P, NT])
    nmr0 = sb(st, "shift_y1", [P, NT])
    stats = sb(st, "statsE", [P, 2, 6])
    mv = sb(st, "mvE", [P, 2, 2])
    veps = sb(st, "vepsE", [P, 2, 1])
    rstd = sb(st, "rstdE", [P, 2, 1])
    (x_in, ar_in, x_rest_in, nmr_ok, w_in, small_in, wb_hi_ok, wb_lo_ok, ar_hi_ok, ar_lo_ok, cb_done, cb_ok, stat0, aggr0, eps0, half_ok,
     rstd0_ok, applied0, x3_ok, turned, tT_hi_ok, tT_lo_ok, small_done, maxed, exped, inverted, routed, z_ok, z_turned,
     zT_ok, out_done, y_ok, x4_ok, stored) = sems(
        st, "E_x_in E_ar_in E_x_rest_in E_nmr E_w_in E_small_in E_wb_hi E_wb_lo E_ar_hi E_ar_lo E_cb_done E_cb E_stat0 E_aggr0 E_eps0 E_half "
            "E_rstd0 E_applied0 E_x3 E_turned E_tT_hi E_tT_lo E_small_done E_maxed E_exped E_inverted E_routed E_z "
            "E_z_turned E_zT E_out_done E_y E_x4 E_stored")
    stat, aggr, eps_ok, rstd_ok, applied = (sems(st, " ".join(f"E_{n}{k}" for k in (1, 2)))
                                            for n in ("stat", "aggr", "eps", "rstd", "applied"))
    out_v = out.rearrange("(t p) h -> p t h", p=P)

    def tile_of(buf, t):
        return buf[:, t, :] if isinstance(t, int) else buf[:, bass.ds(t, 1), :]

    def quads(b):
        return b[:, :].rearrange("p (c q) -> p c q", c=KC)

    def steps(eng, step):
        for odd in range(2):
            step(odd, odd, True)
        with eng.Fori(1, NT // 2 - 1) as i:
            for odd in range(2):
                step(2 * i + odd, odd, True)
        for odd in range(2):
            step(NT - 2 + odd, odd, False)

    GROUPS = (slice(0, 2), slice(2, NT))

    def tile(t, n):
        return isinstance(t, int) and t == n

    with nc.Block() as block:
        @block.sync
        def _(sp):
            mid_v = x_mid.rearrange("(t p) h -> p t h", p=P)
            sp.dma_start(x[:, 0:2, :], mid_v[:, 0:2, :]).then_inc(x_in, 16)
            sp.dma_start(ar_raw[:, :, :], a["ArT"].rearrange("(c p) n -> p c n", p=P)).then_inc(ar_in, 16)
            sp.dma_start(wb_raw[:, :, :], a["WbT"].rearrange("(c p) n -> p c n", p=P)).then_inc(w_in, 16)
            sp.dma_start(cores[:, :], a["coresT"]).then_inc(small_in, 16)
            sp.dma_start(b_w[:, :], a["BwT"]).then_inc(small_in, 16)
            sp.dma_start(bb[:, :], a["bb"].rearrange("(a n) -> a n", a=1).to_broadcast([P, D])).then_inc(small_in, 16)
            sp.dma_start(x[:, 2:NT, :], mid_v[:, 2:NT, :]).then_inc(x_rest_in, 16)

            def store(t, odd, ahead):
                sp.wait_ge(x4_ok, t + 1)
                sp.dma_start(tile_of(out_v, t), tile_of(x, t)).then_inc(stored, 16)
            steps(sp, store)
            sp.wait_ge(stored, 16 * NT)

        @block.gpsimd
        def _(pool):
            def power(n, t):
                pool.wait_ge(eps_ok[n], t + 1)
                settle(pool)
                pool.tensor_tensor(rstd[:, n, :], veps[:, n, :], neghalf[:, :], ALU.pow).then_inc(rstd_ok[n], 1)

            pool.memset(half0[:, :], -0.5).then_inc(half_ok, 1)
            pool.wait_ge(half_ok, 1)
            for n, of in enumerate(GROUPS):
                pool.wait_ge(eps0, n + 1)
                pool.tensor_tensor(rstd0[:, of], veps0[:, of], half0[:, of], ALU.pow).then_inc(rstd0_ok, 1)
                if n == 0:
                    power(0, 0)
            power(0, 1)

            def add(t):
                pool.wait_ge(applied[1], t + 1)
                settle(pool)
                pool.tensor_tensor(tile_of(x, t), tile_of(x, t), y[:, :], ALU.add).then_inc(x4_ok, 1)

            def add_y1(t):
                pool.tensor_tensor(tile_of(x, t), tile_of(x, t), tile_of(y1, t), ALU.add).then_inc(x3_ok, 1)

            def step(t, odd, ahead):
                if tile(t, 0):
                    pool.wait_ge(x_rest_in, 16)
                    pool.wait_ge(applied0, NT)
                    pool.wait_ge(x3_ok, 2)
                if ahead:
                    add_y1(t + 2)
                if not tile(t, 0):
                    power(1, t - 1)
                if ahead:
                    power(0, t + 2)
                if not tile(t, 0):
                    add(t - 1)
            steps(pool, step)
            power(1, NT - 1)
            add(NT - 1)

        @block.tensor
        def _(pe):
            def turn_x(t, first=False):
                pe.wait_ge(applied[0], t + 1)
                if not first:
                    pe.wait_ge(tT_lo_ok, t)
                for c in range(KC):
                    mm = pe.transpose(bank[1][:, c * P:(c + 1) * P], xn[:, c * P:(c + 1) * P], ident[:, :])
                mm.then_inc(turned, 1)

            turn_x(0, True)
            pe.wait_ge(small_in, 48)
            pe.matmul(bank[4][:, :], cores[:, :], b_w[:, :], start=True, stop=True).then_inc(cb_done, 1)
            pe.wait_ge(ar_lo_ok, 1)
            pe.wait_ge(wb_lo_ok, 1)

            def step(t, odd, ahead):
                hi, lo = tT_hi[odd], tT_lo[odd]
                pe.wait_ge(tT_lo_ok, t + 1)
                if not tile(t, 0):
                    pe.wait_ge(z_ok, t)
                three(pe, bank[2][:, 0:NS], [(hi[:, c, :], lo[:, c, :], ar_hi[:, c, :], ar_lo[:, c, :])
                                             for c in range(KC)]).then_inc(small_done, 1)
                if not tile(t, NT - 1):
                    turn_x(t + 1)
                if not tile(t, 0):
                    pe.wait_ge(y_ok, t)
                three(pe, bank[0][:, :], [(hi[:, c, :], lo[:, c, :], wb_hi[:, c, :], wb_lo[:, c, :])
                                          for c in range(KC)], stop=False)
                pe.wait_ge(z_ok, t + 1)
                if not tile(t, 0):
                    pe.wait_ge(zT_ok, t)
                pe.transpose(bank[3][:, 0:P], z[:, :, :].rearrange("p e r -> p (e r)"), ident[:, :]
                             ).then_inc(z_turned, 1)
                pe.wait_ge(zT_ok, t + 1)
                if tile(t, 0):
                    pe.wait_ge(cb_ok, 1)
                pe.matmul(bank[0][:, :], zT[:, :], cb[:, :], start=False, stop=True).then_inc(out_done, 1)
            steps(pe, step)

        @block.scalar
        def _(act):
            nc.scalar.preload_act_table(ACT.Exp)
            act.wait_ge(ar_in, 16)
            act.activation(ar_hi[:, :, :], ar_raw[:, :, :], ACT.Copy).then_inc(ar_hi_ok, 1)

            def normalise(n):
                act.wait_ge(nmr_ok, n + 1)
                for t in range(NT)[GROUPS[n]]:
                    act.activation(y1[:, t, :], y1[:, t, :], ACT.Identity, scale=rstd0[:, t:t + 1],
                                   bias=nmr0[:, t:t + 1]).then_inc(applied0, 1)

            normalise(0)
            act.wait_ge(w_in, 16)
            act.activation(wb_hi[:, :, :], wb_raw[:, :, :], ACT.Copy).then_inc(wb_hi_ok, 1)

            def high(t, odd):
                act.wait_ge(turned, t + 1)
                if not (isinstance(t, int) and t < 2):
                    act.wait_ge(out_done, t - 1)
                act.activation(tT_hi[odd][:, :, :], quads(bank[1]), ACT.Copy).then_inc(tT_hi_ok, 1)

            high(0, 0)
            act.wait_ge(cb_done, 1)
            act.activation(cb[:, :], bank[4][:, :], ACT.Copy, scale=LORA_SCALE).then_inc(cb_ok, 1)
            normalise(1)

            def step(t, odd, ahead):
                act.wait_ge(maxed, t + 1)
                if not tile(t, 0):
                    act.wait_ge(routed, t)
                act.activation(ex[:, :], bank[2][:, R:NS], ACT.Exp, bias=negmax[:, :], accum_out=den[:, :]
                               ).then_inc(exped, 1)
                if not tile(t, NT - 1):
                    high(t + 1, 1 - odd)
                act.wait_ge(z_turned, t + 1)
                if not tile(t, 0):
                    act.wait_ge(out_done, t)
                act.activation(zT[:, :], bank[3][:, 0:P], ACT.Copy).then_inc(zT_ok, 1)
            steps(act, step)

        @block.vector
        def _(dve):
            def statistics(n, t, src, ready, first):
                dve.wait_ge(ready, t + 1)
                if not first:
                    dve.wait_ge(aggr[n], t)
                settle(dve)
                dve.bn_stats(stats[:, n, :], src).then_inc(stat[n], 1)
                dve.wait_ge(stat[n], t + 1)
                if not first:
                    dve.wait_ge(applied[n], t)
                settle(dve)
                dve.bn_aggr(mv[:, n, :], stats[:, n, :]).then_inc(aggr[n], 1)
                dve.wait_ge(aggr[n], t + 1)
                if not first:
                    dve.wait_ge(rstd_ok[n], t)
                dve.tensor_scalar(veps[:, n, :], mv[:, n, 1:2], EPS, None, ALU.add).then_inc(eps_ok[n], 1)

            def front(t, first):
                if isinstance(t, int) and t < 2:
                    dve.tensor_tensor(tile_of(x, t), tile_of(x, t), tile_of(y1, t), ALU.add).then_inc(x3_ok, 1)
                statistics(0, t, tile_of(x, t), x3_ok, first)

            def input_norm(t, first):
                dve.wait_ge(rstd_ok[0], t + 1)
                if not first:
                    dve.wait_ge(turned, t)
                dve.tensor_scalar(xn[:, :], tile_of(x, t), mv[:, 0, 0:1], rstd[:, 0, :], ALU.subtract, ALU.mult
                                  ).then_inc(applied[0], 1)

            def low(t, odd):
                dve.wait_ge(tT_hi_ok, t + 1)
                dve.tensor_tensor(tT_lo[odd][:, :, :], quads(bank[1]), tT_hi[odd][:, :, :].bitcast(F32), ALU.subtract
                                  ).then_inc(tT_lo_ok, 1)

            def output(t, first):
                dve.wait_ge(out_done, t + 1)
                if not first:
                    dve.wait_ge(x4_ok, t)
                dve.tensor_tensor(y[:, :], bank[0][:, :], bb[:, :], ALU.add).then_inc(y_ok, 1)
                statistics(1, t, y[:, :], y_ok, first)

            def normalise(t):
                dve.wait_ge(rstd_ok[1], t + 1)
                dve.tensor_scalar(y[:, :], y[:, :], mv[:, 1, 0:1], rstd[:, 1, :], ALU.subtract, ALU.mult
                                  ).then_inc(applied[1], 1)

            def group_statistics(n):
                of = GROUPS[n]
                for t in range(NT)[of]:
                    dve.bn_stats(stats0[:, t, :], y1[:, t, :]).then_inc(stat0, 1)
                dve.wait_ge(stat0, of.stop)
                for t in range(NT)[of]:
                    dve.bn_aggr(mv0[:, t, :], stats0[:, t, :]).then_inc(aggr0, 1)
                dve.wait_ge(aggr0, of.stop)
                dve.tensor_scalar(veps0[:, of], mv0[:, of, 1], EPS, None, ALU.add).then_inc(eps0, 1)

            def shift(n):
                of = GROUPS[n]
                dve.wait_ge(rstd0_ok, n + 1)
                dve.scalar_tensor_tensor(out=nmr0[:, of], in0=mv0[:, of, 0], scalar=-1.0, in1=rstd0[:, of],
                                         op0=ALU.mult, op1=ALU.mult).then_inc(nmr_ok, 1)

            group_statistics(0)
            shift(0)
            dve.wait_ge(x_in, 16)
            dve.wait_ge(applied0, 1)
            front(0, True)
            dve.wait_ge(ar_hi_ok, 1)
            dve.tensor_tensor(ar_lo[:, :, :], ar_raw[:, :, :], ar_hi[:, :, :].bitcast(F32), ALU.subtract
                              ).then_inc(ar_lo_ok, 1)
            input_norm(0, True)
            group_statistics(1)
            low(0, 0)
            dve.wait_ge(wb_hi_ok, 1)
            dve.tensor_tensor(wb_lo[:, :, :], wb_raw[:, :, :], wb_hi[:, :, :].bitcast(F32), ALU.subtract
                              ).then_inc(wb_lo_ok, 1)
            shift(1)
            dve.wait_ge(applied0, 2)
            front(1, False)
            input_norm(1, False)

            def step(t, odd, ahead):
                dve.wait_ge(small_done, t + 1)
                if not tile(t, 0):
                    dve.wait_ge(exped, t)
                dve.tensor_reduce(negmax[:, :], bank[2][:, R:NS], AX_X, ALU.max, negate=True).then_inc(maxed, 1)
                if not tile(t, 0):
                    output(t - 1, tile(t, 1))
                dve.wait_ge(exped, t + 1)
                if not tile(t, 0):
                    dve.wait_ge(routed, t)
                dve.reciprocal(rden[:, :], den[:, :]).then_inc(inverted, 1)
                dve.wait_ge(inverted, t + 1)
                if not tile(t, 0):
                    dve.wait_ge(z_turned, t)
                dve.tensor_scalar(route[:, :], ex[:, :], rden[:, :], None, ALU.mult).then_inc(routed, 1)
                dve.wait_ge(routed, t + 1)
                dve.tensor_tensor(z[:, :, :], route[:, :, None].to_broadcast([P, E, R]),
                                  bank[2][:, None, 0:R].to_broadcast([P, E, R]), ALU.mult).then_inc(z_ok, 1)
                if not tile(t, NT - 1):
                    low(t + 1, 1 - odd)
                if ahead:
                    front(t + 2, False)
                if not tile(t, 0):
                    normalise(t - 1)
                if ahead:
                    input_norm(t + 2, False)

            steps(dve, step)
            output(NT - 1, False)
            normalise(NT - 1)


def kernel(**inputs):
    import numpy as _np
    import concourse.bacc as _bacc
    from concourse import mybir as _mybir
    from concourse.bass_utils import run_bass_kernel_spmd as _run

    g = {n: _np.asarray(v) for n, v in inputs.items()}
    kv = [g[f"L1_attn_W{n}_down"].reshape(HK, LAT, D) for n in "kv"]
    laid = {
        "x": g["L0_attn_x"].reshape(TOK, D),
        "qkvw": g["L0_attn_attn_qkvw"],
        "qkvb": g["L0_attn_attn_qkvb"],
        "qkvb_cols": g["L0_attn_attn_qkvb"].reshape(3 * KC, P).T,
        "ow": g["L0_attn_attn_ow"],
        "ob": g["L0_attn_attn_ob"],
        "gateT": g["L0_ffn_w_gate"].transpose(2, 0, 1),
        "upT": g["L0_ffn_w_up"].transpose(2, 0, 1),
        "downT": g["L0_ffn_w_down"].transpose(2, 0, 1),
        "WqT": g["L1_attn_Wq"].T,
        "WkvT": _np.stack(kv, axis=1).reshape(2 * NLAT, D).T,
        "WkupT": g["L1_attn_Wk_up"].T,
        "WvupT": g["L1_attn_Wv_up"].T,
        "WoT": g["L1_attn_Wo"].T,
        "WbT": g["L1_ffn_W_base"].T,
        "bb": g["L1_ffn_b_base"],
        "ArT": _np.concatenate([g["L1_ffn_A_w"], g["L1_ffn_router_w"]]).T,
        "BwT": g["L1_ffn_B_w"].T,
        "coresT": g["L1_ffn_cores"].reshape(E * R, R).T,
    }
    nc = _bacc.Bacc("TRN2", target_bir_lowering=False, num_devices=1)
    arrays, aps = {}, {}
    for name, v in laid.items():
        v = _np.ascontiguousarray(v)
        arrays[f"in_{name}"] = v
        aps[name] = nc.dram_tensor(f"in_{name}", v.shape, _mybir.dt.from_np(v.dtype), kind="ExternalInput").ap()
    out = nc.dram_tensor("out_0", (TOK, D), F32, kind="ExternalOutput").ap()
    program(nc, aps, out)
    r = _run(nc, [arrays], core_ids=[0])
    return r.results[0]["out_0"].reshape(B, S, D)
```
